# Optimizing a Trainium2 kernel written in Bass

```python
import numpy as np
import jax
import jax.numpy as jnp

def _softmax(x, axis=-1):
    return jax.nn.softmax(x, axis=axis)

def _gelu(x):
    return jax.nn.gelu(x, approximate=True)

def _silu(x):
    return jax.nn.silu(x)

def _sigmoid(x):
    return jax.nn.sigmoid(x)

def _layernorm(x, axis=-1, eps=1e-05):
    m = jnp.mean(x, axis=axis, keepdims=True)
    v = jnp.var(x, axis=axis, keepdims=True)
    return (x - m) / jnp.sqrt(v + eps)

def _scatter_add(tgt, idx, src, axis=0):
    return tgt.at[idx].add(src)

def _segment_sum(src, seg, n):
    return jax.ops.segment_sum(src, seg, n)
kernel_name = 'mk_perceiver_d2_seqx_r8_6a43cc'

def setup_inputs(seed: int=0):
    np.random.seed(seed)
    _w = jnp.asarray

    def _rec_inputs():
        import jax
        import jax.numpy as jnp
        _rk = jax.random.key(seed)
        x = -9.806e-05 + 1 * jax.random.normal(jax.random.fold_in(_rk, 1), (32, 64, 128), jnp.float32)
        _lenS = 64 - jax.random.randint(jax.random.fold_in(_rk, 7), (32,), 0, max(1, 64 // 4) + 1, jnp.int32)
        _lenS2 = 1601 - jax.random.randint(jax.random.fold_in(_rk, 8), (32,), 0, max(1, 1601 // 4) + 1, jnp.int32)
        _ctx_1024P = jax.random.normal(jax.random.fold_in(_rk, 11), (32, 16, 128), jnp.float32)
        _ctx_1024c = jax.random.dirichlet(jax.random.fold_in(_rk, 511), 0.3 * jnp.ones((16,), jnp.float32), (32, 1601))
        _ctx_1024t = jnp.einsum('bsk,bkd->bsd', _ctx_1024c, _ctx_1024P)
        _ctx_1024t = _ctx_1024t * jax.lax.rsqrt(jnp.mean(jnp.square(_ctx_1024t)) + 1e-12) * 0.953939
        ctx_1024 = -1.52775e-05 + 0.999936 * (_ctx_1024t + 0.3 * jax.random.normal(jax.random.fold_in(_rk, 611), (32, 1601, 128), jnp.float32))
        _validS = jnp.arange(64)[None, :] < _lenS[:, None]
        _validS2 = jnp.arange(1601)[None, :] < _lenS2[:, None]
        _causal = jnp.tril(jnp.ones((64, 64), dtype=bool))
        mask_Bx1xSxS2_if1 = jnp.where(jnp.ones((32, 1, 64, 1601), dtype=bool), 1, 0).astype(jnp.int32)
        return (x, ctx_1024, mask_Bx1xSxS2_if1)
    x, ctx_1024, mask_Bx1xSxS2_if1 = _rec_inputs()

    def _L0_xattn_setup():
        import jax, jax.numpy as jnp
        import numpy as np
        D = 128
        NUM_ITERS = 3
        EPS = 1e-06
        SCALE = D ** (-0.5)

        def rmsnorm(x, w, eps=EPS):
            return x * jax.lax.rsqrt(jnp.mean(x * x, axis=-1, keepdims=True) + eps) * w

        def gru_cell(x, h, wih, whh, bih, bhh):
            gx = x @ wih.T + bih
            gh = h @ whh.T + bhh
            xr, xz, xn = jnp.split(gx, 3, axis=-1)
            hr, hz, hn = jnp.split(gh, 3, axis=-1)
            r = jax.nn.sigmoid(xr + hr)
            z = jax.nn.sigmoid(xz + hz)
            n = jnp.tanh(xn + r * hn)
            return (1.0 - z) * n + z * h
        key = jax.random.key(seed)
        ks = jax.random.split(key, 8)
        B, K, M, d = (8, 64, 512, D)
        w_std = d ** (-0.5)
        return {'slots': jax.random.normal(ks[0], (B, K, d), jnp.float32), 'P': jax.random.normal(ks[1], (B, M, d), jnp.float32), 'Wq': jax.random.normal(ks[2], (d, d), jnp.float32) * w_std, 'Wk': jax.random.normal(ks[3], (d, d), jnp.float32) * w_std, 'Wv': jax.random.normal(ks[4], (d, d), jnp.float32) * w_std, 'gru_wih': jax.random.normal(ks[5], (3 * d, d), jnp.float32) * w_std, 'gru_whh': jax.random.normal(ks[6], (3 * d, d), jnp.float32) * w_std, 'gru_bih': jnp.zeros((3 * d,), jnp.float32), 'gru_bhh': jnp.zeros((3 * d,), jnp.float32), 'slot_norm_w': jnp.ones((d,), jnp.float32), 'input_norm_w': jnp.ones((d,), jnp.float32)}
    _L0_xattn_all = _L0_xattn_setup()
    _L0_xattn_in = {k: v for k, v in _L0_xattn_all.items() if k in ('Wq', 'Wk', 'Wv', 'gru_wih', 'gru_whh', 'gru_bih', 'gru_bhh', 'slot_norm_w', 'input_norm_w')}
    del _L0_xattn_all

    def _L0_attn_setup():
        import jax, jax.numpy as jnp
        import numpy as np
        EMBED_DIM = 128
        PROJ_DIM = 32
        key = jax.random.key(seed)
        kx, kq, kk = jax.random.split(key, 3)
        x = jax.random.normal(kx, (8, 512, EMBED_DIM), dtype=jnp.float32)
        scale = 1.0 / PROJ_DIM ** 0.5
        q_proj = jax.random.normal(kq, (EMBED_DIM, PROJ_DIM), dtype=jnp.float32) * scale
        k_proj = jax.random.normal(kk, (EMBED_DIM, PROJ_DIM), dtype=jnp.float32) * scale
        return {'x': x, 'q_proj': q_proj, 'k_proj': k_proj}
    _L0_attn_all = _L0_attn_setup()
    _L0_attn_in = {k: v for k, v in _L0_attn_all.items() if k in ('q_proj', 'k_proj')}
    del _L0_attn_all

    def _L0_ffn_setup():
        import jax, jax.numpy as jnp
        import numpy as np
        B, L, H, E, I = (4, 256, 128, 8, 512)
        S = B * L
        CAP_FACTOR_EVAL = 2.0
        MIN_CAP = 4
        _cap = int(np.floor(CAP_FACTOR_EVAL * S / E))
        _cap += _cap % 2
        CAPACITY = max(_cap, MIN_CAP)

        def _layer_norm(x, g, b, eps=1e-05):
            mu = x.mean(-1, keepdims=True)
            var = ((x - mu) ** 2).mean(-1, keepdims=True)
            return (x - mu) * jax.lax.rsqrt(var + eps) * g + b
        key = jax.random.key(seed)
        ks = jax.random.split(key, 8)
        gate_std = float(np.sqrt(0.1 / H))
        return {'inputs': jax.random.normal(ks[0], (B, L, H), jnp.float32), 'gate_weight': jax.random.normal(ks[1], (E, H), jnp.float32) * gate_std, 'ln_gamma': jnp.ones((H,), jnp.float32), 'ln_beta': jnp.zeros((H,), jnp.float32), 'wi': jax.random.normal(ks[2], (E, H, I), jnp.float32) * float(1.0 / np.sqrt(H)), 'wo': jax.random.normal(ks[3], (E, I, H), jnp.float32) * float(1.0 / np.sqrt(I)), 'conf_w1': jax.random.normal(ks[4], (H // 2, H), jnp.float32) * float(np.sqrt(2.0 / (H + H // 2))), 'conf_b1': -jnp.ones((H // 2,), jnp.float32), 'conf_w2': jax.random.normal(ks[5], (1, H // 2), jnp.float32) * float(np.sqrt(2.0 / (1 + H // 2))), 'conf_b2': -jnp.ones((1,), jnp.float32), 'comp_w': jax.random.normal(ks[6], (1, H), jnp.float32) * float(1.0 / np.sqrt(H)), 'comp_b': jnp.zeros((1,), jnp.float32)}
    _L0_ffn_all = _L0_ffn_setup()
    _L0_ffn_in = {k: v for k, v in _L0_ffn_all.items() if k in ('gate_weight', 'ln_gamma', 'ln_beta', 'wi', 'wo', 'conf_w1', 'conf_b1', 'conf_w2', 'conf_b2', 'comp_w', 'comp_b')}
    del _L0_ffn_all

    def _L1_xattn_setup():
        import jax, jax.numpy as jnp
        import numpy as np
        from math import sqrt
        H = 16
        key = jax.random.key(seed)
        ks = jax.random.split(key, 8)
        B, Sq, Skv, Dq, Dkv, Dall = (2, 256, 256, 128, 128, 128)
        x = jax.random.normal(ks[0], (B, Sq, Dq), dtype=jnp.float32)
        y = jax.random.normal(ks[1], (B, Skv, Dkv), dtype=jnp.float32)
        attention_mask = jnp.ones((B, 1, Sq, Skv), dtype=jnp.int32)
        Wq = jax.random.normal(ks[2], (Dall, Dq), dtype=jnp.float32) * 0.02
        Wk = jax.random.normal(ks[3], (Dall, Dkv), dtype=jnp.float32) * 0.02
        Wv = jax.random.normal(ks[4], (Dall, Dkv), dtype=jnp.float32) * 0.02
        Wo = jax.random.normal(ks[5], (Dq, Dall), dtype=jnp.float32) * 0.02
        bo = jnp.zeros((Dq,), dtype=jnp.float32)
        return {'x': x, 'y': y, 'attention_mask': attention_mask, 'Wq': Wq, 'Wk': Wk, 'Wv': Wv, 'Wo': Wo, 'bo': bo}
    _L1_xattn_all = _L1_xattn_setup()
    _L1_xattn_in = {k: v for k, v in _L1_xattn_all.items() if k in ('Wq', 'Wk', 'Wv', 'Wo', 'bo')}
    del _L1_xattn_all

    def _L1_attn_setup():
        import jax, jax.numpy as jnp
        import numpy as np
        H = 128
        NH = 8
        DQK = H // NH
        DV = 2 * H // NH
        VDIM = 2 * H
        B, L = (2, 256)
        EPS = 1e-05
        ROPE_BASE = 10000.0

        def rope(x):
            b, t, h, d = x.shape
            inv_freq = 1.0 / ROPE_BASE ** (jnp.arange(0, d, 2, dtype=jnp.float32) / d)
            ang = jnp.arange(t, dtype=jnp.float32)[:, None] * inv_freq[None, :]
            cos = jnp.cos(ang)[None, :, None, :]
            sin = jnp.sin(ang)[None, :, None, :]
            xp = x.reshape(b, t, h, d // 2, 2)
            x0, x1 = (xp[..., 0], xp[..., 1])
            out = jnp.stack([x0 * cos - x1 * sin, x1 * cos + x0 * sin], axis=-1)
            return out.reshape(b, t, h, d).astype(x.dtype)
        key = jax.random.key(seed)
        ks = jax.random.split(key, 6)

        def w(k, shape):
            lim = 2 ** (-2.5) * np.sqrt(6.0 / (shape[0] + shape[1]))
            return jax.random.uniform(k, shape, jnp.float32, -lim, lim)
        return {'hidden_states': jax.random.normal(ks[0], (B, L, H), jnp.float32), 'Wq': w(ks[1], (H, H)), 'Wk': w(ks[2], (H, H)), 'Wv': w(ks[3], (H, VDIM)), 'Wg': w(ks[4], (H, VDIM)), 'Wo': w(ks[5], (VDIM, H)), 'g_norm_w': jnp.ones((DV,), jnp.float32)}
    _L1_attn_all = _L1_attn_setup()
    _L1_attn_in = {k: v for k, v in _L1_attn_all.items() if k in ('Wq', 'Wk', 'Wv', 'Wg', 'Wo', 'g_norm_w')}
    del _L1_attn_all

    def _L1_ffn_setup():
        import jax, jax.numpy as jnp
        import numpy as np
        EXPERTS = 8
        TOP_K = 2

        def swiglu(x, w1, w2, w3):
            h = x @ w1
            return h * jax.nn.sigmoid(h) * (x @ w2) @ w3
        key = jax.random.key(seed)
        ks = jax.random.split(key, 9)
        B, S, D = (4, 256, 128)
        H = 2 * D
        s = 0.02
        x = jax.random.normal(ks[0], (B, S, D), dtype=jnp.float32)
        gate_w = jax.random.normal(ks[1], (D, EXPERTS), dtype=jnp.float32) * s
        ew1 = jax.random.normal(ks[2], (EXPERTS, D, H), dtype=jnp.float32) * s
        ew2 = jax.random.normal(ks[3], (EXPERTS, D, H), dtype=jnp.float32) * s
        ew3 = jax.random.normal(ks[4], (EXPERTS, H, D), dtype=jnp.float32) * s
        sw1 = jax.random.normal(ks[5], (D, H), dtype=jnp.float32) * s
        sw2 = jax.random.normal(ks[6], (D, H), dtype=jnp.float32) * s
        sw3 = jax.random.normal(ks[7], (H, D), dtype=jnp.float32) * s
        return {'x': x, 'gate_w': gate_w, 'ew1': ew1, 'ew2': ew2, 'ew3': ew3, 'sw1': sw1, 'sw2': sw2, 'sw3': sw3}
    _L1_ffn_all = _L1_ffn_setup()
    _L1_ffn_in = {k: v for k, v in _L1_ffn_all.items() if k in ('gate_w', 'ew1', 'ew2', 'ew3', 'sw1', 'sw2', 'sw3')}
    del _L1_ffn_all
    return {'x': x, 'ctx_1024': ctx_1024, 'mask_Bx1xSxS2_if1': mask_Bx1xSxS2_if1, 'L0_xattn_Wq': _L0_xattn_in['Wq'], 'L0_xattn_Wk': _L0_xattn_in['Wk'], 'L0_xattn_Wv': _L0_xattn_in['Wv'], 'L0_xattn_gru_wih': _L0_xattn_in['gru_wih'], 'L0_xattn_gru_whh': _L0_xattn_in['gru_whh'], 'L0_xattn_gru_bih': _L0_xattn_in['gru_bih'], 'L0_xattn_gru_bhh': _L0_xattn_in['gru_bhh'], 'L0_xattn_slot_norm_w': _L0_xattn_in['slot_norm_w'], 'L0_xattn_input_norm_w': _L0_xattn_in['input_norm_w'], 'L0_attn_q_proj': _L0_attn_in['q_proj'], 'L0_attn_k_proj': _L0_attn_in['k_proj'], 'L0_ffn_gate_weight': _L0_ffn_in['gate_weight'], 'L0_ffn_ln_gamma': _L0_ffn_in['ln_gamma'], 'L0_ffn_ln_beta': _L0_ffn_in['ln_beta'], 'L0_ffn_wi': _L0_ffn_in['wi'], 'L0_ffn_wo': _L0_ffn_in['wo'], 'L0_ffn_conf_w1': _L0_ffn_in['conf_w1'], 'L0_ffn_conf_b1': _L0_ffn_in['conf_b1'], 'L0_ffn_conf_w2': _L0_ffn_in['conf_w2'], 'L0_ffn_conf_b2': _L0_ffn_in['conf_b2'], 'L0_ffn_comp_w': _L0_ffn_in['comp_w'], 'L0_ffn_comp_b': _L0_ffn_in['comp_b'], 'L1_xattn_Wq': _L1_xattn_in['Wq'], 'L1_xattn_Wk': _L1_xattn_in['Wk'], 'L1_xattn_Wv': _L1_xattn_in['Wv'], 'L1_xattn_Wo': _L1_xattn_in['Wo'], 'L1_xattn_bo': _L1_xattn_in['bo'], 'L1_attn_Wq': _L1_attn_in['Wq'], 'L1_attn_Wk': _L1_attn_in['Wk'], 'L1_attn_Wv': _L1_attn_in['Wv'], 'L1_attn_Wg': _L1_attn_in['Wg'], 'L1_attn_Wo': _L1_attn_in['Wo'], 'L1_attn_g_norm_w': _L1_attn_in['g_norm_w'], 'L1_ffn_gate_w': _L1_ffn_in['gate_w'], 'L1_ffn_ew1': _L1_ffn_in['ew1'], 'L1_ffn_ew2': _L1_ffn_in['ew2'], 'L1_ffn_ew3': _L1_ffn_in['ew3'], 'L1_ffn_sw1': _L1_ffn_in['sw1'], 'L1_ffn_sw2': _L1_ffn_in['sw2'], 'L1_ffn_sw3': _L1_ffn_in['sw3']}

def reference(x, ctx_1024, mask_Bx1xSxS2_if1, L0_xattn_Wq, L0_xattn_Wk, L0_xattn_Wv, L0_xattn_gru_wih, L0_xattn_gru_whh, L0_xattn_gru_bih, L0_xattn_gru_bhh, L0_xattn_slot_norm_w, L0_xattn_input_norm_w, L0_attn_q_proj, L0_attn_k_proj, L0_ffn_gate_weight, L0_ffn_ln_gamma, L0_ffn_ln_beta, L0_ffn_wi, L0_ffn_wo, L0_ffn_conf_w1, L0_ffn_conf_b1, L0_ffn_conf_w2, L0_ffn_conf_b2, L0_ffn_comp_w, L0_ffn_comp_b, L1_xattn_Wq, L1_xattn_Wk, L1_xattn_Wv, L1_xattn_Wo, L1_xattn_bo, L1_attn_Wq, L1_attn_Wk, L1_attn_Wv, L1_attn_Wg, L1_attn_Wo, L1_attn_g_norm_w, L1_ffn_gate_w, L1_ffn_ew1, L1_ffn_ew2, L1_ffn_ew3, L1_ffn_sw1, L1_ffn_sw2, L1_ffn_sw3):
    import jax
    import jax.numpy as jnp

    def _L0_xattn_ref(slots, P, Wq, Wk, Wv, gru_wih, gru_whh, gru_bih, gru_bhh, slot_norm_w, input_norm_w):
        import jax, jax.numpy as jnp
        import numpy as np
        D = 128
        NUM_ITERS = 3
        EPS = 1e-06
        SCALE = D ** (-0.5)

        def rmsnorm(x, w, eps=EPS):
            return x * jax.lax.rsqrt(jnp.mean(x * x, axis=-1, keepdims=True) + eps) * w

        def gru_cell(x, h, wih, whh, bih, bhh):
            gx = x @ wih.T + bih
            gh = h @ whh.T + bhh
            xr, xz, xn = jnp.split(gx, 3, axis=-1)
            hr, hz, hn = jnp.split(gh, 3, axis=-1)
            r = jax.nn.sigmoid(xr + hr)
            z = jax.nn.sigmoid(xz + hz)
            n = jnp.tanh(xn + r * hn)
            return (1.0 - z) * n + z * h
        Pn = rmsnorm(P, input_norm_w)
        k_proj = Pn @ Wk.T
        v_proj = Pn @ Wv.T
        for _ in range(NUM_ITERS):
            sn = rmsnorm(slots, slot_norm_w)
            q_proj = sn @ Wq.T
            scores = jnp.einsum('bkd,bmd->bkm', q_proj, k_proj) * SCALE
            attn = jax.nn.softmax(scores, axis=-2)
            attn = attn / (jnp.sum(attn, axis=-1, keepdims=True) + EPS)
            updates = jnp.einsum('bkm,bmd->bkd', attn, v_proj)
            slots = gru_cell(updates, slots, gru_wih, gru_whh, gru_bih, gru_bhh)
        return slots

    def _L0_attn_ref(x, q_proj, k_proj):
        import jax, jax.numpy as jnp
        import numpy as np
        EMBED_DIM = 128
        PROJ_DIM = 32
        q_prime = jnp.exp(jnp.einsum('bld,de->ble', x, q_proj))
        k_prime = jnp.exp(jnp.einsum('bld,de->ble', x, k_proj))
        kv = jnp.einsum('ble,bld->bed', k_prime, x)
        num = jnp.einsum('ble,bed->bld', q_prime, kv)
        z = 1.0 / (jnp.sum(q_prime, axis=-1, keepdims=True) + 1e-08)
        return num * z

    def _L0_ffn_ref(inputs, gate_weight, ln_gamma, ln_beta, wi, wo, conf_w1, conf_b1, conf_w2, conf_b2, comp_w, comp_b):
        import jax, jax.numpy as jnp
        import numpy as np
        B, L, H, E, I = (4, 256, 128, 8, 512)
        S = B * L
        CAP_FACTOR_EVAL = 2.0
        MIN_CAP = 4
        _cap = int(np.floor(CAP_FACTOR_EVAL * S / E))
        _cap += _cap % 2
        CAPACITY = max(_cap, MIN_CAP)

        def _layer_norm(x, g, b, eps=1e-05):
            mu = x.mean(-1, keepdims=True)
            var = ((x - mu) ** 2).mean(-1, keepdims=True)
            return (x - mu) * jax.lax.rsqrt(var + eps) * g + b
        tokens = inputs.reshape(-1, H)
        residual = tokens
        tokens = _layer_norm(tokens, ln_gamma, ln_beta)
        complexity_score = jax.nn.sigmoid(tokens @ comp_w.T + comp_b).mean()
        hdn = jax.nn.relu(tokens @ conf_w1.T + conf_b1)
        confidence_score = jax.nn.sigmoid(hdn @ conf_w2.T + conf_b2).mean()
        logits = tokens.astype(jnp.float32) @ gate_weight.astype(jnp.float32).T
        probs = jax.nn.softmax(logits, axis=-1)
        top1 = jnp.argmax(logits, axis=-1)
        onehot = jax.nn.one_hot(top1, E, dtype=jnp.int32)
        rank_e = jnp.cumsum(onehot, axis=0) - onehot
        rank = jnp.sum(rank_e * onehot, axis=-1)
        keep = rank < CAPACITY
        weight = jnp.take_along_axis(probs, top1[:, None], axis=-1)[:, 0]
        weight = (weight * keep).astype(tokens.dtype)
        slot = jnp.where(keep, rank, 0)
        dispatch = jnp.zeros((E, CAPACITY, H), tokens.dtype)
        dispatch = dispatch.at[top1, slot].add(tokens * keep[:, None])
        h = jax.nn.gelu(jnp.einsum('ech,ehi->eci', dispatch, wi), approximate=False)
        expert_out = jnp.einsum('eci,eih->ech', h, wo)
        combined = weight[:, None] * expert_out[top1, slot]
        out = (residual + combined).reshape(inputs.shape)
        return out

    def _L1_xattn_ref(x, y, attention_mask, Wq, Wk, Wv, Wo, bo):
        import jax, jax.numpy as jnp
        import numpy as np
        from math import sqrt
        H = 16
        B, Sq, _ = x.shape
        Dall = Wq.shape[0]
        Dh = Dall // H
        q = (x @ Wq.T).reshape(B, Sq, H, Dh).transpose(0, 2, 1, 3)
        k = (y @ Wk.T).reshape(B, -1, H, Dh).transpose(0, 2, 1, 3)
        v = (y @ Wv.T).reshape(B, -1, H, Dh).transpose(0, 2, 1, 3)
        scores = jnp.einsum('bhqd,bhkd->bhqk', q, k)
        mask = attention_mask == 0
        scores = jnp.where(mask, jnp.float32(-1000000000.0), scores)
        attn = jax.nn.softmax(scores / sqrt(Dh), axis=-1)
        out = jnp.einsum('bhqk,bhkd->bhqd', attn, v)
        out = out.transpose(0, 2, 1, 3).reshape(B, Sq, Dall)
        return out @ Wo.T + bo

    def _L1_attn_ref(hidden_states, Wq, Wk, Wv, Wg, Wo, g_norm_w):
        import jax, jax.numpy as jnp
        import numpy as np
        H = 128
        NH = 8
        DQK = H // NH
        DV = 2 * H // NH
        VDIM = 2 * H
        B, L = (2, 256)
        EPS = 1e-05
        ROPE_BASE = 10000.0

        def rope(x):
            b, t, h, d = x.shape
            inv_freq = 1.0 / ROPE_BASE ** (jnp.arange(0, d, 2, dtype=jnp.float32) / d)
            ang = jnp.arange(t, dtype=jnp.float32)[:, None] * inv_freq[None, :]
            cos = jnp.cos(ang)[None, :, None, :]
            sin = jnp.sin(ang)[None, :, None, :]
            xp = x.reshape(b, t, h, d // 2, 2)
            x0, x1 = (xp[..., 0], xp[..., 1])
            out = jnp.stack([x0 * cos - x1 * sin, x1 * cos + x0 * sin], axis=-1)
            return out.reshape(b, t, h, d).astype(x.dtype)
        b, l, _ = hidden_states.shape
        q = (hidden_states @ Wq).reshape(b, l, NH, DQK)
        k = (hidden_states @ Wk).reshape(b, l, NH, DQK)
        v = (hidden_states @ Wv).reshape(b, l, NH, DV)
        q = rope(q)
        k = rope(k)
        q = jnp.transpose(q, (0, 2, 1, 3)).astype(jnp.float32)
        k = jnp.transpose(k, (0, 2, 1, 3)).astype(jnp.float32)
        v = jnp.transpose(v, (0, 2, 1, 3)).astype(jnp.float32)
        s = jnp.log2(1.0 - jnp.exp2(-5.0 - jnp.arange(NH, dtype=jnp.float32)))
        pos = jnp.arange(l, dtype=jnp.float32)
        diff = pos[:, None] - pos[None, :]
        decay = jnp.where(diff >= 0, jnp.exp2(diff[None] * s[:, None, None]), 0.0)
        scores = jnp.einsum('bhqd,bhkd,hqk->bhqk', q * DQK ** (-0.5), k, decay)
        o = jnp.einsum('bhqk,bhkd->bhqd', scores, v)
        o = jnp.transpose(o, (0, 2, 1, 3))
        o = o * jax.lax.rsqrt(jnp.mean(o * o, axis=-1, keepdims=True) + EPS) * g_norm_w
        g = hidden_states @ Wg
        o = o.reshape(b, l, VDIM) * (g * jax.nn.sigmoid(g))
        return o @ Wo

    def _L1_ffn_ref(x, gate_w, ew1, ew2, ew3, sw1, sw2, sw3):
        import jax, jax.numpy as jnp
        import numpy as np
        EXPERTS = 8
        TOP_K = 2

        def swiglu(x, w1, w2, w3):
            h = x @ w1
            return h * jax.nn.sigmoid(h) * (x @ w2) @ w3
        B, S, D = x.shape
        gate_out = x @ gate_w
        top_v, top_i = jax.lax.top_k(gate_out, TOP_K)
        masked = jnp.full_like(gate_out, -1e+20)
        bi = jnp.arange(B)[:, None, None]
        si = jnp.arange(S)[None, :, None]
        masked = masked.at[bi, si, top_i].set(top_v)
        probs = jax.nn.softmax(masked, axis=-1)
        chosen = jnp.zeros_like(gate_out, dtype=bool).at[bi, si, top_i].set(True)
        w = jnp.where(chosen, probs, 0.0)

        def one_expert(w1, w2, w3, we):
            return swiglu(x, w1, w2, w3) * we[..., None]
        out = jax.vmap(one_expert, in_axes=(0, 0, 0, 2))(ew1, ew2, ew3, w).sum(0)
        out = out + swiglu(x, sw1, sw2, sw3)
        return out
    x = x + _L0_xattn_ref(_layernorm(x, axis=-1), ctx_1024, L0_xattn_Wq, L0_xattn_Wk, L0_xattn_Wv, L0_xattn_gru_wih, L0_xattn_gru_whh, L0_xattn_gru_bih, L0_xattn_gru_bhh, L0_xattn_slot_norm_w, L0_xattn_input_norm_w)
    x = x + _L0_attn_ref(_layernorm(x, axis=-1), L0_attn_q_proj, L0_attn_k_proj)
    x = x + _L0_ffn_ref(_layernorm(x, axis=-1), L0_ffn_gate_weight, L0_ffn_ln_gamma, L0_ffn_ln_beta, L0_ffn_wi, L0_ffn_wo, L0_ffn_conf_w1, L0_ffn_conf_b1, L0_ffn_conf_w2, L0_ffn_conf_b2, L0_ffn_comp_w, L0_ffn_comp_b)
    x = x + _L1_xattn_ref(_layernorm(x, axis=-1), ctx_1024, mask_Bx1xSxS2_if1, L1_xattn_Wq, L1_xattn_Wk, L1_xattn_Wv, L1_xattn_Wo, L1_xattn_bo)
    x = x + _L1_attn_ref(_layernorm(x, axis=-1), L1_attn_Wq, L1_attn_Wk, L1_attn_Wv, L1_attn_Wg, L1_attn_Wo, L1_attn_g_norm_w)
    x = x + _L1_ffn_ref(_layernorm(x, axis=-1), L1_ffn_gate_w, L1_ffn_ew1, L1_ffn_ew2, L1_ffn_ew3, L1_ffn_sw1, L1_ffn_sw2, L1_ffn_sw3)
    return x

_drawn_inputs = setup_inputs


def setup_inputs(seed=0):
    import zlib

    import numpy as np

    out = dict(_drawn_inputs(seed))
    spreads = {'L0_xattn_gru_bih': (0.0, 0.1),
     'L0_xattn_gru_bhh': (0.0, 0.1),
     'L0_xattn_slot_norm_w': (1.0, 0.2),
     'L0_xattn_input_norm_w': (1.0, 0.2),
     'L0_ffn_ln_gamma': (1.0, 0.6),
     'L0_ffn_ln_beta': (0.0, 0.8),
     'L0_ffn_conf_b1': (-1.0, 0.2),
     'L1_xattn_bo': (0.0, 2.0),
     'L1_attn_g_norm_w': (1.0, 0.6)}
    factors = {'L0_ffn_gate_weight': 8.0,
     'L0_ffn_wi': 8.0,
     'L0_ffn_wo': 8.0,
     'L1_xattn_Wq': 53.419,
     'L1_xattn_Wk': 53.149,
     'L1_xattn_Wv': 42.474,
     'L1_xattn_Wo': 43.891,
     'L1_attn_Wq': 64.0,
     'L1_attn_Wk': 64.0,
     'L1_attn_Wv': 64.0,
     'L1_attn_Wg': 64.0,
     'L1_attn_Wo': 64.0,
     'L1_ffn_gate_w': 34.395,
     'L1_ffn_ew1': 34.17,
     'L1_ffn_ew2': 31.05,
     'L1_ffn_ew3': 31.003,
     'L1_ffn_sw1': 28.418,
     'L1_ffn_sw2': 25.103,
     'L1_ffn_sw3': 25.753}
    for name, (base, spread) in spreads.items():
        noise = np.random.default_rng([zlib.crc32(name.encode()), seed]).standard_normal(out[name].shape)
        drawn = base * np.exp(spread * noise) if base else spread * noise
        out[name] = jnp.asarray(drawn.astype(out[name].dtype))
    for name, factor in factors.items():
        out[name] = (out[name] * factor).astype(out[name].dtype)
    return out
```

```python
import concourse.bass as bass
from concourse import mybir
from contextlib import ExitStack

fp32 = mybir.dt.float32
bf16 = mybir.dt.bfloat16
i32 = mybir.dt.int32
ALU = mybir.AluOpType
ACT = mybir.ActivationFunctionType
AX = mybir.AxisListType

B, S, D, M = 32, 64, 128, 1601
T = B * S // 128
NC_ = -(-M // 128)
FULL = M // 128
TAIL = M - 128 * FULL
GROUPS = [(c, min(4, FULL - c)) for c in range(0, FULL, 4)]


class Chain:

    def __init__(self, eng, sem, per_turn=0, turn=None):
        self.eng, self.sem, self.n, self.per_turn, self.turn = eng, sem, 0, per_turn, turn

    def __call__(self, instruction):
        self.n += 1
        instruction.then_inc(self.sem, 1)
        at = self.n if self.turn is None else self.turn * self.per_turn + self.n
        self.eng.wait_ge(self.sem, at)

    def close(self):
        assert self.turn is None or self.n == self.per_turn, (self.n, self.per_turn)


def bc(ap, n):
    return ap.unsqueeze(2).to_broadcast([ap.shape[0], ap.shape[1], n])


class Memory:

    def __init__(self, nc, ctx, tag):
        self.nc, self.ctx, self.tag, self.sems = nc, ctx, tag, []
        ctx.callback(self.clear)

    def sb(self, name, shape, dt=fp32):
        return self.ctx.enter_context(self.nc.sbuf_tensor(f"{self.tag}_{name}", shape, dt))

    def ps(self, name, shape=(128, 512), dt=fp32):
        return self.ctx.enter_context(self.nc.psum_tensor(f"{self.tag}_{name}", list(shape), dt))

    def sem(self, name):
        self.sems.append(self.nc.alloc_semaphore(f"{self.tag}_{name}"))
        return self.sems[-1]

    def clear(self):
        self.nc.clear_and_free_semaphores(self.sems)
        self.nc.all_engine_barrier()


class NormSems:
    def __init__(self, m):
        self.centred, self.squared, self.variance = m.sem("ln_centred"), m.sem("ln_squared"), m.sem("ln_variance")
        self.rstd, self.normed, self.transposed = m.sem("ln_rstd"), m.sem("ln_normed"), m.sem("ln_transposed")
        self.xnt_dve, self.xnt_act = m.sem("ln_xnt_dve"), m.sem("ln_xnt_act")


def norm_dve(nc, dve, link, X, XN, work, st, s, eps):
    link(nc.vector.tensor_reduce(out=st[:, 0, :], in_=X[:, :, :], op=ALU.add, axis=AX.X))
    link(nc.vector.tensor_scalar(st[:, 1, :], st[:, 0, :], -1.0 / D, None, ALU.mult))
    nc.vector.tensor_tensor(XN[:, :, :], X[:, :, :], bc(st[:, 1, :], D), ALU.add).then_inc(s.centred, 1)
    dve.wait_ge(s.squared, 1)
    link(nc.vector.tensor_reduce(out=st[:, 2, :], in_=work[:, :, :], op=ALU.add, axis=AX.X))
    nc.vector.tensor_scalar(st[:, 3, :], st[:, 2, :], 1.0 / D, eps, ALU.mult, ALU.add).then_inc(s.variance, 1)
    dve.wait_ge(s.rstd, 1)
    nc.vector.tensor_tensor(XN[:, :, :], XN[:, :, :], bc(st[:, 4, :], D), ALU.mult).then_inc(s.normed, 1)


def norm_act(nc, act, XN, work, s):
    act.wait_ge(s.centred, 1)
    nc.scalar.activation(work[:, :, :], XN[:, :, :], ACT.Square).then_inc(s.squared, 1)


def norm_pool(nc, pool, st, half, s):
    pool.wait_ge(s.variance, 1)
    nc.gpsimd.tensor_tensor(st[:, 4, :], st[:, 3, :], half[:, 0:T], ALU.pow).then_inc(s.rstd, 1)


def transpose_pe(nc, pe, XN, banks, ident, s):
    pe.wait_ge(s.normed, 1)
    for q in range(T // 4):
        for j in range(4):
            last = nc.tensor.transpose(banks[q][:, 128 * j:128 * j + 128], XN[:, 4 * q + j, :], ident[:, :])
        last.then_inc(s.transposed, 1)


def transpose_out_dve(nc, dve, XNT, banks, s):
    for q in range(0, T // 4, 2):
        dve.wait_ge(s.transposed, q + 1)
        nc.vector.tensor_copy(XNT[:, 512 * q:512 * q + 512], banks[q][:, :]).then_inc(s.xnt_dve, 1)


def transpose_out_act(nc, act, XNT, banks, s):
    for q in range(1, T // 4, 2):
        act.wait_ge(s.transposed, q + 1)
        nc.scalar.activation(XNT[:, 512 * q:512 * q + 512], banks[q][:, :], ACT.Copy).then_inc(s.xnt_act, 1)


def norm_block(nc, c, tag, eps=1e-5, x_out=False):
    with ExitStack() as ctx:
        m = Memory(nc, ctx, tag)
        work, st = m.sb("work", [128, T, D]), m.sb("stats", [128, 5, T])
        banks = [m.ps(f"bank{q}") for q in range(T // 4)]
        s, own = NormSems(m), m.sem("dve_own")
        with nc.Block() as block:
            @block.vector
            def _(dve):
                norm_dve(nc, dve, Chain(dve, own), c.X, c.XN, work, st, s, eps)
                transpose_out_dve(nc, dve, c.XNT, banks, s)

            @block.scalar
            def _(act):
                norm_act(nc, act, c.XN, work, s)
                transpose_out_act(nc, act, c.XNT, banks, s)

            @block.gpsimd
            def _(pool):
                norm_pool(nc, pool, st, c.half, s)

            @block.tensor
            def _(pe):
                transpose_pe(nc, pe, c.XN, banks, c.ident, s)


class Common:
    pass


def setup_stage(nc, c, p):
    with ExitStack() as ctx:
        m = Memory(nc, ctx, "su")
        wq, wk, wv = m.sb("wq", [128, 128]), m.sb("wk", [128, 128]), m.sb("wv", [128, 128])
        wpb, wkw = m.sb("wp_bc", [128, 128]), m.sb("wk_scaled", [128, 128])
        wih = m.sb("wihT", [128, 384])
        bih, bhh, ws, wp = m.sb("bih", [128, 3]), m.sb("bhh", [128, 3]), m.sb("ws", [128, 1]), m.sb("wp", [128, 1])
        mq_ps, wc_ps = m.ps("mq"), m.ps("wc")
        loaded, x_loaded, zeroed, wk_scaled, folded = (m.sem(n) for n in ("loaded", "x_loaded", "zeroed", "wk_scaled", "folded"))
        own = m.sem("dve_own")
        loads = [(wq, p["L0_xattn_Wq"]), (wk, p["L0_xattn_Wk"]), (wv, p["L0_xattn_Wv"]), (wih, p["wihT"]),
                 (c.whhT, p["whhT"]), (bih, p["bih3"]), (bhh, p["bhh3"]), (ws, p["ws_col"]), (wp, p["wp_col"])]
        with nc.Block() as block:
            @block.sync
            def _(sp):
                sp.dma_start(c.X[:, :, :], p["x"].rearrange("b s d -> (b s) d").rearrange("(t p) d -> p t d", p=128)).then_inc(x_loaded, 16)
                for dst, src in loads:
                    sp.dma_start(dst[:, :], src).then_inc(loaded, 16)
                sp.dma_start(wpb[:, :], p["wp_row"].partition_broadcast(128)).then_inc(loaded, 16)
                sp.wait_ge(x_loaded, 16)
                sp.wait_ge(loaded, 16 * (len(loads) + 1))

            @block.gpsimd
            def _(pool):
                nc.gpsimd.memset(c.ones[:, :], 1.0)
                nc.gpsimd.memset(c.half[:, :], -0.5)
                nc.gpsimd.memset(c.ident[:, :], 0.0).then_inc(zeroed, 1)
                pool.wait_ge(zeroed, 1)
                nc.gpsimd.affine_select(out=c.ident[:, :], in_=c.ident[:, :], compare_op=ALU.not_equal, fill=1.0,
                                        base=0, pattern=[[-1, 128]], channel_multiplier=1).then_inc(zeroed, 1)
                pool.wait_ge(zeroed, 2)

            @block.vector
            def _(dve):
                link = Chain(dve, own)
                dve.wait_ge(loaded, 16 * (len(loads) + 1))
                nc.vector.tensor_tensor(wkw[:, :], wk[:, :], wpb[:, :], ALU.mult).then_inc(wk_scaled, 1)
                link(nc.vector.tensor_tensor(c.bias[:, 0:3], bih[:, :], bhh[:, :], ALU.add))
                link(nc.vector.tensor_scalar(c.bias[:, 0:2], c.bias[:, 0:2], 0.5, None, ALU.mult))
                nc.vector.tensor_copy(c.bias[:, 3:4], bih[:, 2:3])
                nc.vector.tensor_copy(c.bias[:, 4:5], bhh[:, 2:3])
                dve.wait_ge(folded, 2)
                nc.vector.tensor_scalar(c.mq[:, :], mq_ps[:, 0:128], ws[:, 0:1], float(D) ** -0.5, ALU.mult, ALU.mult)
                link(nc.vector.tensor_scalar(c.wcT[:, :], wc_ps[:, 0:384], wp[:, 0:1], None, ALU.mult))

            @block.tensor
            def _(pe):
                pe.wait_ge(wk_scaled, 1)
                nc.tensor.matmul(mq_ps[:, 0:128], wq[:, :], wkw[:, :], start=True, stop=True).then_inc(folded, 1)
                nc.tensor.matmul(wc_ps[:, 0:384], wv[:, :], wih[:, :], start=True, stop=True).then_inc(folded, 1)


def slot_attention_stage(nc, c, ctx_dram):
    R = 3
    LANES = range(2)
    TURNS = B // 4
    EPS = 1e-6
    with ExitStack() as ctx:
        m = Memory(nc, ctx, "sa")
        raw = [[m.sb(f"raw{l}{b}", [128, NC_, D]) for b in range(2)] for l in LANES]
        pn = [[m.sb(f"pn{l}{b}", [128, NC_, D + 1]) for b in range(2)] for l in LANES]
        pnT = [[m.sb(f"pnT{l}{b}", [128, NC_ * 128]) for b in range(2)] for l in LANES]
        e = [[m.sb(f"e{l}{b}", [128, NC_, S]) for b in range(2)] for l in LANES]
        ms = [[m.sb(f"ms{l}{b}", [128, 3, NC_]) for b in range(2)] for l in LANES]
        col = [[m.sb(f"col{l}{b}", [128, 3, NC_]) for b in range(2)] for l in LANES]
        slT = [m.sb(f"slotsT{l}", [128, 128]) for l in LANES]
        slsq = [m.sb(f"slots_sq{l}", [128, 128]) for l in LANES]
        sc = [m.sb(f"sc{l}", [128, 4]) for l in LANES]
        qn = [m.sb(f"qn{l}", [128, 128]) for l in LANES]
        qT = [m.sb(f"qT{l}", [128, 128]) for l in LANES]
        un = [m.sb(f"un{l}", [128, 128]) for l in LANES]
        uT = [m.sb(f"uT{l}", [128, 128]) for l in LANES]
        tr = [m.sb(f"tr{l}", [128, 2, 128]) for l in LANES]
        hn = [m.sb(f"hn{l}", [128, 2, 128]) for l in LANES]
        nn = [m.sb(f"nn{l}", [128, 128]) for l in LANES]
        Sb = [m.ps(f"scores{b}", [128, 1024]) for b in range(2)]
        U = [m.ps(f"u{l}") for l in LANES]
        G = [m.ps(f"g{l}") for l in LANES]

        per_lane = lambda name: [m.sem(f"{name}{l}") for l in LANES]
        loaded, squared, meansq, rstd, normed = map(per_lane, ("ctx_loaded", "ctx_squared", "ctx_meansq", "ctx_rstd", "ctx_normed"))
        t_psum, t_sbuf = m.sem("ctxT_psum"), m.sem("ctxT_sbuf")
        slots_in, sl_sq, q_nat, sl_meansq, sl_rstd, q_scaled, q_turned, q_ready = map(per_lane, (
            "slots_in", "slots_squared", "q_natural", "slots_meansq", "slots_rstd", "q_scaled", "q_turned", "q_ready"))
        scored = [m.sem(f"scored{b}") for b in range(2)]
        centred, exped, slot_sum, attn = map(per_lane, ("centred", "exped", "slot_sum_inv", "attn_ready"))
        summed, u_inv, u_scaled, u_turned, u_ready = map(per_lane, ("u_summed", "u_inv", "u_scaled", "u_turned", "u_ready"))
        gates, rz, n_in, n_out, slots, out_turned, added = map(per_lane, (
            "gates", "rz", "n_in", "n_out", "slots_new", "out_turned", "x_added"))
        zeroed, own = m.sem("zeroed"), m.sem("dve_own")
        OWN = 2 * (2 + R * (2 + 2 + 1 + 4))

        with nc.Block() as block:
            @block.sync
            def _(sp):
                def load(i, l):
                    for b in range(2):
                        rows = ctx_dram[bass.ds(4 * i + 2 * l + b, 1), :, :].rearrange("a m d -> (a m) d")
                        sp.dma_start(raw[l][b][:, 0:FULL, :], rows[0:128 * FULL, :].rearrange("(p c) d -> p c d", p=128)).then_inc(loaded[l], 16)
                        sp.dma_start(raw[l][b][0:TAIL, FULL, :], rows[128 * FULL:M, :]).then_inc(loaded[l], 16)

                sp.wait_ge(zeroed, 1)
                for l in LANES:
                    load(0, l)
                with sp.Fori(0, TURNS - 1) as i:
                    for l in LANES:
                        sp.wait_ge(normed[l], 2 * i + 2)
                        load(i + 1, l)

            @block.gpsimd
            def _(pool):
                with pool.Fori(0, TURNS) as i:
                    for l in LANES:
                        for b in range(2):
                            pool.wait_ge(meansq[l], 2 * i + b + 1)
                            nc.gpsimd.tensor_tensor(ms[l][b][:, 2, :], ms[l][b][:, 1, :], c.half[:, 0:NC_], ALU.pow).then_inc(rstd[l], 1)
                            pool.wait_ge(rstd[l], 2 * i + b + 1)
                            nc.gpsimd.tensor_tensor(pn[l][b][:, :, 0:D], raw[l][b][:, :, :], bc(ms[l][b][:, 2, :], D), ALU.mult).then_inc(normed[l], 1)
                    for t in range(R):
                        for l in LANES:
                            pool.wait_ge(sl_meansq[l], R * i + t + 1)
                            nc.gpsimd.tensor_tensor(sc[l][:, 1:2], sc[l][:, 0:1], c.half[:, 0:1], ALU.pow).then_inc(sl_rstd[l], 1)
                        for l in LANES:
                            for b in range(2):
                                pool.wait_ge(slot_sum[l], 2 * (R * i + t) + b + 1)
                                nc.gpsimd.tensor_tensor(e[l][b][:, :, :], e[l][b][:, :, :], bc(col[l][b][:, 2, :], S), ALU.mult).then_inc(attn[l], 1)

            @block.scalar
            def _(act):
                with act.Fori(0, TURNS) as i:
                    for l in LANES:
                        act.wait_ge(loaded[l], 64 * i + 64)
                        for b in range(2):
                            nc.scalar.activation(pn[l][b][:, :, 0:D], raw[l][b][:, :, :], ACT.Square).then_inc(squared[l], 1)
                    for l in LANES:
                        for b in range(2):
                            for q in range(4):
                                act.wait_ge(t_psum, 16 * i + 8 * l + 4 * b + q + 1)
                                w = min(512, NC_ * 128 - 512 * q)
                                nc.scalar.activation(pnT[l][b][:, 512 * q:512 * q + w], Sb[q // 2][:, 512 * (q % 2):512 * (q % 2) + w],
                                                     ACT.Copy).then_inc(t_sbuf, 1)
                        act.wait_ge(slots_in[l], i + 1)
                        nc.scalar.activation(slsq[l][:, :], slT[l][:, :], ACT.Square).then_inc(sl_sq[l], 1)
                    for t in range(R):
                        for l in LANES:
                            k = R * i + t + 1
                            act.wait_ge(sl_rstd[l], k)
                            nc.scalar.activation(qn[l][:, :], U[l][:, 0:128], ACT.Copy, scale=sc[l][:, 1:2]).then_inc(q_scaled[l], 1)
                            act.wait_ge(q_turned[l], k)
                            nc.scalar.activation(qT[l][:, :], U[l][:, 0:128], ACT.Copy).then_inc(q_ready[l], 1)
                        for l in LANES:
                            for b in range(2):
                                act.wait_ge(centred[l], 2 * (R * i + t) + b + 1)
                                nc.scalar.activation(e[l][b][:, :, :], e[l][b][:, :, :], ACT.Exp).then_inc(exped[l], 1)
                        for l in LANES:
                            k = R * i + t + 1
                            act.wait_ge(u_inv[l], k)
                            nc.scalar.activation(un[l][:, :], U[l][:, 0:128], ACT.Copy, scale=sc[l][:, 3:4]).then_inc(u_scaled[l], 1)
                            act.wait_ge(u_turned[l], k)
                            nc.scalar.activation(uT[l][:, :], U[l][:, 0:128], ACT.Copy).then_inc(u_ready[l], 1)
                        for l in LANES:
                            k = R * i + t + 1
                            act.wait_ge(gates[l], k)
                            nc.scalar.activation(tr[l][:, 0, :], G[l][:, 0:128], ACT.Tanh, bias=c.bias[:, 0:1], scale=0.5)
                            nc.scalar.activation(tr[l][:, 1, :], G[l][:, 128:256], ACT.Tanh, bias=c.bias[:, 1:2], scale=0.5).then_inc(rz[l], 1)
                            act.wait_ge(n_in[l], k)
                            nc.scalar.activation(nn[l][:, :], hn[l][:, 1, :], ACT.Tanh, bias=c.bias[:, 3:4]).then_inc(n_out[l], 1)
                            if t < R - 1:
                                act.wait_ge(slots[l], k)
                                nc.scalar.activation(slsq[l][:, :], slT[l][:, :], ACT.Square).then_inc(sl_sq[l], 1)

            @block.vector
            def _(dve):
                for l in LANES:
                    for b in range(2):
                        nc.vector.memset(raw[l][b][:, FULL, :], 0.0)
                        last = nc.vector.memset(pn[l][b][:, :, D:D + 1], 1.0)
                last.then_inc(zeroed, 1)
                with dve.Fori(0, TURNS) as i:
                    link = Chain(dve, own, OWN, i)
                    for l in LANES:
                        tile = 2 * i + l
                        nc.vector.tensor_copy(slT[l][:, :], c.XNT[:, bass.ts(tile, 128)]).then_inc(slots_in[l], 1)
                        for b in range(2):
                            dve.wait_ge(squared[l], 2 * i + b + 1)
                            link(nc.vector.tensor_reduce(out=ms[l][b][:, 0, :], in_=pn[l][b][:, :, 0:D], op=ALU.add, axis=AX.X))
                            nc.vector.tensor_scalar(ms[l][b][:, 1, :], ms[l][b][:, 0, :], 1.0 / D, EPS, ALU.mult, ALU.add).then_inc(meansq[l], 1)
                    for t in range(R):
                        for l in LANES:
                            k = R * i + t + 1
                            dve.wait_ge(q_nat[l], k)
                            nc.vector.tensor_scalar(sc[l][:, 0:1], U[l][:, 256:257], 1.0 / D, EPS, ALU.mult, ALU.add).then_inc(sl_meansq[l], 1)
                        for l in LANES:
                            for b in range(2):
                                view = Sb[b][:, 0:NC_ * S].rearrange("p (c s) -> p c s", s=S)
                                dve.wait_ge(scored[b], 2 * (R * i + t) + l + 1)
                                link(nc.vector.tensor_reduce(out=col[l][b][:, 0, :], in_=view, op=ALU.max, axis=AX.X))
                                nc.vector.tensor_tensor(e[l][b][:, :, :], view, bc(col[l][b][:, 0, :], S), ALU.subtract).then_inc(centred[l], 1)
                        for l in LANES:
                            for b in range(2):
                                dve.wait_ge(exped[l], 2 * (R * i + t) + b + 1)
                                link(nc.vector.tensor_reduce(out=col[l][b][:, 1, :], in_=e[l][b][:, :, :], op=ALU.add, axis=AX.X))
                                nc.vector.reciprocal(col[l][b][:, 2, :], col[l][b][:, 1, :]).then_inc(slot_sum[l], 1)
                        for l in LANES:
                            k = R * i + t + 1
                            dve.wait_ge(summed[l], k)
                            link(nc.vector.tensor_scalar(sc[l][:, 2:3], U[l][:, 128:129], EPS, None, ALU.add))
                            nc.vector.reciprocal(sc[l][:, 3:4], sc[l][:, 2:3]).then_inc(u_inv[l], 1)
                        for l in LANES:
                            k = R * i + t + 1
                            dve.wait_ge(rz[l], k)
                            link(nc.vector.tensor_scalar(hn[l][:, 0, :], U[l][:, 128:256], c.bias[:, 4:5], 0.5, ALU.add, ALU.mult))
                            link(nc.vector.scalar_tensor_tensor(out=hn[l][:, 0, :], in0=tr[l][:, 0, :], scalar=1.0, in1=hn[l][:, 0, :],
                                                                op0=ALU.add, op1=ALU.mult))
                            nc.vector.tensor_tensor(hn[l][:, 1, :], U[l][:, 0:128], hn[l][:, 0, :], ALU.add).then_inc(n_in[l], 1)
                            dve.wait_ge(n_out[l], k)
                            link(nc.vector.tensor_tensor(slT[l][:, :], slT[l][:, :], nn[l][:, :], ALU.subtract))
                            link(nc.vector.scalar_tensor_tensor(out=hn[l][:, 0, :], in0=tr[l][:, 1, :], scalar=1.0, in1=slT[l][:, :],
                                                                op0=ALU.add, op1=ALU.mult))
                            nc.vector.scalar_tensor_tensor(out=slT[l][:, :], in0=hn[l][:, 0, :], scalar=0.5, in1=nn[l][:, :],
                                                           op0=ALU.mult, op1=ALU.add).then_inc(slots[l], 1)
                    for l in LANES:
                        tile = 2 * i + l
                        dve.wait_ge(out_turned[l], i + 1)
                        xs = c.X[:, bass.ds(tile, 1), :].rearrange("p a d -> p (a d)")
                        nc.vector.tensor_tensor(xs, U[l][:, 0:128], xs, ALU.add).then_inc(added[l], 1)
                    link.close()

            @block.tensor
            def _(pe):
                with pe.Fori(0, TURNS) as i:
                    for l in LANES:
                        for b in range(2):
                            n = 2 * l + b
                            pe.wait_ge(normed[l], 2 * i + b + 1)
                            if n:
                                pe.wait_ge(t_sbuf, 16 * i + 4 * n)
                            for q in range(4):
                                for ch in range(4 * q, min(4 * q + 4, NC_)):
                                    o = 128 * (ch % 8)
                                    last = nc.tensor.transpose(Sb[q // 2][:, o:o + 128], pn[l][b][:, ch, 0:D], c.ident[:, :])
                                last.then_inc(t_psum, 1)
                    for t in range(R):
                        for l in LANES:
                            k = R * i + t + 1
                            pe.wait_ge(sl_sq[l], k)
                            nc.tensor.matmul(U[l][:, 256:257], slsq[l][:, :], c.ones[:, 0:1], start=True, stop=True)
                            nc.tensor.matmul(U[l][:, 0:128], slT[l][:, :], c.mq[:, :], start=True, stop=True).then_inc(q_nat[l], 1)
                        for l in LANES:
                            k = R * i + t + 1
                            pe.wait_ge(q_scaled[l], k)
                            nc.tensor.transpose(U[l][:, 0:128], qn[l][:, :], c.ident[:, :]).then_inc(q_turned[l], 1)
                            pe.wait_ge(q_ready[l], k)
                            if t == 0 and l == 0:
                                pe.wait_ge(t_sbuf, 16 * i + 16)
                            for b in range(2):
                                if l == 1:
                                    pe.wait_ge(centred[0], 2 * (R * i + t) + b + 1)
                                for ch in range(NC_):
                                    last = nc.tensor.matmul(Sb[b][:, S * ch:S * ch + S], pnT[l][b][:, 128 * ch:128 * ch + 128],
                                                            qT[l][:, S * b:S * b + S], start=True, stop=True)
                                last.then_inc(scored[b], 1)
                        for l in LANES:
                            k = R * i + t + 1
                            pe.wait_ge(attn[l], 2 * k)
                            for ch in range(NC_):
                                h = 128 if ch < FULL else TAIL
                                for b in range(2):
                                    last = nc.tensor.matmul(U[l][S * b:S * b + S, 0:D + 1], e[l][b][0:h, ch, :], pn[l][b][0:h, ch, :],
                                                            start=(ch == 0), stop=(ch == NC_ - 1))
                            last.then_inc(summed[l], 1)
                        for l in LANES:
                            k = R * i + t + 1
                            pe.wait_ge(u_scaled[l], k)
                            nc.tensor.transpose(U[l][:, 0:128], un[l][:, :], c.ident[:, :]).then_inc(u_turned[l], 1)
                            pe.wait_ge(u_ready[l], k)
                            for g, (out, parts) in enumerate([(G[l][:, 0:128], "xh"), (G[l][:, 128:256], "xh"), (U[l][:, 0:128], "x"), (U[l][:, 128:256], "h")]):
                                f = min(g, 2)
                                for part in parts:
                                    w, v = (c.wcT, uT[l]) if part == "x" else (c.whhT, slT[l])
                                    last = nc.tensor.matmul(out, w[:, 128 * f:128 * f + 128], v[:, :], start=(part == parts[0]), stop=(part == parts[-1]))
                            last.then_inc(gates[l], 1)
                    for l in LANES:
                        pe.wait_ge(slots[l], R * i + R)
                        nc.tensor.transpose(U[l][:, 0:128], slT[l][:, :], c.ident[:, :]).then_inc(out_turned[l], 1)


def linear_attention_stage(nc, c, p):
    E = 32
    with ExitStack() as ctx:
        m = Memory(nc, ctx, "la")
        wq, wk = m.sb("wq", [128, E]), m.sb("wk", [128, E])
        qe, ke, kv = m.sb("q_expT", [E, T * 128]), m.sb("k_exp", [128, T, E]), m.sb("kv", [E, B, D + 1])
        z = m.sb("z", [128, 2, T])
        bank = [m.ps(f"bank{q}") for q in range(8)]
        loaded, q_mm, q_exp, k_mm, k_exp, kv_mm, kv_out, num_mm, ones_set, done = (m.sem(n) for n in (
            "loaded", "q_projected", "q_exp", "k_projected", "k_exp", "kv_summed", "kv_copied", "numerators", "ones_set", "added"))
        own = m.sem("dve_own")
        PER = 3
        SETS = [(t, min(PER, T - t)) for t in range(0, T, PER)]
        with nc.Block() as block:
            @block.sync
            def _(sp):
                sp.dma_start(wq[:, :], p["L0_attn_q_proj"]).then_inc(loaded, 16)
                sp.dma_start(wk[:, :], p["L0_attn_k_proj"]).then_inc(loaded, 16)

            @block.tensor
            def _(pe):
                pe.wait_ge(loaded, 32)
                for t in range(T):
                    last = nc.tensor.matmul(bank[4][:, E * t:E * t + E], c.XNT[:, 128 * t:128 * t + 128], wk[:, :], start=True, stop=True)
                last.then_inc(k_mm, 1)
                for q in range(4):
                    nc.tensor.matmul(bank[q][0:E, :], wq[:, :], c.XNT[:, 512 * q:512 * q + 512], start=True, stop=True).then_inc(q_mm, 1)
                pe.wait_ge(k_exp, 1)
                for b in range(B):
                    q, h, o = 2 * (b // 8) + b % 2, 64 * (b % 2), 128 * (b // 2 % 4)
                    if q < 4 and b % 8 < 2:
                        pe.wait_ge(q_exp, q + 1)
                    last = nc.tensor.matmul(bank[q][0:E, o:o + 128], ke[h:h + 64, b // 2, :],
                                            c.XN[h:h + 64, b // 2, :], start=True, stop=True)
                    if b % 8 >= 6:
                        last.then_inc(kv_mm, 1)
                for n, (t0, k) in enumerate(SETS):
                    pe.wait_ge(kv_out, 9)
                    for t in range(t0, t0 + k):
                        for b in (2 * t, 2 * t + 1):
                            h, o = 64 * (b % 2), (D + 1) * (t - t0)
                            last = nc.tensor.matmul(bank[n][h:h + 64, o:o + D + 1], qe[:, 64 * b:64 * b + 64], kv[:, b, :], start=True, stop=True)
                    last.then_inc(num_mm, 1)

            @block.scalar
            def _(act):
                act.wait_ge(k_mm, 1)
                nc.scalar.activation(ke[:, :, :], bank[4][:, 0:T * E].rearrange("p (t e) -> p t e", e=E), ACT.Exp).then_inc(k_exp, 1)
                for q in range(4):
                    act.wait_ge(q_mm, q + 1)
                    nc.scalar.activation(qe[:, 512 * q:512 * q + 512], bank[q][0:E, :], ACT.Exp).then_inc(q_exp, 1)

            @block.vector
            def _(dve):
                link = Chain(dve, own)
                nc.vector.memset(kv[:, :, D:D + 1], 1.0).then_inc(kv_out, 1)
                for q in range(8):
                    dve.wait_ge(kv_mm, q + 1)
                    b0 = 8 * (q // 2) + q % 2
                    nc.vector.tensor_copy(kv[:, b0:b0 + 7:2, 0:D], bank[q][0:E, :].rearrange("p (b d) -> p b d", d=D)).then_inc(kv_out, 1)
                for n, (t0, k) in enumerate(SETS):
                    dve.wait_ge(num_mm, n + 1)
                    sums = bank[n][:, 0:k * (D + 1)].rearrange("p (t d) -> p t d", d=D + 1)[:, :, D]
                    link(nc.vector.tensor_scalar(z[:, 0, t0:t0 + k], sums, 1e-8, None, ALU.add))
                    link(nc.vector.reciprocal(z[:, 1, t0:t0 + k], z[:, 0, t0:t0 + k]))
                    for t in range(t0, t0 + k):
                        o = (D + 1) * (t - t0)
                        last = nc.vector.scalar_tensor_tensor(out=c.X[:, t, :], in0=bank[n][:, o:o + D], scalar=z[:, 1, t:t + 1],
                                                              in1=c.X[:, t, :], op0=ALU.mult, op1=ALU.add)
                last.then_inc(done, 1)


def capacity_moe_stage(nc, c, p):
    X8, I, CAP = 8, 512, 256
    J, SL = I // 128, CAP // 128
    TRASH = X8 * CAP
    with ExitStack() as ctx:
        m = Memory(nc, ctx, "cm")
        TK, DS, DT = m.sb("tokens", [128, T, D]), m.sb("dispatched", [128, T, D]), m.sb("dispatchedT", [128, T * 128])
        wi, wo = m.sb("wi", [128, X8, I]), m.sb("wo", [128, X8, J, D])
        H = [m.sb(f"hidden{k}", [128, J, CAP]) for k in range(2)]
        gw, ln = m.sb("gateT", [128, X8]), m.sb("ln", [128, 2])
        tokT = m.sb("tokT", [128, T * 128])
        before, rev, offs = m.sb("before", [128, 128]), m.sb("rev", [128, X8]), m.sb("offs", [128, X8])
        lg, w1, w2, oh = (m.sb(n, [128, T, X8]) for n in ("logits", "work1", "work2", "onehot"))
        col = m.sb("col", [128, 8, T])
        idx, gidx = m.sb("idx", [128, T], i32), m.sb("gather_idx", [128, T], i32)
        zrow, trash = m.sb("zrow", [128, D]), m.sb("trash_row", [128, T])
        st, work = m.sb("stats", [128, 5, T]), DS
        bank = [m.ps(f"bank{q}") for q in range(8)]
        slots_dram = nc.dram_tensor("slots_in", (TRASH + 128 * T, D), fp32, kind="Internal").ap()
        eout_dram = nc.dram_tensor("slots_out", (TRASH + 128, D), fp32, kind="Internal").ap()
        s, own = NormSems(m), m.sem("dve_own")
        loaded, w_loaded, const, zero, zeroed, logit, expd, chose, ranked, routed = (m.sem(n) for n in (
            "loaded", "w_loaded", "const", "zero", "zeroed", "logits", "exp", "chosen", "ranks", "routed"))
        sent, back, turned, dt_out, up, act_out, down, eo, eo_out, got, added, trashed, dve_up = (m.sem(n) for n in (
            "sent", "back", "turned", "dispT", "up", "hidden", "down", "expert_rows", "stored", "gathered", "added", "trashed", "dve_up"))
        with nc.Block() as block:
            @block.sync
            def _(sp):
                sp.dma_start(gw[:, :], p["gateT0"]).then_inc(loaded, 16)
                sp.dma_start(ln[:, :], p["ln_cols"]).then_inc(loaded, 16)
                sp.dma_start(wi[:, :, :], p["wi"].rearrange("e h i -> h e i")).then_inc(w_loaded, 16)
                sp.dma_start(wo[:, :, :, :], p["wo"].rearrange("e (j i) h -> i e j h", i=128)).then_inc(w_loaded, 16)
                sp.wait_ge(zero, 1)
                sp.dma_start(slots_dram[0:TRASH, :].rearrange("(t p) d -> p t d", p=128), TK[:, :, :]).then_inc(zeroed, 16)
                sp.dma_start(eout_dram[TRASH:TRASH + 128, :], zrow[:, :]).then_inc(zeroed, 16)
                sp.wait_ge(sent, 16 * T)
                sp.dma_start(DS[:, :, :], slots_dram[0:TRASH, :].rearrange("(t p) d -> p t d", p=128)).then_inc(back, 16)
                for e in range(X8):
                    sp.wait_ge(eo, e + 1)
                    rows = eout_dram[CAP * e:CAP * e + CAP, :].rearrange("(t p) d -> p t d", p=128)
                    sp.dma_start(rows, DS[:, SL * e:SL * e + SL, :]).then_inc(eo_out, 16)
                sp.wait_ge(eo_out, 16 * X8)
                sp.wait_ge(zeroed, 32)

            @block.gpsimd
            def _(pool):
                nc.gpsimd.memset(TK[:, :, :], 0.0)
                nc.gpsimd.memset(zrow[:, :], 0.0).then_inc(zero, 1)
                nc.gpsimd.iota(trash[:, :], pattern=[[128, T]], base=TRASH, channel_multiplier=1, allow_small_or_imprecise_dtypes=True)
                nc.gpsimd.iota(rev[:, :], pattern=[[-1, X8]], base=X8, channel_multiplier=0, allow_small_or_imprecise_dtypes=True)
                nc.gpsimd.iota(offs[:, :], pattern=[[CAP, X8]], base=0, channel_multiplier=0, allow_small_or_imprecise_dtypes=True).then_inc(const, 1)
                nc.gpsimd.affine_select(out=before[:, :], in_=c.ones[:, :], compare_op=ALU.is_gt, fill=0.0,
                                        base=0, pattern=[[1, 128]], channel_multiplier=-1).then_inc(const, 1)
                norm_pool(nc, pool, st, c.half, s)
                pool.wait_ge(routed, 1)
                pool.wait_ge(zeroed, 32)
                pool.wait_ge(s.normed, 1)
                for t in range(T):
                    nc.gpsimd.indirect_dma_start(out=slots_dram, out_offset=bass.IndirectOffsetOnAxis(ap=idx[:, t:t + 1], axis=0),
                                                 in_=TK[:, t, :], in_offset=None).then_inc(sent, 16)
                pool.wait_ge(eo_out, 16 * X8)
                pool.wait_ge(sent, 16 * T)
                for t in range(T):
                    nc.gpsimd.indirect_dma_start(out=TK[:, t, :], out_offset=None, in_=eout_dram,
                                                 in_offset=bass.IndirectOffsetOnAxis(ap=gidx[:, t:t + 1], axis=0)).then_inc(got, 16)
                pool.wait_ge(got, 16 * T)

            @block.vector
            def _(dve):
                link = Chain(dve, own)
                dve.wait_ge(zeroed, 32)
                norm_dve(nc, dve, link, c.XN, TK, work, st, s, 1e-5)
                dve.wait_ge(loaded, 32)
                for q in range(4):
                    dve.wait_ge(s.transposed, q + 1)
                    nc.vector.tensor_scalar(tokT[:, 512 * q:512 * q + 512], bank[q][:, :], ln[:, 0:1], ln[:, 1:2], ALU.mult, ALU.add).then_inc(s.xnt_dve, 1)
                dve.wait_ge(logit, 1)
                dve.wait_ge(const, 2)
                link(nc.vector.tensor_copy(lg[:, :, :], bank[4][:, 0:T * X8].rearrange("p (t e) -> p t e", e=X8)))
                link(nc.vector.tensor_reduce(out=col[:, 0, :], in_=lg[:, :, :], op=ALU.max, axis=AX.X))
                link(nc.vector.tensor_tensor(w1[:, :, :], lg[:, :, :], bc(col[:, 0, :], X8), ALU.subtract))
                nc.vector.tensor_scalar(w2[:, :, :], w1[:, :, :], 0.0, None, ALU.is_equal).then_inc(chose, 1)
                dve.wait_ge(chose, 1)
                rev_all = rev[:, :].unsqueeze(1).to_broadcast([128, T, X8])
                link(nc.vector.tensor_tensor(w2[:, :, :], w2[:, :, :], rev_all, ALU.mult))
                link(nc.vector.tensor_reduce(out=col[:, 1, :], in_=w2[:, :, :], op=ALU.max, axis=AX.X))
                nc.vector.tensor_tensor(oh[:, :, :], w2[:, :, :], bc(col[:, 1, :], X8), ALU.is_equal).then_inc(chose, 1)
                dve.wait_ge(expd, 1)
                link(nc.vector.tensor_reduce(out=col[:, 2, :], in_=w1[:, :, :], op=ALU.add, axis=AX.X))
                link(nc.vector.reciprocal(col[:, 3, :], col[:, 2, :]))
                dve.wait_ge(ranked, 1)
                src, dst = w1, w2
                link(nc.vector.memset(src[:, 0:1, :], 0.0))
                link(nc.vector.tensor_copy(src[:, 1:T, :], bank[5][:, 128:128 + (T - 1) * X8].rearrange("p (t e) -> p t e", e=X8)))
                k = 1
                while k < T:
                    nc.vector.tensor_copy(dst[:, 0:k, :], src[:, 0:k, :])
                    link(nc.vector.tensor_tensor(dst[:, k:T, :], src[:, k:T, :], src[:, 0:T - k, :], ALU.add))
                    src, dst, k = dst, src, 2 * k
                link(nc.vector.tensor_tensor(dst[:, :, :], bank[5][:, 0:128].rearrange("p (t e) -> p t e", e=X8), src[:, :, :], ALU.add))
                link(nc.vector.tensor_tensor(dst[:, :, :], dst[:, :, :], oh[:, :, :], ALU.mult))
                link(nc.vector.tensor_reduce(out=col[:, 4, :], in_=dst[:, :, :], op=ALU.add, axis=AX.X))
                link(nc.vector.tensor_scalar(col[:, 5, :], col[:, 4, :], float(CAP), None, ALU.is_lt))
                link(nc.vector.tensor_tensor(col[:, 3, :], col[:, 3, :], col[:, 5, :], ALU.mult))
                link(nc.vector.tensor_tensor(src[:, :, :], oh[:, :, :], offs[:, :].unsqueeze(1).to_broadcast([128, T, X8]), ALU.mult))
                link(nc.vector.tensor_reduce(out=col[:, 6, :], in_=src[:, :, :], op=ALU.add, axis=AX.X))
                link(nc.vector.tensor_tensor(col[:, 6, :], col[:, 6, :], col[:, 4, :], ALU.add))
                link(nc.vector.tensor_tensor(col[:, 0, :], col[:, 6, :], trash[:, :], ALU.subtract))
                link(nc.vector.tensor_tensor(col[:, 0, :], col[:, 0, :], col[:, 5, :], ALU.mult))
                nc.vector.tensor_tensor(idx[:, :], col[:, 0, :], trash[:, :], ALU.add)
                link(nc.vector.tensor_scalar(col[:, 1, :], col[:, 6, :], -float(TRASH), None, ALU.add))
                link(nc.vector.tensor_tensor(col[:, 1, :], col[:, 1, :], col[:, 5, :], ALU.mult))
                nc.vector.tensor_scalar(gidx[:, :], col[:, 1, :], float(TRASH), None, ALU.add).then_inc(routed, 1)
                link(nc.vector.tensor_tensor(c.X[:, :, :], c.X[:, :, :], c.XN[:, :, :], ALU.add))
                for q in range(4):
                    dve.wait_ge(turned, q + 1)
                    nc.vector.tensor_scalar(DT[:, 512 * q:512 * q + 512], bank[q][:, :], ln[:, 0:1], ln[:, 1:2], ALU.mult, ALU.add).then_inc(dt_out, 1)
                for e in range(X8):
                    dve.wait_ge(down, e + 1)
                    nc.vector.tensor_copy(DS[:, SL * e:SL * e + SL, :], bank[6 + e % 2][:, 0:SL * D].rearrange("p (t d) -> p t d", d=D)).then_inc(eo, 1)
                dve.wait_ge(got, 16 * T)
                for t in range(T):
                    last = nc.vector.scalar_tensor_tensor(out=c.X[:, t, :], in0=TK[:, t, :], scalar=col[:, 3, t:t + 1], in1=c.X[:, t, :],
                                                          op0=ALU.mult, op1=ALU.add)
                last.then_inc(added, 1)

            @block.scalar
            def _(act):
                norm_act(nc, act, TK, work, s)
                act.wait_ge(chose, 1)
                nc.scalar.activation(w1[:, :, :], w1[:, :, :], ACT.Exp).then_inc(expd, 1)
                for e in range(X8):
                    for j in range(J):
                        n = J * e + j
                        act.wait_ge(up, n + 1)
                        if e >= 2 and j == 0:
                            act.wait_ge(down, e - 1)
                        nc.scalar.activation(H[e % 2][:, j, :], bank[n % 4][:, 0:CAP], ACT.Gelu).then_inc(act_out, 1)

            @block.tensor
            def _(pe):
                transpose_pe(nc, pe, TK, bank, c.ident, s)
                pe.wait_ge(s.xnt_dve, 4)
                for t in range(T):
                    last = nc.tensor.matmul(bank[4][:, X8 * t:X8 * t + X8], tokT[:, 128 * t:128 * t + 128], gw[:, :], start=True, stop=True)
                last.then_inc(logit, 1)
                pe.wait_ge(chose, 2)
                oh2 = oh[:, :, :].rearrange("p t e -> p (t e)")
                nc.tensor.matmul(bank[5][:, 0:128], before[:, :], oh2, start=True, stop=True)
                nc.tensor.matmul(bank[5][:, 128:256], c.ones[:, :], oh2, start=True, stop=True).then_inc(ranked, 1)
                pe.wait_ge(back, 16)
                for q in range(4):
                    for j in range(4):
                        last = nc.tensor.transpose(bank[q][:, 128 * j:128 * j + 128], DS[:, 4 * q + j, :], c.ident[:, :])
                    last.then_inc(turned, 1)
                pe.wait_ge(w_loaded, 32)
                pe.wait_ge(dt_out, 4)
                for e in range(X8):
                    for j in range(J):
                        n = J * e + j
                        if n >= 4:
                            pe.wait_ge(act_out, n - 3)
                        nc.tensor.matmul(bank[n % 4][:, 0:CAP], wi[:, e, 128 * j:128 * j + 128], DT[:, CAP * e:CAP * e + CAP],
                                         start=True, stop=True).then_inc(up, 1)
                    pe.wait_ge(act_out, J * e + J)
                    if e >= 2:
                        pe.wait_ge(eo, e - 1)
                    for k in range(SL):
                        for j in range(J):
                            last = nc.tensor.matmul(bank[6 + e % 2][:, D * k:D * k + D], H[e % 2][:, j, 128 * k:128 * k + 128], wo[:, e, j, :],
                                                    start=(j == 0), stop=(j == J - 1))
                    last.then_inc(down, 1)


def masked_attention_stage(nc, c, p):
    H, DH, MASKED = 16, 8, -1e30
    ORDER = ((0, 2), (1, 3))
    PIECES = [(512 * w, min(512, M - 512 * w)) for w in range(4)]
    STEPS = [(j, w) for js in ORDER for w in range(4) for j in js]
    FIRST, MID = 4, 9
    AHEAD = {4: 0, 6: 1, 8: 2, 10: 3, 12: 4, 13: 5, 14: 6, 15: 7}
    BY_ACT = (1, 3, 5, 6, 8, 10, 12)
    acts = lambda ch: sum(x < ch for x in BY_ACT)
    A, V_ = len(BY_ACT), NC_ - len(BY_ACT)
    with ExitStack() as ctx:
        m = Memory(nc, ctx, "ma")
        wq, wk, wv, wo, bo = (m.sb(n, [128, 128]) for n in ("wq", "wk", "wv", "wo", "bo"))
        QT, OT = c.XN[:, :, :].rearrange("p t d -> p (t d)"), m.sb("outT", [128, T * 128])
        cT = [m.sb(f"ctxT{k}", [128, M]) for k in range(2)]
        KT = [m.sb(f"kT{k}", [128, M]) for k in range(2)]
        V = [m.sb(f"v{k}", [128, NC_, 128]) for k in range(2)]
        mraw = [m.sb("mask_raw", [128, M], i32)] * 2
        mb = [m.sb(f"mask_bias{k}", [128, M]) for k in range(2)]
        QB = [m.sb(f"q_blocks{k}", [128, 8, S]) for k in range(2)]
        E = [[m.sb(f"e{k}{j}", [128, M]) for j in range(4)] for k in range(2)]
        ET = [m.sb(f"eT{k}", [128, 512]) for k in range(4)]
        mx, nmx, den = ([m.sb(f"{n}{k}", [128, w]) for k in range(2)] for n, w in (("mx", 16), ("nmx", 4), ("den", 8)))
        rden, lm = m.sb("rden", [128, 8]), m.sb("den_blocks", [128, 8, 16])
        acc = m.sb("acc", [128, S])
        blk8, blk4, half2, eye2 = m.sb("blk8", [128, 8]), m.sb("blk4", [128, 4]), m.sb("half2", [128, 2]), m.sb("eye2", [128, S])
        Sb = [m.ps(f"scores{w}") for w in range(4)]
        TB = [m.ps(f"turned{w}") for w in range(2)]
        OB, PB = m.ps("sums"), m.ps("proj")

        (w_loaded, const, q_mm, q_out, mask_ready, q_ready, scored, maxed, nmaxed, exped, turned, et_act, et_dve, summed, o_read,
         projected, k_out, v_out, lm_ready, out_mm, added) = (m.sem(n) for n in (
            "w_loaded", "const", "q_projected", "q_scaled", "mask_ready", "q_ready", "scored", "maxed", "nmaxed", "exped", "turned",
            "et_act", "et_dve", "summed", "o_read", "projected", "k_out", "v_out", "lm_ready", "out_projected", "added"))
        ctx_loaded = [m.sem(f"ctx_loaded{k}") for k in range(2)]
        mask_loaded = m.sem("mask_loaded")
        own, own_first, own_last = m.sem("dve_own"), m.sem("dve_own_first"), m.sem("dve_own_last")
        dve_passed, pool_passed = m.sem("dve_passed"), m.sem("pool_passed")
        PAIRS = B // 2

        def slots(turn):
            return [(s, s // 2, s % 2) for s in range(4)]

        with nc.Block() as block:
            @block.sync
            def _(sp):
                for dst, name in ((wq, "WqT1"), (wk, "WkT1"), (wv, "WvT1"), (wo, "WoT1")):
                    sp.dma_start(dst[:, :], p[name]).then_inc(w_loaded, 16)
                sp.dma_start(bo[:, :], p["bo"].partition_broadcast(128)).then_inc(w_loaded, 16)
                sp.wait_ge(w_loaded, 80)

            @block.gpsimd
            def _(pool):
                nc.gpsimd.memset(blk8[:, :], 0.0)
                nc.gpsimd.memset(blk4[:, :], 0.0)
                nc.gpsimd.affine_select(out=half2[:, 0:1], in_=c.ones[:, 0:1], compare_op=ALU.is_ge, fill=0.0, base=63, pattern=[[0, 1]], channel_multiplier=-1)
                nc.gpsimd.affine_select(out=half2[:, 1:2], in_=c.ones[:, 0:1], compare_op=ALU.is_ge, fill=0.0, base=-64, pattern=[[0, 1]], channel_multiplier=1)
                nc.gpsimd.memset(eye2[:, :], 0.0).then_inc(const, 1)
                n = 1
                fills = [(blk8, 8, 8, r + 64 * h) for h in range(2) for r in range(8)]
                fills += [(blk4, 4, 8, r + 32 * h) for h in range(4) for r in range(8)]
                fills += [(eye2, S, 1, 64 * h) for h in range(2)]
                for dst, k, step, base in fills:
                    pool.wait_ge(const, n)
                    nc.gpsimd.affine_select(out=dst[:, :], in_=dst[:, :], compare_op=ALU.not_equal, fill=1.0, base=-base,
                                            pattern=[[-step, k]], channel_multiplier=1).then_inc(const, 1)
                    n += 1

            @block.tensor
            def _(pe):
                pe.wait_ge(w_loaded, 80)
                for q in range(4):
                    nc.tensor.matmul(Sb[q][:, :], wq[:, :], c.XNT[:, 512 * q:512 * q + 512], start=True, stop=True).then_inc(q_mm, 1)

            @block.scalar
            def _(act):
                for q in range(4):
                    act.wait_ge(q_mm, q + 1)
                    nc.scalar.activation(QT[:, 512 * q:512 * q + 512], Sb[q][:, :], ACT.Copy, scale=float(DH) ** -0.5).then_inc(q_out, 1)

        with nc.Block() as block:
            @block.sync
            def _(sp):
                def load(b, k, first=False):
                    sp.dma_start(cT[k][:, :], p["ctxT"][bass.ds(b, 1), :, :].rearrange("a d m -> (a d) m")).then_inc(ctx_loaded[k], 16)
                    if not first:
                        sp.wait_ge(mask_ready, b)
                    rows = p["mask"][bass.ds(b, 1), :, :].rearrange("a s m -> (a s) m")
                    for h in range(2):
                        sp.dma_start(mraw[k][64 * h:64 * h + 64, :], rows).then_inc(mask_loaded, 16)

                load(0, 0, True)
                load(1, 1)
                with sp.Fori(1, PAIRS) as i:
                    for k in range(2):
                        sp.wait_ge(projected, 16 * i - 8 + 8 * k)
                        load(2 * i + k, k)

            @block.gpsimd
            def _(pool):
                def prepare(i, k, first=False):
                    b = 2 * i + k
                    if not first:
                        pool.wait_ge(maxed, 64 * i + 32 * k - 32)
                    pool.wait_ge(mask_loaded, 32 * b + 32)
                    pool.sem_inc(pool_passed, 1)
                    nc.gpsimd.tensor_scalar(mb[k][:, :], mraw[k][:, :], 0, MASKED, ALU.is_equal, ALU.mult).then_inc(mask_ready, 1)
                    q = QT[:, bass.ds(64 * b, S)].unsqueeze(1).to_broadcast([128, 8, S])
                    nc.gpsimd.tensor_tensor(QB[k][:, :, :], q, bc(blk8[:, :], S), ALU.mult).then_inc(q_ready, 1)

                prepare(0, 0, True)
                prepare(0, 1, True)
                with pool.Fori(1, PAIRS) as i:
                    prepare(i, 0)
                    prepare(i, 1)

            @block.tensor
            def _(pe):
                def project(i, k, n, last_of_all=False):
                    if n == 0:
                        pe.wait_ge(ctx_loaded[k], 16 * i + 16)
                    if n < 4:
                        o, w = PIECES[n]
                        if not (isinstance(i, int) and i == 0 and k == 0 and n == 0):
                            if n == 0:
                                pe.wait_ge(v_out, 4 * (2 * i + k))
                            else:
                                pe.wait_ge(k_out, 4 * (2 * i + k) + n)
                        nc.tensor.matmul(PB[:, 0:w], wk[:, :], cT[k][:, o:o + w], start=True, stop=True).then_inc(projected, 1)
                        return
                    if n == 4:
                        pe.wait_ge(k_out, 4 * (2 * i + k) + 4)
                    else:
                        pe.wait_ge(v_out, 4 * (2 * i + k) + n - 4)
                    for ch in range(4 * (n - 4), min(4 * (n - 4) + 4, NC_)):
                        h = 128 if ch < FULL else TAIL
                        last = nc.tensor.matmul(PB[0:h, 128 * (ch % 4):128 * (ch % 4) + 128], cT[k][:, 128 * ch:128 * ch + h], wv[:, :], start=True, stop=True)
                    last.then_inc(projected, 1)

                def step(i, s, k, a, r):
                    j, w = STEPS[r]
                    o, width = PIECES[w]
                    g = 2 * j + a
                    n = 16 * (4 * i + s) + r
                    if r == 0 and a == 0:
                        pe.wait_ge(q_ready, 2 * i + k + 1)
                        pe.wait_ge(k_out, 4 * (2 * i + k) + 4)
                    if not (isinstance(n, int) and n < 4):
                        pe.wait_ge(maxed, n - 3)
                    rows = slice(64 * (g // 4), 64 * (g // 4) + 64)
                    nc.tensor.matmul(Sb[r % 4][:, 0:width], QB[k][rows, 2 * (g % 4):2 * (g % 4) + 2, :].rearrange("p n q -> p (n q)"),
                                     KT[k][rows, o:o + width], start=True, stop=True).then_inc(scored, 1)

                def turn(i, s, ch):
                    h = 128 if ch < FULL else TAIL
                    if ch == 0:
                        pe.wait_ge(exped, 4 * (4 * i + s))
                    for j in range(4):
                        last = nc.tensor.transpose(TB[ch % 2][0:h, 128 * j:128 * j + 128], E[(s - 1) % 2][j][:, 128 * ch:128 * ch + h], c.ident[:, :])
                    last.then_inc(turned, 1)

                def weigh(i, s, ch):
                    v, h = 4 * i + s - 1, 128 if ch < FULL else TAIL
                    kb = ((s - 1) // 2) % 2
                    if ch in BY_ACT:
                        pe.wait_ge(et_act, A * v + acts(ch) + 1)
                    else:
                        pe.wait_ge(et_dve, V_ * v + ch - acts(ch) + 1)
                    if ch == 0:
                        if not (isinstance(v, int) and v == 0):
                            pe.wait_ge(o_read, v)
                        pe.wait_ge(v_out, 4 * (v_batch(i, s) + 1))
                    for j in range(4):
                        last = nc.tensor.matmul(OB[32 * j:32 * j + 32, 0:128], V[kb][0:h, ch, 32 * j:32 * j + 32], ET[ch % 4][0:h, 128 * j:128 * j + 128],
                                                start=(ch == 0), stop=(ch == NC_ - 1))
                    if ch == NC_ - 1:
                        if (s - 1) % 2 == 1:
                            pe.wait_ge(lm_ready, v_batch(i, s) + 1)
                            last = nc.tensor.matmul(OB[:, 128:128 + S], lm[:, :, :].rearrange("p g n -> p (g n)"), eye2[:, :], start=True, stop=True)
                        last.then_inc(summed, 1)

                def v_batch(i, s):
                    return 2 * i + (s - 1) // 2

                def slot(i, s, k, a, scores=True, before=True, ahead=True):
                    for r in range(16):
                        if scores:
                            step(i, s, k, a, r)
                        if before and r >= FIRST:
                            chunks = [r - FIRST] + ([NC_ - 1] if r == 15 else [])
                            for ch in chunks:
                                turn(i, s, ch)
                                if ch:
                                    weigh(i, s, ch - 1)
                        if a == 1 and ahead and r in AHEAD:
                            project(i + k, 1 - k, AHEAD[r])
                    if before:
                        weigh(i, s, NC_ - 1)

                for n in range(8):
                    project(0, 0, n)
                for s, k, a in slots(0):
                    slot(0, s, k, a, before=s > 0)
                with pe.Fori(1, PAIRS - 1) as i:
                    for s, k, a in slots(i):
                        slot(i, s, k, a)
                for s, k, a in slots(0):
                    slot(PAIRS - 1, s, k, a, ahead=s < 2)
                slot(PAIRS, 0, 0, 0, scores=False)

            @block.vector
            def _(dve):
                def finish(i, s, link):
                    w = 4 * i + s - 2
                    a = (s - 2) % 2
                    dve.wait_ge(summed, w + 1)
                    if a == 0:
                        link(nc.vector.tensor_scalar(acc[:, :], OB[:, 0:S], blk4[:, 0:1], None, ALU.mult))
                    else:
                        link(nc.vector.scalar_tensor_tensor(out=acc[:, :], in0=OB[:, 0:S], scalar=blk4[:, 2:3], in1=acc[:, :], op0=ALU.mult, op1=ALU.add))
                    ins = nc.vector.scalar_tensor_tensor(out=acc[:, :], in0=OB[:, S:2 * S], scalar=blk4[:, 2 * a + 1:2 * a + 2], in1=acc[:, :], op0=ALU.mult, op1=ALU.add)
                    if a == 0:
                        ins.then_inc(o_read, 1)
                        return
                    link(ins)
                    b = 2 * i + (s - 2) // 2
                    nc.vector.tensor_tensor(OT[:, bass.ds(64 * b, S)], acc[:, :], OB[:, 128:128 + S], ALU.mult).then_inc(o_read, 1)

                def slot(i, s, k, a, link, scores=True, before=True, ahead=True, after=True):
                    e = s % 2
                    if scores and (a == 0):
                        dve.wait_ge(mask_ready, 2 * i + k + 1)
                    if after and scores:
                        dve.wait_ge(turned, NC_ * (4 * i + s - 1))
                    for r in range(16):
                        if scores:
                            j, w = STEPS[r]
                            o, width = PIECES[w]
                            dve.wait_ge(scored, 16 * (4 * i + s) + r + 1)
                            dve.sem_inc(dve_passed, 1)
                            nc.vector.tensor_tensor_reduce(out=E[e][j][:, o:o + width], in0=Sb[r % 4][:, 0:width], in1=mb[k][:, o:o + width],
                                                           scale=1.0, scalar=-3e38, op0=ALU.add, op1=ALU.max,
                                                           accum_out=mx[e][:, 4 * j + w:4 * j + w + 1]).then_inc(maxed, 1)
                            if r in (7, 15):
                                dve.wait_ge(maxed, 16 * (4 * i + s) + r + 1)
                                for jj in ORDER[r // 8]:
                                    nc.vector.tensor_reduce(out=nmx[e][:, jj:jj + 1], in_=mx[e][:, 4 * jj:4 * jj + 4], op=ALU.max, axis=AX.X,
                                                            negate=True).then_inc(nmaxed, 1)
                        if r == 1 and after:
                            finish(i, s, link)
                        if before and r == 6 and (s - 1) % 2 == 1:
                            dve.wait_ge(exped, 4 * (4 * i + s))
                            link(nc.vector.reciprocal(rden[:, :], den[((s - 1) // 2) % 2][:, :]))
                            nc.vector.tensor_tensor(lm[:, :, :].rearrange("p g (h d) -> p g h d", h=2), rden[:, :].unsqueeze(2).unsqueeze(3).to_broadcast([128, 8, 2, 8]),
                                                    half_view, ALU.mult).then_inc(lm_ready, 1)
                        if before and r >= FIRST:
                            for ch in [r - FIRST] + ([NC_ - 1] if r == 15 else []):
                                if ch not in BY_ACT:
                                    h = 128 if ch < FULL else TAIL
                                    dve.wait_ge(turned, NC_ * (4 * i + s - 1) + ch + 1)
                                    nc.vector.tensor_copy(ET[ch % 4][0:h, :], TB[ch % 2][0:h, :]).then_inc(et_dve, 1)
                        if a == 1 and ahead and AHEAD.get(r, 0) >= 4:
                            values(i + k, 1 - k, AHEAD[r] - 4)

                def values(i, k, n):
                    dve.wait_ge(projected, 8 * (2 * i + k) + 5 + n)
                    if n < 3:
                        nc.vector.tensor_copy(V[k][:, 4 * n:4 * n + 4, :], PB[:, :].rearrange("p (c d) -> p c d", d=128)).then_inc(v_out, 1)
                    else:
                        nc.vector.tensor_copy(V[k][0:TAIL, FULL, :], PB[0:TAIL, 0:128]).then_inc(v_out, 1)

                half_view = half2[:, :].unsqueeze(1).unsqueeze(3).to_broadcast([128, 8, 2, 8])
                OWN = 2 * (1 + 2) + 2

                for n in range(4):
                    values(0, 0, n)
                link = Chain(dve, own_first)
                for s, k, a in slots(0):
                    slot(0, s, k, a, link, before=s > 0, after=s > 1)
                with dve.Fori(1, PAIRS - 1) as i:
                    link = Chain(dve, own, OWN, i - 1)
                    for s, k, a in slots(i):
                        slot(i, s, k, a, link)
                    link.close()
                link = Chain(dve, own_last)
                for s, k, a in slots(0):
                    slot(PAIRS - 1, s, k, a, link, ahead=s < 2)
                slot(PAIRS, 0, 0, 0, link, scores=False)
                finish(PAIRS, 1, link)

            @block.scalar
            def _(act):
                def exps(i, s, which):
                    for n, j in enumerate(ORDER[which]):
                        act.wait_ge(nmaxed, 4 * (4 * i + s) + 2 * which + n + 1)
                        nc.scalar.activation(E[s % 2][j][:, :], E[s % 2][j][:, :], ACT.Exp, bias=nmx[s % 2][:, j:j + 1],
                                             accum_out=den[(s // 2) % 2][:, 2 * j + s % 2:2 * j + s % 2 + 1]).then_inc(exped, 1)

                def keys(i, k, n):
                    act.wait_ge(projected, 8 * (2 * i + k) + n + 1)
                    o, w = PIECES[n]
                    nc.scalar.activation(KT[k][:, o:o + w], PB[:, 0:w], ACT.Copy).then_inc(k_out, 1)

                def slot(i, s, k, a, scores=True, before=True, ahead=True):
                    if before:
                        exps(i, s - 1, 1)
                    for r in range(16):
                        if before and r >= FIRST:
                            for ch in [r - FIRST] + ([NC_ - 1] if r == 15 else []):
                                if ch in BY_ACT:
                                    h = 128 if ch < FULL else TAIL
                                    act.wait_ge(turned, NC_ * (4 * i + s - 1) + ch + 1)
                                    nc.scalar.activation(ET[ch % 4][0:h, :], TB[ch % 2][0:h, :], ACT.Copy).then_inc(et_act, 1)
                        if a == 1 and ahead and AHEAD.get(r, 4) < 4:
                            keys(i + k, 1 - k, AHEAD[r])
                        if scores and r == MID:
                            exps(i, s, 0)

                for n in range(4):
                    keys(0, 0, n)
                for s, k, a in slots(0):
                    slot(0, s, k, a, before=s > 0)
                with act.Fori(1, PAIRS - 1) as i:
                    for s, k, a in slots(i):
                        slot(i, s, k, a)
                for s, k, a in slots(0):
                    slot(PAIRS - 1, s, k, a, ahead=s < 2)
                slot(PAIRS, 0, 0, 0, scores=False)

        with nc.Block() as block:
            @block.tensor
            def _(pe):
                for t in range(T):
                    last = nc.tensor.matmul(Sb[t // 4][:, 128 * (t % 4):128 * (t % 4) + 128], OT[:, 128 * t:128 * t + 128], wo[:, :], start=True, stop=True)
                    if t % 4 == 3:
                        last.then_inc(out_mm, 1)

            @block.vector
            def _(dve):
                nc.vector.tensor_tensor(c.X[:, :, :], c.X[:, :, :], bo[:, :].unsqueeze(1).to_broadcast([128, T, D]), ALU.add).then_inc(added, 1)
                dve.wait_ge(added, 1)
                for q in range(4):
                    dve.wait_ge(out_mm, q + 1)
                    nc.vector.tensor_tensor(c.X[:, 4 * q:4 * q + 4, :], Sb[q][:, :].rearrange("p (t d) -> p t d", d=D), c.X[:, 4 * q:4 * q + 4, :], ALU.add).then_inc(added, 1)


def retention_stage(nc, c, p):
    NH, DQ, DV = 8, 16, 32
    HH, NG = 2, 4
    with ExitStack() as ctx:
        m = Memory(nc, ctx, "re")
        w = {n: m.sb(n, [128, 128]) for n in ("rWq", "rWqs", "rWk", "rWks")}
        wv, wg, wo, woraw = m.sb("wv", [128, 256]), m.sb("wg", [128, 256]), m.sb("wo", [128, 2, 128]), m.sb("wo_raw", [128, 2, 128])
        cosT, sinT, gcol, head = m.sb("cos", [128, S]), m.sb("sin", [128, S]), m.sb("gcol", [128, 1]), m.sb("head", [128, HH])
        decay = m.sb("decay", [128, 512])
        tmp = [m.sb(f"tmp{k}", [128, 512]) for k in range(2)]
        qr, kr, QB = c.XN[:, :, :].rearrange("p t d -> p (t d)"), m.sb("k_rot", [128, T * 128]), m.sb("q_blocks", [128, HH, T * 128])
        V, G, P = m.sb("v", [128, T, 256]), m.sb("gate", [128, T, 256]), m.sb("weights", [128, T, 512])
        O, ms = V, m.sb("ms", [128, 3, T * NH])
        big_half = m.sb("big_half", [128, T * NH])
        OT = P[:, :, :].rearrange("p t n -> p (t n)")[:, 0:2 * T * 128].rearrange("p (j n) -> p j n", j=2)
        bank = [m.ps(f"bank{q}") for q in range(8)]
        (loaded, qk_mm, roped, blocked, vg_mm, v_out, g_act, g_out, s_mm, p_out, o_mm, o_sq, o_ms, o_rs, o_done, t_mm, t_act, y_mm, added, own, half_set) = (
            m.sem(n) for n in ("loaded", "qk_projected", "roped", "q_blocked", "vg_projected", "v_out", "gate_tanh", "gate_out", "scored", "decayed",
                               "o_summed", "o_squared", "o_meansq", "o_rstd", "o_done", "turned", "turned_out", "y_projected", "added", "dve_own", "half_set"))
        loads = [(w[n], p[n]) for n in w] + [(wv, p["rWv"]), (wg, p["rWg"]), (cosT, p["cosT"]), (sinT, p["sinT"]), (gcol, p["gcol"]),
                                             (head, p["head"]), (decay, p["decay"])]

        with nc.Block() as block:
            @block.sync
            def _(sp):
                for dst, src in loads:
                    sp.dma_start(dst[:, :], src).then_inc(loaded, 16)
                sp.dma_start(woraw[:, :, :], p["rWo"].rearrange("(j i) d -> i j d", i=128)).then_inc(loaded, 16)
                sp.wait_ge(loaded, 16 * (len(loads) + 1))

            @block.tensor
            def _(pe):
                pe.wait_ge(loaded, 16 * (len(loads) + 1))
                for q in range(4):
                    if q >= 2:
                        pe.wait_ge(roped, 2 * (q - 1))
                    for k, n in enumerate(w):
                        nc.tensor.matmul(bank[4 * (q % 2) + k][:, :], w[n][:, :], c.XNT[:, 512 * q:512 * q + 512], start=True, stop=True).then_inc(qk_mm, 1)

            @block.vector
            def _(dve):
                link = Chain(dve, own)
                cs, sn = (v[:, :].unsqueeze(1).to_broadcast([128, 8, S]) for v in (cosT, sinT))
                for q in range(4):
                    for k, dst in enumerate((qr, kr)):
                        straight, swapped = (bank[4 * (q % 2) + 2 * k + x][:, :].rearrange("p (b s) -> p b s", s=S) for x in range(2))
                        dve.wait_ge(qk_mm, 4 * q + 2 * k + 2)
                        nc.vector.tensor_tensor(tmp[0][:, :].rearrange("p (b s) -> p b s", s=S), straight, cs, ALU.mult)
                        link(nc.vector.tensor_tensor(tmp[1][:, :].rearrange("p (b s) -> p b s", s=S), swapped, sn, ALU.mult))
                        nc.vector.tensor_tensor(dst[:, 512 * q:512 * q + 512], tmp[0][:, :], tmp[1][:, :], ALU.add).then_inc(roped, 1)
                        dve.wait_ge(roped, 2 * q + k + 1)
                for j in range(2):
                    nc.vector.tensor_scalar(wo[:, j, :], woraw[:, j, :], gcol[:, 0:1], 0.5, ALU.mult, ALU.mult)
                nc.vector.memset(big_half[:, :], -0.5).then_inc(half_set, 1)

            @block.scalar
            def _(act):
                for q in range(4):
                    act.wait_ge(roped, 2 * q + 1)
                    for hh in range(HH):
                        nc.scalar.activation(QB[:, hh, 512 * q:512 * q + 512], qr[:, 512 * q:512 * q + 512], ACT.Copy, scale=head[:, hh:hh + 1]).then_inc(blocked, 1)

        with nc.Block() as block:
            @block.tensor
            def _(pe):
                for n in range(T // 2):
                    for k, wt in enumerate((wv, wg)):
                        if n >= 4:
                            pe.wait_ge((v_out, g_out)[k], n - 3)
                        for t in (2 * n, 2 * n + 1):
                            last = nc.tensor.matmul(bank[4 * k + n % 4][:, 256 * (t % 2):256 * (t % 2) + 256], c.XNT[:, 128 * t:128 * t + 128], wt[:, :], start=True, stop=True)
                        last.then_inc(vg_mm, 1)

            @block.scalar
            def _(act):
                for n in range(T // 2):
                    act.wait_ge(vg_mm, 2 * n + 1)
                    nc.scalar.activation(V[:, 2 * n:2 * n + 2, :], bank[n % 4][:, :].rearrange("p (t d) -> p t d", t=2), ACT.Copy).then_inc(v_out, 1)
                    act.wait_ge(vg_mm, 2 * n + 2)
                    nc.scalar.activation(G[:, 2 * n:2 * n + 2, :], bank[4 + n % 4][:, :].rearrange("p (t d) -> p t d", t=2), ACT.Tanh, scale=0.5).then_inc(g_act, 1)

            @block.vector
            def _(dve):
                for n in range(T // 2):
                    dve.wait_ge(g_act, n + 1)
                    g2 = G[:, 2 * n:2 * n + 2, :].rearrange("p t d -> p (t d)")
                    nc.vector.scalar_tensor_tensor(out=g2, in0=g2, scalar=1.0, in1=bank[4 + n % 4][:, :], op0=ALU.add, op1=ALU.mult).then_inc(g_out, 1)

        with nc.Block() as block:
            @block.tensor
            def _(pe):
                for r in range(4):
                    for g in range(NG):
                        if r >= 2:
                            pe.wait_ge(p_out, NG * (r - 2) + g + 1)
                        for t in range(4 * r, 4 * r + 4):
                            for b in (2 * t, 2 * t + 1):
                                h = 64 * (b % 2)
                                last = nc.tensor.matmul(bank[4 * (r % 2) + g][h:h + 64, 128 * (t % 4):128 * (t % 4) + 128],
                                                        kr[32 * g:32 * g + 32, 64 * b:64 * b + 64],
                                                        QB[32 * g:32 * g + 32, :, 64 * b:64 * b + 64], start=True, stop=True)
                        last.then_inc(s_mm, 1)

            @block.vector
            def _(dve):
                for r in range(4):
                    for g in range(NG):
                        dve.wait_ge(s_mm, NG * r + g + 1)
                        dec = decay[:, 128 * g:128 * g + 128].unsqueeze(1).to_broadcast([128, 4, 128])
                        nc.vector.tensor_tensor(P[:, 4 * r:4 * r + 4, 128 * g:128 * g + 128], bank[4 * (r % 2) + g][:, :].rearrange("p (t n) -> p t n", t=4),
                                                dec, ALU.mult).then_inc(p_out, 1)

        with nc.Block() as block:
            @block.tensor
            def _(pe):
                for n in range(T // 2):
                    for t in (2 * n, 2 * n + 1):
                        for hd in range(NH):
                            for b in (2 * t, 2 * t + 1):
                                h = 64 * (b % 2)
                                o = 256 * (t % 2) + DV * hd
                                last = nc.tensor.matmul(bank[n][h:h + 64, o:o + DV], P[h:h + 64, t, 64 * hd:64 * hd + 64], V[h:h + 64, t, DV * hd:DV * hd + DV],
                                                        start=True, stop=True)
                    last.then_inc(o_mm, 1)

            @block.scalar
            def _(act):
                sq = QB[:, :, :].rearrange("p h n -> p (h n)")
                for n in range(T // 2):
                    act.wait_ge(o_mm, n + 1)
                    nc.scalar.activation(sq[:, 512 * n:512 * n + 512], bank[n][:, :], ACT.Square).then_inc(o_sq, 1)

            @block.gpsimd
            def _(pool):
                for n in range(4):
                    pool.wait_ge(o_ms, n + 1)
                    part = slice(4 * NH * n, 4 * NH * n + 4 * NH)
                    nc.gpsimd.tensor_tensor(ms[:, 2, part], ms[:, 1, part], big_half[:, part], ALU.pow).then_inc(o_rs, 1)

            @block.vector
            def _(dve):
                link = Chain(dve, own)
                link.n = 8
                sq = QB[:, :, :].rearrange("p h n -> p (h n)")
                for n in range(4):
                    part = slice(4 * NH * n, 4 * NH * n + 4 * NH)
                    dve.wait_ge(o_sq, 2 * n + 2)
                    link(nc.vector.tensor_reduce(out=ms[:, 0, part], in_=sq[:, 1024 * n:1024 * n + 1024].rearrange("p (h d) -> p h d", d=DV), op=ALU.add, axis=AX.X))
                    nc.vector.tensor_scalar(ms[:, 1, part], ms[:, 0, part], 1.0 / DV, 1e-5, ALU.mult, ALU.add).then_inc(o_ms, 1)
                dve.wait_ge(o_mm, T // 2)
                for n in range(T // 2):
                    dve.wait_ge(o_rs, n // 2 + 1)
                    o2 = O[:, 2 * n:2 * n + 2, :].rearrange("p t d -> p (t d)")
                    rs = ms[:, 2, 2 * NH * n:2 * NH * n + 2 * NH]
                    link(nc.vector.tensor_tensor(o2.rearrange("p (h d) -> p h d", d=DV), bank[n][:, :].rearrange("p (h d) -> p h d", d=DV), bc(rs, DV), ALU.mult))
                    nc.vector.tensor_tensor(o2, o2, G[:, 2 * n:2 * n + 2, :].rearrange("p t d -> p (t d)"), ALU.mult).then_inc(o_done, 1)

        with nc.Block() as block:
            @block.tensor
            def _(pe):
                for n in range(T // 2):
                    j, q = n % 2, n // 2
                    if n >= 4:
                        pe.wait_ge(t_act, n - 3)
                    for t in range(4 * q, 4 * q + 4):
                        last = nc.tensor.transpose(bank[n % 4][:, 128 * (t % 4):128 * (t % 4) + 128], O[:, t, 128 * j:128 * j + 128], c.ident[:, :])
                    last.then_inc(t_mm, 1)
                for q in range(4):
                    pe.wait_ge(t_act, 2 * q + 2)
                    for t in range(4 * q, 4 * q + 4):
                        for j in range(2):
                            last = nc.tensor.matmul(bank[4 + q][:, 128 * (t % 4):128 * (t % 4) + 128], OT[:, j, 128 * t:128 * t + 128], wo[:, j, :], start=(j == 0), stop=(j == 1))
                    last.then_inc(y_mm, 1)

            @block.scalar
            def _(act):
                for n in range(T // 2):
                    j, q = n % 2, n // 2
                    act.wait_ge(t_mm, n + 1)
                    nc.scalar.activation(OT[:, j, 512 * q:512 * q + 512], bank[n % 4][:, :], ACT.Copy).then_inc(t_act, 1)

            @block.vector
            def _(dve):
                for q in range(4):
                    dve.wait_ge(y_mm, q + 1)
                    xs = c.X[:, 4 * q:4 * q + 4, :]
                    nc.vector.tensor_tensor(xs, bank[4 + q][:, :].rearrange("p (t d) -> p t d", d=D), xs, ALU.add).then_inc(added, 1)


def top2_moe_stage(nc, c, p):
    X8, H = 8, 256
    J, Q = H // 128, 4
    N = X8 + 1
    with ExitStack() as ctx:
        m = Memory(nc, ctx, "tm")
        w1, w2, w3 = m.sb("w1", [128, N, H]), m.sb("w2", [128, N, H]), m.sb("w3", [128, N, J, D])
        gw = m.sb("gate", [128, X8])
        lg, a1, a2, o1, o2 = (m.sb(n, [128, T, X8]) for n in ("logits", "work1", "work2", "first", "second"))
        col, wt = m.sb("col", [128, 8, T]), m.sb("weights", [128, T, N])
        rev = m.sb("rev", [128, X8])
        SIL = [m.sb(f"silu{k}", [128, 512]) for k in range(3)]
        G = [m.sb(f"hidden{k}", [128, J, 512]) for k in range(3)]
        bank = [m.ps(f"bank{q}") for q in range(8)]
        g_loaded, w_loaded, rev_set, logit, expd, shifted, weighed, up, silu, gated, down, added, own = (m.sem(n) for n in (
            "g_loaded", "w_loaded", "rev_set", "logits", "exp", "shifted", "weighed", "up", "silu", "gated", "down", "added", "dve_own"))
        with nc.Block() as block:
            @block.sync
            def _(sp):
                sp.dma_start(gw[:, :], p["gate1"]).then_inc(g_loaded, 16)
                for e in range(N):
                    src = [p[n][e] for n in ("ew1", "ew2", "ew3")] if e < X8 else [p[n] for n in ("sw1", "sw2", "sw3")]
                    sp.dma_start(w1[:, e, :], src[0]).then_inc(w_loaded, 16)
                    sp.dma_start(w2[:, e, :], src[1]).then_inc(w_loaded, 16)
                    sp.dma_start(w3[:, e, :, :], src[2].rearrange("(j i) d -> i j d", i=128)).then_inc(w_loaded, 16)
                sp.wait_ge(w_loaded, 48 * N)

            @block.gpsimd
            def _(pool):
                nc.gpsimd.iota(rev[:, :], pattern=[[-1, X8]], base=X8, channel_multiplier=0, allow_small_or_imprecise_dtypes=True).then_inc(rev_set, 1)

            @block.tensor
            def _(pe):
                pe.wait_ge(g_loaded, 16)
                for t in range(T):
                    last = nc.tensor.matmul(bank[6][:, X8 * t:X8 * t + X8], c.XNT[:, 128 * t:128 * t + 128], gw[:, :], start=True, stop=True)
                last.then_inc(logit, 1)

                def rise(e, q):
                    for j in range(J):
                        n = (e * Q + q) * J + j
                        if n >= 3:
                            pe.wait_ge(gated, n - 2)
                        for k, w in enumerate((w1, w2)):
                            last = nc.tensor.matmul(bank[2 * (n % 3) + k][:, :], w[:, e, 128 * j:128 * j + 128], c.XNT[:, 512 * q:512 * q + 512], start=True, stop=True)
                        last.then_inc(up, 1)

                def fall(e, q):
                    n = e * Q + q
                    pe.wait_ge(gated, J * n + J)
                    if n >= 2:
                        pe.wait_ge(added, n - 1)
                    if n == 0:
                        pe.wait_ge(weighed, 1)
                    for t in range(4):
                        for j in range(J):
                            last = nc.tensor.matmul(bank[6 + n % 2][:, 128 * t:128 * t + 128], G[n % 3][:, j, 128 * t:128 * t + 128], w3[:, e, j, :],
                                                    start=(j == 0), stop=(j == J - 1))
                    last.then_inc(down, 1)

                pe.wait_ge(w_loaded, 48 * N)
                before = None
                for e in range(N):
                    for q in range(Q):
                        rise(e, q)
                        if before:
                            fall(*before)
                        before = (e, q)
                fall(*before)

            @block.scalar
            def _(act):
                act.wait_ge(shifted, 1)
                nc.scalar.activation(col[:, 3, :], col[:, 2, :], ACT.Exp).then_inc(expd, 1)
                for n in range(N * Q * J):
                    act.wait_ge(up, n + 1)
                    if n >= 3:
                        act.wait_ge(gated, n - 2)
                    nc.scalar.activation(SIL[n % 3][:, :], bank[2 * (n % 3)][:, :], ACT.Silu).then_inc(silu, 1)

            @block.vector
            def _(dve):
                link = Chain(dve, own)
                rev_all = rev[:, :].unsqueeze(1).to_broadcast([128, T, X8])
                dve.wait_ge(logit, 1)
                link(nc.vector.tensor_copy(lg[:, :, :], bank[6][:, 0:T * X8].rearrange("p (t e) -> p t e", e=X8)))
                dve.wait_ge(rev_set, 1)

                def best(src, top, onehot):
                    link(nc.vector.tensor_reduce(out=col[:, top, :], in_=src, op=ALU.max, axis=AX.X))
                    link(nc.vector.tensor_tensor(a1[:, :, :], src, bc(col[:, top, :], X8), ALU.is_equal))
                    link(nc.vector.tensor_tensor(a1[:, :, :], a1[:, :, :], rev_all, ALU.mult))
                    link(nc.vector.tensor_reduce(out=col[:, 7, :], in_=a1[:, :, :], op=ALU.max, axis=AX.X))
                    link(nc.vector.tensor_tensor(onehot, a1[:, :, :], bc(col[:, 7, :], X8), ALU.is_equal))

                best(lg[:, :, :], 0, o1[:, :, :])
                link(nc.vector.tensor_scalar(a2[:, :, :], o1[:, :, :], -1e38, None, ALU.mult))
                link(nc.vector.tensor_tensor(a2[:, :, :], a2[:, :, :], lg[:, :, :], ALU.add))
                best(a2[:, :, :], 1, o2[:, :, :])
                nc.vector.tensor_tensor(col[:, 2, :], col[:, 1, :], col[:, 0, :], ALU.subtract).then_inc(shifted, 1)
                dve.wait_ge(expd, 1)
                link(nc.vector.tensor_scalar(col[:, 4, :], col[:, 3, :], 1.0, None, ALU.add))
                link(nc.vector.reciprocal(col[:, 5, :], col[:, 4, :]))
                link(nc.vector.tensor_tensor(col[:, 6, :], col[:, 5, :], col[:, 3, :], ALU.mult))
                nc.vector.tensor_tensor(o1[:, :, :], o1[:, :, :], bc(col[:, 5, :], X8), ALU.mult)
                link(nc.vector.tensor_tensor(o2[:, :, :], o2[:, :, :], bc(col[:, 6, :], X8), ALU.mult))
                nc.vector.tensor_tensor(wt[:, :, 0:X8], o1[:, :, :], o2[:, :, :], ALU.add)
                nc.vector.memset(wt[:, :, X8:N], 1.0).then_inc(weighed, 1)
                dve.wait_ge(weighed, 1)

                def gate(e, q):
                    for j in range(J):
                        n = (e * Q + q) * J + j
                        dve.wait_ge(silu, n + 1)
                        nc.vector.tensor_tensor(G[(n // J) % 3][:, j, :], bank[2 * (n % 3) + 1][:, :], SIL[n % 3][:, :], ALU.mult).then_inc(gated, 1)

                def collect(e, q):
                    n = e * Q + q
                    dve.wait_ge(down, n + 1)
                    for t in range(4):
                        last = nc.vector.scalar_tensor_tensor(out=c.X[:, 4 * q + t, :], in0=bank[6 + n % 2][:, 128 * t:128 * t + 128],
                                                              scalar=wt[:, 4 * q + t, e:e + 1], in1=c.X[:, 4 * q + t, :], op0=ALU.mult, op1=ALU.add)
                    last.then_inc(added, 1)
                    if n >= 1:
                        dve.wait_ge(added, n)

                before = []
                for e in range(N):
                    for q in range(Q):
                        gate(e, q)
                        before.append((e, q))
                        if len(before) > 2:
                            collect(*before.pop(0))
                for b in before:
                    collect(*b)


def store_stage(nc, c, out):
    with ExitStack() as ctx:
        m = Memory(nc, ctx, "st")
        stored = m.sem("stored")
        with nc.Block() as block:
            @block.sync
            def _(sp):
                sp.dma_start(out.rearrange("b s d -> (b s) d").rearrange("(t p) d -> p t d", p=128), c.X[:, :, :]).then_inc(stored, 16)
                sp.wait_ge(stored, 16)


def perceiver(nc, p, out):
    with ExitStack() as ctx:
        m = Memory(nc, ctx, "c")
        c = Common()
        c.X, c.XN, c.XNT = m.sb("X", [128, T, D]), m.sb("XN", [128, T, D]), m.sb("XNT", [128, T * 128])
        c.ident, c.ones, c.half = m.sb("ident", [128, 128]), m.sb("ones", [128, 128]), m.sb("minus_half", [128, 16])
        c.mq, c.wcT, c.whhT, c.bias = m.sb("mq", [128, 128]), m.sb("wcT", [128, 384]), m.sb("whhT", [128, 384]), m.sb("bias", [128, 5])
        setup_stage(nc, c, p)
        norm_block(nc, c, "n0")
        slot_attention_stage(nc, c, p["ctx"])
        norm_block(nc, c, "n1")
        linear_attention_stage(nc, c, p)
        norm_block(nc, c, "n2")
        capacity_moe_stage(nc, c, p)
        norm_block(nc, c, "n3")
        masked_attention_stage(nc, c, p)
        norm_block(nc, c, "n4")
        retention_stage(nc, c, p)
        norm_block(nc, c, "n5")
        top2_moe_stage(nc, c, p)
        store_stage(nc, c, out)


def rotary_tables(np):
    NH, DQ = 8, 16
    inv = 1.0 / 10000.0 ** (np.arange(0, DQ, 2, dtype=np.float32) / DQ)
    ang = (np.arange(S, dtype=np.float32)[None, :] * inv.astype(np.float32)[:, None]).astype(np.float32)
    row = np.arange(128)
    sign = np.where(row % 2 == 0, -1.0, 1.0)[:, None]
    pair = row % DQ // 2
    s = np.log2(1.0 - np.exp2(-5.0 - np.arange(NH)))
    diff = np.arange(S)[None, :] - np.arange(S)[:, None]
    dec = np.where(diff[:, None, :] >= 0, np.exp2(diff[:, None, :] * s[None, :, None]), 0.0).reshape(S, NH * S)
    head = (row[:, None] // DQ % 2 == np.arange(2)[None, :]) * float(DQ) ** -0.5
    f = np.float32
    return {"cosT": np.cos(ang)[pair].astype(f), "sinT": (np.sin(ang)[pair] * sign).astype(f),
            "decay": np.concatenate([dec, dec]).astype(f), "head": head.astype(f)}


def kernel(**inputs):
    import numpy as np
    import concourse.bacc as bacc
    from concourse.bass_utils import run_bass_kernel_spmd

    a = {k: np.asarray(v) for k, v in inputs.items()}
    swap = np.arange(128) ^ 1
    laid = {
        "x": a["x"], "ctx": a["ctx_1024"],
        "L0_xattn_Wq": a["L0_xattn_Wq"], "L0_xattn_Wk": a["L0_xattn_Wk"], "L0_xattn_Wv": a["L0_xattn_Wv"],
        "wihT": a["L0_xattn_gru_wih"].T, "whhT": a["L0_xattn_gru_whh"].T,
        "bih3": a["L0_xattn_gru_bih"].reshape(3, 128).T, "bhh3": a["L0_xattn_gru_bhh"].reshape(3, 128).T,
        "ws_col": a["L0_xattn_slot_norm_w"].reshape(128, 1), "wp_col": a["L0_xattn_input_norm_w"].reshape(128, 1),
        "wp_row": a["L0_xattn_input_norm_w"],
        "L0_attn_q_proj": a["L0_attn_q_proj"], "L0_attn_k_proj": a["L0_attn_k_proj"],
        "gateT0": a["L0_ffn_gate_weight"].T, "ln_cols": np.stack([a["L0_ffn_ln_gamma"], a["L0_ffn_ln_beta"]], 1),
        "wi": a["L0_ffn_wi"], "wo": a["L0_ffn_wo"],
        "ctxT": a["ctx_1024"].transpose(0, 2, 1), "mask": a["mask_Bx1xSxS2_if1"].reshape(B, S, M),
        "WqT1": a["L1_xattn_Wq"].T, "WkT1": a["L1_xattn_Wk"].T, "WvT1": a["L1_xattn_Wv"].T, "WoT1": a["L1_xattn_Wo"].T,
        "bo": a["L1_xattn_bo"],
        "rWq": a["L1_attn_Wq"], "rWqs": a["L1_attn_Wq"][:, swap], "rWk": a["L1_attn_Wk"], "rWks": a["L1_attn_Wk"][:, swap],
        "rWv": a["L1_attn_Wv"], "rWg": a["L1_attn_Wg"], "rWo": a["L1_attn_Wo"],
        "gcol": np.tile(a["L1_attn_g_norm_w"], 4).reshape(128, 1), **rotary_tables(np),
        "gate1": a["L1_ffn_gate_w"], "ew1": a["L1_ffn_ew1"], "ew2": a["L1_ffn_ew2"], "ew3": a["L1_ffn_ew3"],
        "sw1": a["L1_ffn_sw1"], "sw2": a["L1_ffn_sw2"], "sw3": a["L1_ffn_sw3"],

    }
    nc = bacc.Bacc("TRN2", target_bir_lowering=False, num_devices=1)
    arrays, p = {}, {}
    for name, v in laid.items():
        v = np.ascontiguousarray(v)
        arrays["in_" + name] = v
        p[name] = nc.dram_tensor("in_" + name, v.shape, mybir.dt.from_np(v.dtype), kind="ExternalInput").ap()
    out = nc.dram_tensor("out", (B, S, D), fp32, kind="ExternalOutput").ap()
    perceiver(nc, p, out)
    r = run_bass_kernel_spmd(nc, [arrays], core_ids=[0])
    return r.results[0]["out"]
```

```python
import concourse.bass as bass
from concourse import mybir
from contextlib import ExitStack

fp32 = mybir.dt.float32
bf16 = mybir.dt.bfloat16
i32 = mybir.dt.int32
ALU = mybir.AluOpType
ACT = mybir.ActivationFunctionType
AX = mybir.AxisListType

B, S, D, M = 32, 64, 128, 1601
T = B * S // 128
NC_ = -(-M // 128)
FULL = M // 128
TAIL = M - 128 * FULL
GROUPS = [(c, min(4, FULL - c)) for c in range(0, FULL, 4)]


class Chain:

    def __init__(self, eng, sem, per_turn=0, turn=None):
        self.eng, self.sem, self.n, self.per_turn, self.turn = eng, sem, 0, per_turn, turn

    def __call__(self, instruction):
        self.n += 1
        instruction.then_inc(self.sem, 1)
        at = self.n if self.turn is None else self.turn * self.per_turn + self.n
        self.eng.wait_ge(self.sem, at)

    def close(self):
        assert self.turn is None or self.n == self.per_turn, (self.n, self.per_turn)


def bc(ap, n):
    return ap.unsqueeze(2).to_broadcast([ap.shape[0], ap.shape[1], n])


class Memory:

    def __init__(self, nc, ctx, tag):
        self.nc, self.ctx, self.tag, self.sems = nc, ctx, tag, []
        ctx.callback(self.clear)

    def sb(self, name, shape, dt=fp32):
        return self.ctx.enter_context(self.nc.sbuf_tensor(f"{self.tag}_{name}", shape, dt))

    def ps(self, name, shape=(128, 512), dt=fp32):
        return self.ctx.enter_context(self.nc.psum_tensor(f"{self.tag}_{name}", list(shape), dt))

    def sem(self, name):
        self.sems.append(self.nc.alloc_semaphore(f"{self.tag}_{name}"))
        return self.sems[-1]

    def clear(self):
        self.nc.clear_and_free_semaphores(self.sems)
        self.nc.all_engine_barrier()


class NormSems:
    def __init__(self, m):
        self.centred, self.squared, self.variance = m.sem("ln_centred"), m.sem("ln_squared"), m.sem("ln_variance")
        self.rstd, self.normed, self.transposed = m.sem("ln_rstd"), m.sem("ln_normed"), m.sem("ln_transposed")
        self.xnt_dve, self.xnt_act = m.sem("ln_xnt_dve"), m.sem("ln_xnt_act")


def norm_dve(nc, dve, link, X, XN, work, st, s, eps):
    link(nc.vector.tensor_reduce(out=st[:, 0, :], in_=X[:, :, :], op=ALU.add, axis=AX.X))
    link(nc.vector.tensor_scalar(st[:, 1, :], st[:, 0, :], -1.0 / D, None, ALU.mult))
    nc.vector.tensor_tensor(XN[:, :, :], X[:, :, :], bc(st[:, 1, :], D), ALU.add).then_inc(s.centred, 1)
    dve.wait_ge(s.squared, 1)
    link(nc.vector.tensor_reduce(out=st[:, 2, :], in_=work[:, :, :], op=ALU.add, axis=AX.X))
    nc.vector.tensor_scalar(st[:, 3, :], st[:, 2, :], 1.0 / D, eps, ALU.mult, ALU.add).then_inc(s.variance, 1)
    dve.wait_ge(s.rstd, 1)
    nc.vector.tensor_tensor(XN[:, :, :], XN[:, :, :], bc(st[:, 4, :], D), ALU.mult).then_inc(s.normed, 1)


def norm_act(nc, act, XN, work, s):
    act.wait_ge(s.centred, 1)
    nc.scalar.activation(work[:, :, :], XN[:, :, :], ACT.Square).then_inc(s.squared, 1)


def norm_pool(nc, pool, st, half, s):
    pool.wait_ge(s.variance, 1)
    nc.gpsimd.tensor_tensor(st[:, 4, :], st[:, 3, :], half[:, 0:T], ALU.pow).then_inc(s.rstd, 1)


def transpose_pe(nc, pe, XN, banks, ident, s):
    pe.wait_ge(s.normed, 1)
    for q in range(T // 4):
        for j in range(4):
            last = nc.tensor.transpose(banks[q][:, 128 * j:128 * j + 128], XN[:, 4 * q + j, :], ident[:, :])
        last.then_inc(s.transposed, 1)


def transpose_out_dve(nc, dve, XNT, banks, s):
    for q in range(0, T // 4, 2):
        dve.wait_ge(s.transposed, q + 1)
        nc.vector.tensor_copy(XNT[:, 512 * q:512 * q + 512], banks[q][:, :]).then_inc(s.xnt_dve, 1)


def transpose_out_act(nc, act, XNT, banks, s):
    for q in range(1, T // 4, 2):
        act.wait_ge(s.transposed, q + 1)
        nc.scalar.activation(XNT[:, 512 * q:512 * q + 512], banks[q][:, :], ACT.Copy).then_inc(s.xnt_act, 1)


def norm_block(nc, c, tag, eps=1e-5, x_out=False):
    with ExitStack() as ctx:
        m = Memory(nc, ctx, tag)
        work, st = m.sb("work", [128, T, D]), m.sb("stats", [128, 5, T])
        banks = [m.ps(f"bank{q}") for q in range(T // 4)]
        s, own = NormSems(m), m.sem("dve_own")
        with nc.Block() as block:
            @block.vector
            def _(dve):
                norm_dve(nc, dve, Chain(dve, own), c.X, c.XN, work, st, s, eps)
                transpose_out_dve(nc, dve, c.XNT, banks, s)

            @block.scalar
            def _(act):
                norm_act(nc, act, c.XN, work, s)
                transpose_out_act(nc, act, c.XNT, banks, s)

            @block.gpsimd
            def _(pool):
                norm_pool(nc, pool, st, c.half, s)

            @block.tensor
            def _(pe):
                transpose_pe(nc, pe, c.XN, banks, c.ident, s)


class Common:
    pass


def setup_stage(nc, c, p):
    with ExitStack() as ctx:
        m = Memory(nc, ctx, "su")
        wq, wk, wv = m.sb("wq", [128, 128]), m.sb("wk", [128, 128]), m.sb("wv", [128, 128])
        wpb, wkw = m.sb("wp_bc", [128, 128]), m.sb("wk_scaled", [128, 128])
        wih = m.sb("wihT", [128, 384])
        bih, bhh, ws, wp = m.sb("bih", [128, 3]), m.sb("bhh", [128, 3]), m.sb("ws", [128, 1]), m.sb("wp", [128, 1])
        mq_ps, wc_ps = m.ps("mq"), m.ps("wc")
        loaded, x_loaded, zeroed, wk_scaled, folded = (m.sem(n) for n in ("loaded", "x_loaded", "zeroed", "wk_scaled", "folded"))
        own = m.sem("dve_own")
        loads = [(wq, p["L0_xattn_Wq"]), (wk, p["L0_xattn_Wk"]), (wv, p["L0_xattn_Wv"]), (wih, p["wihT"]),
                 (c.whhT, p["whhT"]), (bih, p["bih3"]), (bhh, p["bhh3"]), (ws, p["ws_col"]), (wp, p["wp_col"])]
        with nc.Block() as block:
            @block.sync
            def _(sp):
                sp.dma_start(c.X[:, :, :], p["x"].rearrange("b s d -> (b s) d").rearrange("(t p) d -> p t d", p=128)).then_inc(x_loaded, 16)
                for dst, src in loads:
                    sp.dma_start(dst[:, :], src).then_inc(loaded, 16)
                sp.dma_start(wpb[:, :], p["wp_row"].partition_broadcast(128)).then_inc(loaded, 16)
                sp.wait_ge(x_loaded, 16)
                sp.wait_ge(loaded, 16 * (len(loads) + 1))

            @block.gpsimd
            def _(pool):
                nc.gpsimd.memset(c.ones[:, :], 1.0)
                nc.gpsimd.memset(c.half[:, :], -0.5)
                nc.gpsimd.memset(c.ident[:, :], 0.0).then_inc(zeroed, 1)
                pool.wait_ge(zeroed, 1)
                nc.gpsimd.affine_select(out=c.ident[:, :], in_=c.ident[:, :], compare_op=ALU.not_equal, fill=1.0,
                                        base=0, pattern=[[-1, 128]], channel_multiplier=1).then_inc(zeroed, 1)
                pool.wait_ge(zeroed, 2)

            @block.vector
            def _(dve):
                link = Chain(dve, own)
                dve.wait_ge(loaded, 16 * (len(loads) + 1))
                nc.vector.tensor_tensor(wkw[:, :], wk[:, :], wpb[:, :], ALU.mult).then_inc(wk_scaled, 1)
                link(nc.vector.tensor_tensor(c.bias[:, 0:3], bih[:, :], bhh[:, :], ALU.add))
                link(nc.vector.tensor_scalar(c.bias[:, 0:2], c.bias[:, 0:2], 0.5, None, ALU.mult))
                nc.vector.tensor_copy(c.bias[:, 3:4], bih[:, 2:3])
                nc.vector.tensor_copy(c.bias[:, 4:5], bhh[:, 2:3])
                dve.wait_ge(folded, 2)
                nc.vector.tensor_scalar(c.mq[:, :], mq_ps[:, 0:128], ws[:, 0:1], float(D) ** -0.5, ALU.mult, ALU.mult)
                link(nc.vector.tensor_scalar(c.wcT[:, :], wc_ps[:, 0:384], wp[:, 0:1], None, ALU.mult))

            @block.tensor
            def _(pe):
                pe.wait_ge(wk_scaled, 1)
                nc.tensor.matmul(mq_ps[:, 0:128], wq[:, :], wkw[:, :], start=True, stop=True).then_inc(folded, 1)
                nc.tensor.matmul(wc_ps[:, 0:384], wv[:, :], wih[:, :], start=True, stop=True).then_inc(folded, 1)


def slot_attention_stage(nc, c, ctx_dram):
    R, LANES, NB = 3, range(2), 4
    TURNS = B // (2 * NB)
    EPS = 1e-6
    HALVES = 2 * R
    with ExitStack() as ctx:
        m = Memory(nc, ctx, "sa")
        pn = [[m.sb(f"pn{l}{b}", [128, NC_, D + 1]) for b in range(NB)] for l in LANES]
        pnT = [[m.sb(f"pnT{l}{b}", [128, NC_ * 128]) for b in range(NB)] for l in LANES]
        e = [[m.sb(f"e{l}{b}", [128, NC_, S]) for b in range(NB)] for l in LANES]
        ms = [[m.sb(f"ms{l}{b}", [128, 3, NC_]) for b in range(NB)] for l in LANES]
        col = [[m.sb(f"col{l}{b}", [128, 3, NC_]) for b in range(NB)] for l in LANES]
        slT, qn, qT, un, uT, nn = ([m.sb(f"{n}{l}", [128, 256]) for l in LANES] for n in ("slotsT", "qn", "qT", "un", "uT", "nn"))
        slsq, tr, hn = un, [m.sb(f"tr{l}", [128, 2, 256]) for l in LANES], [m.sb(f"hn{l}", [128, 2, 256]) for l in LANES]
        sc = [m.sb(f"sc{l}", [128, 4, 2]) for l in LANES]
        Sb = [m.ps(f"scores{b}", [128, 1024]) for b in range(2)]
        U = [m.ps(f"u{l}") for l in LANES]
        G = [m.ps(f"g{l}") for l in LANES]

        per_lane = lambda name: [m.sem(f"{name}{l}") for l in LANES]
        loaded, squared, meansq, rstd, normed, turned_act, turned_dve = map(per_lane, (
            "ctx_loaded", "ctx_squared", "ctx_meansq", "ctx_rstd", "ctx_normed", "ctxT_act", "ctxT_dve"))
        turned = per_lane("ctxT_psum")
        slots_in, sl_sq, q_nat, sl_meansq, sl_rstd, q_scaled, q_turned, q_ready = map(per_lane, (
            "slots_in", "slots_squared", "q_natural", "slots_meansq", "slots_rstd", "q_scaled", "q_turned", "q_ready"))
        scored, centred, exped, slot_sum, attn = (m.sem(n) for n in ("scored", "centred", "exped", "slot_sum_inv", "attn_ready"))
        summed, u_inv, u_scaled, u_turned, u_ready = map(per_lane, ("u_summed", "u_inv", "u_scaled", "u_turned", "u_ready"))
        gates, rz, n_in, n_out, slots, out_turned, added = map(per_lane, (
            "gates", "rz", "n_in", "n_out", "slots_new", "out_turned", "x_added"))
        zeroed, own_first, own, own_last = m.sem("zeroed"), m.sem("dve_own_first"), m.sem("dve_own"), m.sem("dve_own_last")

        def half(i, l, t):
            return NB * (HALVES * i + 2 * t + l)

        with nc.Block() as block:
            @block.sync
            def _(sp):
                def load(i, l):
                    for b in range(NB):
                        rows = ctx_dram[bass.ds(2 * NB * i + NB * l + b, 1), :, :].rearrange("a m d -> (a m) d")
                        sp.dma_start(pn[l][b][:, 0:FULL, 0:D], rows[0:128 * FULL, :].rearrange("(p c) d -> p c d", p=128)).then_inc(loaded[l], 16)
                        sp.dma_start(pn[l][b][0:TAIL, FULL, 0:D], rows[128 * FULL:M, :]).then_inc(loaded[l], 16)

                sp.wait_ge(zeroed, 1)
                for l in LANES:
                    load(0, l)
                with sp.Fori(0, TURNS - 1) as i:
                    for l in LANES:
                        sp.wait_ge(summed[l], R * i + R)
                        load(i + 1, l)

            @block.gpsimd
            def _(pool):
                def prepare(i, l):
                    for b in range(NB):
                        pool.wait_ge(meansq[l], NB * i + b + 1)
                        nc.gpsimd.tensor_tensor(ms[l][b][:, 2, :], ms[l][b][:, 1, :], c.half[:, 0:NC_], ALU.pow).then_inc(rstd[l], 1)
                        pool.wait_ge(rstd[l], NB * i + b + 1)
                        nc.gpsimd.tensor_tensor(pn[l][b][:, :, 0:D], pn[l][b][:, :, 0:D], bc(ms[l][b][:, 2, :], D), ALU.mult).then_inc(normed[l], 1)

                def scores(i, l, t):
                    pool.wait_ge(sl_meansq[l], R * i + t + 1)
                    nc.gpsimd.tensor_tensor(sc[l][:, 1, :], sc[l][:, 0, :], c.half[:, 0:2], ALU.pow).then_inc(sl_rstd[l], 1)
                    for b in range(NB):
                        pool.wait_ge(slot_sum, half(i, l, t) + b + 1)
                        nc.gpsimd.tensor_tensor(e[l][b][:, :, :], e[l][b][:, :, :], bc(col[l][b][:, 2, :], S), ALU.mult).then_inc(attn, 1)

                def turn(i, last):
                    scores(i, 0, 0)
                    prepare(i, 1)
                    for t in range(R):
                        if t:
                            scores(i, 0, t)
                        scores(i, 1, t)
                    if not last:
                        prepare(i + 1, 0)

                prepare(0, 0)
                with pool.Fori(0, TURNS - 1) as i:
                    turn(i, False)
                turn(TURNS - 1, True)

            @block.scalar
            def _(act):
                def prepare(i, l):
                    act.wait_ge(loaded[l], 32 * NB * i + 32 * NB)
                    for b in range(NB):
                        nc.scalar.activation(pnT[l][b][:, :].rearrange("p (c d) -> p c d", d=D), pn[l][b][:, :, 0:D], ACT.Square).then_inc(squared[l], 1)
                    for b in range(NB):
                        for q in (0, 2):
                            act.wait_ge(turned[l], 4 * (NB * i + b) + q + 1)
                            nc.scalar.activation(pnT[l][b][:, 512 * q:512 * q + 512], Sb[q // 2][:, 0:512], ACT.Copy).then_inc(turned_act[l], 1)

                def square(i, l, first):
                    act.wait_ge(*first)
                    nc.scalar.activation(slsq[l][:, :], slT[l][:, :], ACT.Square).then_inc(sl_sq[l], 1)

                def query(i, l, t):
                    k = R * i + t + 1
                    act.wait_ge(sl_rstd[l], k)
                    for pr in range(2):
                        last = nc.scalar.activation(qn[l][:, 128 * pr:128 * pr + 128], U[l][:, 128 * pr:128 * pr + 128], ACT.Copy, scale=sc[l][:, 1, pr:pr + 1])
                    last.then_inc(q_scaled[l], 1)

                def update(i, l, t):
                    k = R * i + t + 1
                    act.wait_ge(u_inv[l], k)
                    for pr in range(2):
                        last = nc.scalar.activation(un[l][:, 128 * pr:128 * pr + 128], U[l][:, (D + 1) * pr:(D + 1) * pr + D], ACT.Copy, scale=sc[l][:, 3, pr:pr + 1])
                    last.then_inc(u_scaled[l], 1)

                def exp(i, l, t, b):
                    act.wait_ge(centred, half(i, l, t) + b + 1)
                    nc.scalar.activation(e[l][b][:, :, :], e[l][b][:, :, :], ACT.Exp).then_inc(exped, 1)

                def reset_and_update(i, l, t):
                    act.wait_ge(gates[l], R * i + t + 1)
                    nc.scalar.activation(tr[l][:, 0, :], G[l][:, 0:256], ACT.Tanh, bias=c.bias[:, 0:1], scale=0.5)
                    nc.scalar.activation(tr[l][:, 1, :], G[l][:, 256:512], ACT.Tanh, bias=c.bias[:, 1:2], scale=0.5).then_inc(rz[l], 1)

                def new(i, l, t):
                    act.wait_ge(n_in[l], R * i + t + 1)
                    nc.scalar.activation(nn[l][:, :], hn[l][:, 1, :], ACT.Tanh, bias=c.bias[:, 3:4]).then_inc(n_out[l], 1)

                def scores(i, l, t, other):
                    o, k = 1 - l, R * i + t + 1
                    if other is not None:
                        update(i, o, other)
                    query(i, l, t)
                    if other is not None:
                        act.wait_ge(u_turned[o], R * i + other + 1)
                        nc.scalar.activation(uT[o][:, :], U[o][:, 0:256], ACT.Copy).then_inc(u_ready[o], 1)
                    act.wait_ge(q_turned[l], k)
                    nc.scalar.activation(qT[l][:, :], U[l][:, 0:256], ACT.Copy).then_inc(q_ready[l], 1)
                    exp(i, l, t, 0)
                    if other is not None:
                        reset_and_update(i, o, other)
                    exp(i, l, t, 1)
                    if other is not None:
                        new(i, o, other)
                        if other < R - 1:
                            square(i, o, (slots[o], R * i + other + 1))
                    exp(i, l, t, 2)
                    exp(i, l, t, 3)

                def turn(i, last):
                    square(i, 0, (slots_in[0], i + 1))
                    scores(i, 0, 0, None)
                    prepare(i, 1)
                    square(i, 1, (slots_in[1], i + 1))
                    for t in range(R):
                        if t:
                            scores(i, 0, t, t - 1)
                        scores(i, 1, t, t)
                    update(i, 1, R - 1)
                    act.wait_ge(u_turned[1], R * i + R)
                    nc.scalar.activation(uT[1][:, :], U[1][:, 0:256], ACT.Copy).then_inc(u_ready[1], 1)
                    reset_and_update(i, 1, R - 1)
                    new(i, 1, R - 1)
                    if not last:
                        prepare(i + 1, 0)

                prepare(0, 0)
                with act.Fori(0, TURNS - 1) as i:
                    turn(i, False)
                turn(TURNS - 1, True)

            @block.vector
            def _(dve):
                def prepare(i, l, link):
                    for b in range(NB):
                        dve.wait_ge(squared[l], NB * i + b + 1)
                        link(nc.vector.tensor_reduce(out=ms[l][b][:, 0, :], in_=pnT[l][b][:, :].rearrange("p (c d) -> p c d", d=D), op=ALU.add, axis=AX.X))
                        nc.vector.tensor_scalar(ms[l][b][:, 1, :], ms[l][b][:, 0, :], 1.0 / D, EPS, ALU.mult, ALU.add).then_inc(meansq[l], 1)
                    for b in range(NB):
                        for q in (1, 3):
                            w = min(512, NC_ * 128 - 512 * q)
                            dve.wait_ge(turned[l], 4 * (NB * i + b) + q + 1)
                            nc.vector.tensor_copy(pnT[l][b][:, 512 * q:512 * q + w], Sb[q // 2][:, 512:512 + w]).then_inc(turned_dve[l], 1)

                def start(i, l):
                    tile = 4 * i + 2 * l
                    nc.vector.tensor_copy(slT[l][:, :], c.XNT[:, bass.ds(128 * tile, 256)]).then_inc(slots_in[l], 1)

                def query(i, l, t):
                    dve.wait_ge(q_nat[l], R * i + t + 1)
                    nc.vector.tensor_scalar(sc[l][:, 0, :], U[l][:, 256:258], 1.0 / D, EPS, ALU.mult, ALU.add).then_inc(sl_meansq[l], 1)

                def update(i, l, t, link):
                    dve.wait_ge(summed[l], R * i + t + 1)
                    sums = U[l][:, 0:2 * (D + 1)].rearrange("p (t d) -> p t d", d=D + 1)[:, :, D]
                    link(nc.vector.tensor_scalar(sc[l][:, 2, :], sums, EPS, None, ALU.add))
                    nc.vector.reciprocal(sc[l][:, 3, :], sc[l][:, 2, :]).then_inc(u_inv[l], 1)

                def centre(i, l, t, b, link):
                    view = Sb[b % 2][:, 0:NC_ * S].rearrange("p (c s) -> p c s", s=S)
                    dve.wait_ge(scored, half(i, l, t) + b + 1)
                    link(nc.vector.tensor_reduce(out=col[l][b][:, 0, :], in_=view, op=ALU.max, axis=AX.X))
                    nc.vector.tensor_tensor(e[l][b][:, :, :], view, bc(col[l][b][:, 0, :], S), ALU.subtract).then_inc(centred, 1)

                def total(i, l, t, b, link):
                    dve.wait_ge(exped, half(i, l, t) + b + 1)
                    link(nc.vector.tensor_reduce(out=col[l][b][:, 1, :], in_=e[l][b][:, :, :], op=ALU.add, axis=AX.X))
                    nc.vector.reciprocal(col[l][b][:, 2, :], col[l][b][:, 1, :]).then_inc(slot_sum, 1)

                def new(i, l, t, link):
                    dve.wait_ge(rz[l], R * i + t + 1)
                    link(nc.vector.tensor_scalar(hn[l][:, 0, :], U[l][:, 256:512], c.bias[:, 4:5], 0.5, ALU.add, ALU.mult))
                    link(nc.vector.scalar_tensor_tensor(out=hn[l][:, 0, :], in0=tr[l][:, 0, :], scalar=1.0, in1=hn[l][:, 0, :], op0=ALU.add, op1=ALU.mult))
                    nc.vector.tensor_tensor(hn[l][:, 1, :], U[l][:, 0:256], hn[l][:, 0, :], ALU.add).then_inc(n_in[l], 1)

                def blend(i, l, t, link):
                    dve.wait_ge(n_out[l], R * i + t + 1)
                    link(nc.vector.tensor_tensor(slT[l][:, :], slT[l][:, :], nn[l][:, :], ALU.subtract))
                    link(nc.vector.scalar_tensor_tensor(out=hn[l][:, 0, :], in0=tr[l][:, 1, :], scalar=1.0, in1=slT[l][:, :], op0=ALU.add, op1=ALU.mult))
                    nc.vector.scalar_tensor_tensor(out=slT[l][:, :], in0=hn[l][:, 0, :], scalar=0.5, in1=nn[l][:, :],
                                                   op0=ALU.mult, op1=ALU.add).then_inc(slots[l], 1)

                def scores(i, l, t, other, link):
                    o = 1 - l
                    if other is not None:
                        update(i, o, other, link)
                    query(i, l, t)
                    centre(i, l, t, 0, link)
                    centre(i, l, t, 1, link)
                    if other is not None:
                        new(i, o, other, link)
                    total(i, l, t, 0, link)
                    if other is not None:
                        blend(i, o, other, link)
                    centre(i, l, t, 2, link)
                    total(i, l, t, 1, link)
                    centre(i, l, t, 3, link)
                    total(i, l, t, 2, link)
                    total(i, l, t, 3, link)

                def finish(i, l):
                    tile = 4 * i + 2 * l
                    dve.wait_ge(out_turned[l], i + 1)
                    xs = c.X[:, bass.ds(tile, 2), :]
                    nc.vector.tensor_tensor(xs, U[l][:, 0:256].rearrange("p (t d) -> p t d", d=D), xs, ALU.add).then_inc(added[l], 1)

                def turn(i, last, link):
                    start(i, 0)
                    scores(i, 0, 0, None, link)
                    start(i, 1)
                    prepare(i, 1, link)
                    for t in range(R):
                        if t:
                            scores(i, 0, t, t - 1, link)
                        scores(i, 1, t, t, link)
                    finish(i, 0)
                    update(i, 1, R - 1, link)
                    new(i, 1, R - 1, link)
                    blend(i, 1, R - 1, link)
                    if not last:
                        prepare(i + 1, 0, link)
                    finish(i, 1)

                for l in LANES:
                    for b in range(NB):
                        nc.vector.memset(pn[l][b][:, FULL, 0:D], 0.0)
                        last = nc.vector.memset(pn[l][b][:, :, D:D + 1], 1.0)
                last.then_inc(zeroed, 1)
                link = Chain(dve, own_first)
                prepare(0, 0, link)
                OWN = 2 * NB + HALVES * (2 * NB + 1 + 2 + 2)
                with dve.Fori(0, TURNS - 1) as i:
                    link = Chain(dve, own, OWN, i)
                    turn(i, False, link)
                    link.close()
                turn(TURNS - 1, True, Chain(dve, own_last))

            @block.tensor
            def _(pe):
                def prepare(i, l, before):
                    if before is not None:
                        pe.wait_ge(centred, before)
                    for b in range(NB):
                        pe.wait_ge(normed[l], NB * i + b + 1)
                        for q in range(4):
                            if b:
                                pe.wait_ge((turned_act, turned_dve)[q % 2][l], 2 * (NB * i + b - 1) + q // 2 + 1)
                            for ch in range(4 * q, min(4 * q + 4, NC_)):
                                o = 128 * (ch % 8)
                                last = nc.tensor.transpose(Sb[q // 2][:, o:o + 128], pn[l][b][:, ch, 0:D], c.ident[:, :])
                            last.then_inc(turned[l], 1)

                def query(i, l, t):
                    pe.wait_ge(sl_sq[l], R * i + t + 1)
                    for pr in range(2):
                        nc.tensor.matmul(U[l][:, 256 + pr:257 + pr], slsq[l][:, 128 * pr:128 * pr + 128], c.ones[:, 0:1], start=True, stop=True)
                        last = nc.tensor.matmul(U[l][:, 128 * pr:128 * pr + 128], slT[l][:, 128 * pr:128 * pr + 128], c.mq[:, :], start=True, stop=True)
                    last.then_inc(q_nat[l], 1)

                def flip(src, l, ready, k, done):
                    pe.wait_ge(ready[l], k)
                    for pr in range(2):
                        last = nc.tensor.transpose(U[l][:, 128 * pr:128 * pr + 128], src[l][:, 128 * pr:128 * pr + 128], c.ident[:, :])
                    last.then_inc(done[l], 1)

                def score(i, l, t, b):
                    n = half(i, l, t) + b
                    if t or b >= 2:
                        pe.wait_ge(centred, n - 1)
                    for ch in range(NC_):
                        last = nc.tensor.matmul(Sb[b % 2][:, S * ch:S * ch + S], pnT[l][b][:, 128 * ch:128 * ch + 128],
                                                qT[l][:, S * b:S * b + S], start=True, stop=True)
                    last.then_inc(scored, 1)

                def sums(i, l, t):
                    for pr in range(2):
                        pe.wait_ge(attn, half(i, l, t) + 2 * pr + 2)
                        for ch in range(NC_):
                            h = 128 if ch < FULL else TAIL
                            for b in range(2):
                                last = nc.tensor.matmul(U[l][S * b:S * b + S, (D + 1) * pr:(D + 1) * pr + D + 1], e[l][2 * pr + b][0:h, ch, :],
                                                        pn[l][2 * pr + b][0:h, ch, :], start=(ch == 0), stop=(ch == NC_ - 1))
                    last.then_inc(summed[l], 1)

                def gate(i, l, t):
                    pe.wait_ge(u_ready[l], R * i + t + 1)
                    for out, f, parts in ((G[l][:, 0:256], 0, "xh"), (G[l][:, 256:512], 1, "xh"), (U[l][:, 0:256], 2, "x"), (U[l][:, 256:512], 2, "h")):
                        for part in parts:
                            w, v = (c.wcT, uT[l]) if part == "x" else (c.whhT, slT[l])
                            last = nc.tensor.matmul(out, w[:, 128 * f:128 * f + 128], v[:, :], start=(part == parts[0]), stop=(part == parts[-1]))
                    last.then_inc(gates[l], 1)

                def scores(i, l, t, other):
                    o = 1 - l
                    query(i, l, t)
                    if other is not None:
                        flip(un, o, u_scaled, R * i + other + 1, u_turned)
                    flip(qn, l, q_scaled, R * i + t + 1, q_turned)
                    pe.wait_ge(q_ready[l], R * i + t + 1)
                    if t == 0:
                        pe.wait_ge(turned_act[l], 2 * NB * i + 2 * NB)
                        pe.wait_ge(turned_dve[l], 2 * NB * i + 2 * NB)
                    score(i, l, t, 0)
                    if other is not None:
                        gate(i, o, other)
                    for b in range(1, NB):
                        score(i, l, t, b)

                def finish(i, l):
                    pe.wait_ge(slots[l], R * i + R)
                    flip_out = [nc.tensor.transpose(U[l][:, 128 * pr:128 * pr + 128], slT[l][:, 128 * pr:128 * pr + 128], c.ident[:, :]) for pr in range(2)]
                    flip_out[-1].then_inc(out_turned[l], 1)

                def turn(i, last):
                    scores(i, 0, 0, None)
                    prepare(i, 1, half(i, 1, 0))
                    for t in range(R):
                        if t:
                            sums(i, 1, t - 1)
                            scores(i, 0, t, t - 1)
                        sums(i, 0, t)
                        scores(i, 1, t, t)
                    finish(i, 0)
                    sums(i, 1, R - 1)
                    flip(un, 1, u_scaled, R * i + R, u_turned)
                    gate(i, 1, R - 1)
                    if not last:
                        prepare(i + 1, 0, half(i + 1, 0, 0))
                    finish(i, 1)

                prepare(0, 0, None)
                with pe.Fori(0, TURNS - 1) as i:
                    turn(i, False)
                turn(TURNS - 1, True)


def linear_attention_stage(nc, c, p):
    E = 32
    with ExitStack() as ctx:
        m = Memory(nc, ctx, "la")
        wq, wk = m.sb("wq", [128, E]), m.sb("wk", [128, E])
        qe, ke, kv = m.sb("q_expT", [E, T * 128]), m.sb("k_exp", [128, T, E]), m.sb("kv", [E, B, D + 1])
        z = m.sb("z", [128, 2, T])
        bank = [m.ps(f"bank{q}") for q in range(8)]
        loaded, q_mm, q_exp, k_mm, k_exp, kv_mm, kv_out, num_mm, ones_set, done = (m.sem(n) for n in (
            "loaded", "q_projected", "q_exp", "k_projected", "k_exp", "kv_summed", "kv_copied", "numerators", "ones_set", "added"))
        own = m.sem("dve_own")
        PER = 3
        SETS = [(t, min(PER, T - t)) for t in range(0, T, PER)]
        with nc.Block() as block:
            @block.sync
            def _(sp):
                sp.dma_start(wq[:, :], p["L0_attn_q_proj"]).then_inc(loaded, 16)
                sp.dma_start(wk[:, :], p["L0_attn_k_proj"]).then_inc(loaded, 16)

            @block.tensor
            def _(pe):
                pe.wait_ge(loaded, 32)
                for t in range(T):
                    last = nc.tensor.matmul(bank[4][:, E * t:E * t + E], c.XNT[:, 128 * t:128 * t + 128], wk[:, :], start=True, stop=True)
                last.then_inc(k_mm, 1)
                for q in range(4):
                    nc.tensor.matmul(bank[q][0:E, :], wq[:, :], c.XNT[:, 512 * q:512 * q + 512], start=True, stop=True).then_inc(q_mm, 1)
                pe.wait_ge(k_exp, 1)
                for b in range(B):
                    q, h, o = 2 * (b // 8) + b % 2, 64 * (b % 2), 128 * (b // 2 % 4)
                    if q < 4 and b % 8 < 2:
                        pe.wait_ge(q_exp, q + 1)
                    last = nc.tensor.matmul(bank[q][0:E, o:o + 128], ke[h:h + 64, b // 2, :],
                                            c.XN[h:h + 64, b // 2, :], start=True, stop=True)
                    if b % 8 >= 6:
                        last.then_inc(kv_mm, 1)
                for n, (t0, k) in enumerate(SETS):
                    pe.wait_ge(kv_out, 9)
                    for t in range(t0, t0 + k):
                        for b in (2 * t, 2 * t + 1):
                            h, o = 64 * (b % 2), (D + 1) * (t - t0)
                            last = nc.tensor.matmul(bank[n][h:h + 64, o:o + D + 1], qe[:, 64 * b:64 * b + 64], kv[:, b, :], start=True, stop=True)
                    last.then_inc(num_mm, 1)

            @block.scalar
            def _(act):
                act.wait_ge(k_mm, 1)
                nc.scalar.activation(ke[:, :, :], bank[4][:, 0:T * E].rearrange("p (t e) -> p t e", e=E), ACT.Exp).then_inc(k_exp, 1)
                for q in range(4):
                    act.wait_ge(q_mm, q + 1)
                    nc.scalar.activation(qe[:, 512 * q:512 * q + 512], bank[q][0:E, :], ACT.Exp).then_inc(q_exp, 1)

            @block.vector
            def _(dve):
                link = Chain(dve, own)
                nc.vector.memset(kv[:, :, D:D + 1], 1.0).then_inc(kv_out, 1)
                for q in range(8):
                    dve.wait_ge(kv_mm, q + 1)
                    b0 = 8 * (q // 2) + q % 2
                    nc.vector.tensor_copy(kv[:, b0:b0 + 7:2, 0:D], bank[q][0:E, :].rearrange("p (b d) -> p b d", d=D)).then_inc(kv_out, 1)
                for n, (t0, k) in enumerate(SETS):
                    dve.wait_ge(num_mm, n + 1)
                    sums = bank[n][:, 0:k * (D + 1)].rearrange("p (t d) -> p t d", d=D + 1)[:, :, D]
                    link(nc.vector.tensor_scalar(z[:, 0, t0:t0 + k], sums, 1e-8, None, ALU.add))
                    link(nc.vector.reciprocal(z[:, 1, t0:t0 + k], z[:, 0, t0:t0 + k]))
                    for t in range(t0, t0 + k):
                        o = (D + 1) * (t - t0)
                        last = nc.vector.scalar_tensor_tensor(out=c.X[:, t, :], in0=bank[n][:, o:o + D], scalar=z[:, 1, t:t + 1],
                                                              in1=c.X[:, t, :], op0=ALU.mult, op1=ALU.add)
                last.then_inc(done, 1)


def capacity_moe_stage(nc, c, p):
    X8, I, CAP = 8, 512, 256
    J, SL = I // 128, CAP // 128
    TRASH = X8 * CAP
    with ExitStack() as ctx:
        m = Memory(nc, ctx, "cm")
        TK, DS, DT = m.sb("tokens", [128, T, D]), m.sb("dispatched", [128, T, D]), m.sb("dispatchedT", [128, T * 128])
        wi, wo = m.sb("wi", [128, X8, I]), m.sb("wo", [128, X8, J, D])
        H = [m.sb(f"hidden{k}", [128, J, CAP]) for k in range(2)]
        gw, ln = m.sb("gateT", [128, X8]), m.sb("ln", [128, 2])
        tokT = m.sb("tokT", [128, T * 128])
        before, rev, offs = m.sb("before", [128, 128]), m.sb("rev", [128, X8]), m.sb("offs", [128, X8])
        lg, w1, w2, oh = (m.sb(n, [128, T, X8]) for n in ("logits", "work1", "work2", "onehot"))
        col = m.sb("col", [128, 8, T])
        idx, gidx = m.sb("idx", [128, T], i32), m.sb("gather_idx", [128, T], i32)
        zrow, trash = m.sb("zrow", [128, D]), m.sb("trash_row", [128, T])
        st, work = m.sb("stats", [128, 5, T]), DS
        bank = [m.ps(f"bank{q}") for q in range(8)]
        slots_dram = nc.dram_tensor("slots_in", (TRASH + 128 * T, D), fp32, kind="Internal").ap()
        eout_dram = nc.dram_tensor("slots_out", (TRASH + 128, D), fp32, kind="Internal").ap()
        s, own = NormSems(m), m.sem("dve_own")
        loaded, w_loaded, const, zero, zeroed, logit, expd, chose, ranked, routed = (m.sem(n) for n in (
            "loaded", "w_loaded", "const", "zero", "zeroed", "logits", "exp", "chosen", "ranks", "routed"))
        sent, back, turned, dt_out, up, act_out, down, eo, eo_out, got, added, trashed, dve_up = (m.sem(n) for n in (
            "sent", "back", "turned", "dispT", "up", "hidden", "down", "expert_rows", "stored", "gathered", "added", "trashed", "dve_up"))
        with nc.Block() as block:
            @block.sync
            def _(sp):
                sp.dma_start(gw[:, :], p["gateT0"]).then_inc(loaded, 16)
                sp.dma_start(ln[:, :], p["ln_cols"]).then_inc(loaded, 16)
                sp.dma_start(wi[:, :, :], p["wi"].rearrange("e h i -> h e i")).then_inc(w_loaded, 16)
                sp.dma_start(wo[:, :, :, :], p["wo"].rearrange("e (j i) h -> i e j h", i=128)).then_inc(w_loaded, 16)
                sp.wait_ge(zero, 1)
                sp.dma_start(slots_dram[0:TRASH, :].rearrange("(t p) d -> p t d", p=128), TK[:, :, :]).then_inc(zeroed, 16)
                sp.dma_start(eout_dram[TRASH:TRASH + 128, :], zrow[:, :]).then_inc(zeroed, 16)
                sp.wait_ge(sent, 16 * T)
                sp.dma_start(DS[:, :, :], slots_dram[0:TRASH, :].rearrange("(t p) d -> p t d", p=128)).then_inc(back, 16)
                for e in range(X8):
                    sp.wait_ge(eo, e + 1)
                    rows = eout_dram[CAP * e:CAP * e + CAP, :].rearrange("(t p) d -> p t d", p=128)
                    sp.dma_start(rows, DS[:, SL * e:SL * e + SL, :]).then_inc(eo_out, 16)
                sp.wait_ge(eo_out, 16 * X8)
                sp.wait_ge(zeroed, 32)

            @block.gpsimd
            def _(pool):
                nc.gpsimd.memset(TK[:, :, :], 0.0)
                nc.gpsimd.memset(zrow[:, :], 0.0).then_inc(zero, 1)
                nc.gpsimd.iota(trash[:, :], pattern=[[128, T]], base=TRASH, channel_multiplier=1, allow_small_or_imprecise_dtypes=True)
                nc.gpsimd.iota(rev[:, :], pattern=[[-1, X8]], base=X8, channel_multiplier=0, allow_small_or_imprecise_dtypes=True)
                nc.gpsimd.iota(offs[:, :], pattern=[[CAP, X8]], base=0, channel_multiplier=0, allow_small_or_imprecise_dtypes=True).then_inc(const, 1)
                nc.gpsimd.affine_select(out=before[:, :], in_=c.ones[:, :], compare_op=ALU.is_gt, fill=0.0,
                                        base=0, pattern=[[1, 128]], channel_multiplier=-1).then_inc(const, 1)
                norm_pool(nc, pool, st, c.half, s)
                pool.wait_ge(routed, 1)
                pool.wait_ge(zeroed, 32)
                pool.wait_ge(s.normed, 1)
                for t in range(T):
                    nc.gpsimd.indirect_dma_start(out=slots_dram, out_offset=bass.IndirectOffsetOnAxis(ap=idx[:, t:t + 1], axis=0),
                                                 in_=TK[:, t, :], in_offset=None).then_inc(sent, 16)
                pool.wait_ge(eo_out, 16 * X8)
                pool.wait_ge(sent, 16 * T)
                for t in range(T):
                    nc.gpsimd.indirect_dma_start(out=TK[:, t, :], out_offset=None, in_=eout_dram,
                                                 in_offset=bass.IndirectOffsetOnAxis(ap=gidx[:, t:t + 1], axis=0)).then_inc(got, 16)
                pool.wait_ge(got, 16 * T)

            @block.vector
            def _(dve):
                link = Chain(dve, own)
                dve.wait_ge(zeroed, 32)
                norm_dve(nc, dve, link, c.XN, TK, work, st, s, 1e-5)
                dve.wait_ge(loaded, 32)
                for q in range(4):
                    dve.wait_ge(s.transposed, q + 1)
                    nc.vector.tensor_scalar(tokT[:, 512 * q:512 * q + 512], bank[q][:, :], ln[:, 0:1], ln[:, 1:2], ALU.mult, ALU.add).then_inc(s.xnt_dve, 1)
                dve.wait_ge(logit, 1)
                dve.wait_ge(const, 2)
                link(nc.vector.tensor_copy(lg[:, :, :], bank[4][:, 0:T * X8].rearrange("p (t e) -> p t e", e=X8)))
                link(nc.vector.tensor_reduce(out=col[:, 0, :], in_=lg[:, :, :], op=ALU.max, axis=AX.X))
                link(nc.vector.tensor_tensor(w1[:, :, :], lg[:, :, :], bc(col[:, 0, :], X8), ALU.subtract))
                nc.vector.tensor_scalar(w2[:, :, :], w1[:, :, :], 0.0, None, ALU.is_equal).then_inc(chose, 1)
                dve.wait_ge(chose, 1)
                rev_all = rev[:, :].unsqueeze(1).to_broadcast([128, T, X8])
                link(nc.vector.tensor_tensor(w2[:, :, :], w2[:, :, :], rev_all, ALU.mult))
                link(nc.vector.tensor_reduce(out=col[:, 1, :], in_=w2[:, :, :], op=ALU.max, axis=AX.X))
                nc.vector.tensor_tensor(oh[:, :, :], w2[:, :, :], bc(col[:, 1, :], X8), ALU.is_equal).then_inc(chose, 1)
                dve.wait_ge(expd, 1)
                link(nc.vector.tensor_reduce(out=col[:, 2, :], in_=w1[:, :, :], op=ALU.add, axis=AX.X))
                link(nc.vector.reciprocal(col[:, 3, :], col[:, 2, :]))
                dve.wait_ge(ranked, 1)
                src, dst = w1, w2
                link(nc.vector.memset(src[:, 0:1, :], 0.0))
                link(nc.vector.tensor_copy(src[:, 1:T, :], bank[5][:, 128:128 + (T - 1) * X8].rearrange("p (t e) -> p t e", e=X8)))
                k = 1
                while k < T:
                    nc.vector.tensor_copy(dst[:, 0:k, :], src[:, 0:k, :])
                    link(nc.vector.tensor_tensor(dst[:, k:T, :], src[:, k:T, :], src[:, 0:T - k, :], ALU.add))
                    src, dst, k = dst, src, 2 * k
                link(nc.vector.tensor_tensor(dst[:, :, :], bank[5][:, 0:128].rearrange("p (t e) -> p t e", e=X8), src[:, :, :], ALU.add))
                link(nc.vector.tensor_tensor(dst[:, :, :], dst[:, :, :], oh[:, :, :], ALU.mult))
                link(nc.vector.tensor_reduce(out=col[:, 4, :], in_=dst[:, :, :], op=ALU.add, axis=AX.X))
                link(nc.vector.tensor_scalar(col[:, 5, :], col[:, 4, :], float(CAP), None, ALU.is_lt))
                link(nc.vector.tensor_tensor(col[:, 3, :], col[:, 3, :], col[:, 5, :], ALU.mult))
                link(nc.vector.tensor_tensor(src[:, :, :], oh[:, :, :], offs[:, :].unsqueeze(1).to_broadcast([128, T, X8]), ALU.mult))
                link(nc.vector.tensor_reduce(out=col[:, 6, :], in_=src[:, :, :], op=ALU.add, axis=AX.X))
                link(nc.vector.tensor_tensor(col[:, 6, :], col[:, 6, :], col[:, 4, :], ALU.add))
                link(nc.vector.tensor_tensor(col[:, 0, :], col[:, 6, :], trash[:, :], ALU.subtract))
                link(nc.vector.tensor_tensor(col[:, 0, :], col[:, 0, :], col[:, 5, :], ALU.mult))
                nc.vector.tensor_tensor(idx[:, :], col[:, 0, :], trash[:, :], ALU.add)
                link(nc.vector.tensor_scalar(col[:, 1, :], col[:, 6, :], -float(TRASH), None, ALU.add))
                link(nc.vector.tensor_tensor(col[:, 1, :], col[:, 1, :], col[:, 5, :], ALU.mult))
                nc.vector.tensor_scalar(gidx[:, :], col[:, 1, :], float(TRASH), None, ALU.add).then_inc(routed, 1)
                link(nc.vector.tensor_tensor(c.X[:, :, :], c.X[:, :, :], c.XN[:, :, :], ALU.add))
                for q in range(4):
                    dve.wait_ge(turned, q + 1)
                    nc.vector.tensor_scalar(DT[:, 512 * q:512 * q + 512], bank[q][:, :], ln[:, 0:1], ln[:, 1:2], ALU.mult, ALU.add).then_inc(dt_out, 1)
                for e in range(X8):
                    dve.wait_ge(down, e + 1)
                    nc.vector.tensor_copy(DS[:, SL * e:SL * e + SL, :], bank[6 + e % 2][:, 0:SL * D].rearrange("p (t d) -> p t d", d=D)).then_inc(eo, 1)
                dve.wait_ge(got, 16 * T)
                for t in range(T):
                    last = nc.vector.scalar_tensor_tensor(out=c.X[:, t, :], in0=TK[:, t, :], scalar=col[:, 3, t:t + 1], in1=c.X[:, t, :],
                                                          op0=ALU.mult, op1=ALU.add)
                last.then_inc(added, 1)

            @block.scalar
            def _(act):
                norm_act(nc, act, TK, work, s)
                act.wait_ge(chose, 1)
                nc.scalar.activation(w1[:, :, :], w1[:, :, :], ACT.Exp).then_inc(expd, 1)
                for e in range(X8):
                    for j in range(J):
                        n = J * e + j
                        act.wait_ge(up, n + 1)
                        if e >= 2 and j == 0:
                            act.wait_ge(down, e - 1)
                        nc.scalar.activation(H[e % 2][:, j, :], bank[n % 4][:, 0:CAP], ACT.Gelu).then_inc(act_out, 1)

            @block.tensor
            def _(pe):
                transpose_pe(nc, pe, TK, bank, c.ident, s)
                pe.wait_ge(s.xnt_dve, 4)
                for t in range(T):
                    last = nc.tensor.matmul(bank[4][:, X8 * t:X8 * t + X8], tokT[:, 128 * t:128 * t + 128], gw[:, :], start=True, stop=True)
                last.then_inc(logit, 1)
                pe.wait_ge(chose, 2)
                oh2 = oh[:, :, :].rearrange("p t e -> p (t e)")
                nc.tensor.matmul(bank[5][:, 0:128], before[:, :], oh2, start=True, stop=True)
                nc.tensor.matmul(bank[5][:, 128:256], c.ones[:, :], oh2, start=True, stop=True).then_inc(ranked, 1)
                pe.wait_ge(back, 16)
                for q in range(4):
                    for j in range(4):
                        last = nc.tensor.transpose(bank[q][:, 128 * j:128 * j + 128], DS[:, 4 * q + j, :], c.ident[:, :])
                    last.then_inc(turned, 1)
                pe.wait_ge(w_loaded, 32)
                pe.wait_ge(dt_out, 4)
                for e in range(X8):
                    for j in range(J):
                        n = J * e + j
                        if n >= 4:
                            pe.wait_ge(act_out, n - 3)
                        nc.tensor.matmul(bank[n % 4][:, 0:CAP], wi[:, e, 128 * j:128 * j + 128], DT[:, CAP * e:CAP * e + CAP],
                                         start=True, stop=True).then_inc(up, 1)
                    pe.wait_ge(act_out, J * e + J)
                    if e >= 2:
                        pe.wait_ge(eo, e - 1)
                    for k in range(SL):
                        for j in range(J):
                            last = nc.tensor.matmul(bank[6 + e % 2][:, D * k:D * k + D], H[e % 2][:, j, 128 * k:128 * k + 128], wo[:, e, j, :],
                                                    start=(j == 0), stop=(j == J - 1))
                    last.then_inc(down, 1)


def masked_attention_stage(nc, c, p):
    H, DH, MASKED = 16, 8, -1e30
    NP, F = H // 2, 2 * DH
    PARTS_Q, PARTS_K = (0, 0, 1, 1, 0, 2), (0, 1, 0, 1, 2, 0)
    ROWS = F * len(PARTS_Q)
    PIECES = [(512 * w, min(512, M - 512 * w)) for w in range(4)]
    AHEAD = (0, 2, 5, 8)
    TURN_ROWS = 1
    FIRST, LAG = 2, 3
    OUT1, OUT2 = 6, 10
    STACKED = 16 * len(PARTS_K)
    with ExitStack() as ctx:
        m = Memory(nc, ctx, "ma")
        wq, wk, wv, wo, bo = (m.sb(n, [128, 128]) for n in ("wq", "wk", "wv", "wo", "bo"))
        QT = OT = c.XN[:, :, :].rearrange("p t d -> p (t d)")
        cT = [m.sb(f"ctxT{k}", [128, M]) for k in range(2)]
        KP, KR = m.sb("k_parts", [128, 3, M], bf16), m.sb("k_rest", [128, M])
        KS = [m.sb(f"k_stack{k}", [128, NP, M], bf16) for k in range(2)]
        QR = m.sb("q_stack", [ROWS, NP, B * S], bf16)
        Q = [m.sb(f"q_blocks{k}", [128, NP, 2 * S], bf16) for k in range(2)]
        V = [m.sb(f"v{k}", [128, NC_, NP, F + 1]) for k in range(2)]
        mraw = m.sb("mask_raw", [128, M], i32)
        mb = [m.sb(f"mask_bias{k}", [128, M], bf16) for k in range(2)]
        masked = [m.sb(f"masked_scores{k}", [128, 512], bf16) for k in range(2)]
        ET = [m.sb(f"eT{k}", [128, 512]) for k in range(4)]
        mx, nmx = m.sb("mx", [128, 4, 4]), m.sb("nmx", [128, 4])
        mp = m.sb("max_parts", [128, 4, 3], bf16)
        Osb, On, rden, acc = m.sb("sums_sb", [128, 256]), m.sb("out_norm", [128, 128]), m.sb("rden", [128, NP]), m.sb("acc", [128, S])
        blk2, eye2 = m.sb("blk2", [128, 2]), m.sb("eye2", [128, S])
        identb, eyes = m.sb("identb", [128, 128], bf16), m.sb("eyes", [S, 8, S], bf16)
        S1 = [m.ps(f"scores{w}") for w in range(2)]
        S2 = [m.ps(f"scoresT{w}") for w in range(3)]
        OB, PB, MB = m.ps("sums"), m.ps("proj"), m.ps("misc")
        Qparts = KS[1][:, :, :].rearrange("p n m -> p (n m)")[:, 0:3 * B * S].rearrange("p (t q) -> p t q", t=3)

        (w_loaded, const, q_mm, q_out, q_rest, q_split, q_stacked, mask_ready, q_ready, scored, maxed, max_ready, rows_mm, rows_ready,
         scored2, exped, weighed, o_read, o_turned, o_normed, o_back, o_done, projected, kh_out, k_out, split, v_out,
         out_mm, added, mask_loaded, bank_zero) = (m.sem(n) for n in (
            "w_loaded", "const", "q_projected", "q_scaled", "q_rest", "q_split", "q_stacked", "mask_ready", "q_ready", "scored", "maxed",
            "max_ready", "max_rows_mm", "max_rows", "scoredT", "exped", "weighed", "o_read", "o_turned", "o_normed",
            "o_back", "o_done", "projected", "kh_out", "k_out", "k_split", "v_out", "out_projected", "added", "mask_loaded", "bank_zero"))
        pool_own = m.sem("pool_own")
        ctx_loaded = [m.sem(f"ctx_loaded{k}") for k in range(2)]
        stacked = [m.sem(f"k_stacked{a}") for a in range(2)]
        own, own_first, own_last = m.sem("dve_own"), m.sem("dve_own_first"), m.sem("dve_own_last")
        dve_passed, pool_passed = m.sem("dve_passed"), m.sem("pool_passed")
        PAIRS = B // 2

        def bank_of(s, ch):
            x = NC_ * s + ch
            return x % 3, 3 if x > 2 else (1, 4, 4)[x]

        with nc.Block() as block:
            @block.sync
            def _(sp):
                for dst, name in ((wq, "WqT1"), (wk, "WkT1"), (wv, "WvT1"), (wo, "WoT1")):
                    sp.dma_start(dst[:, :], p[name]).then_inc(w_loaded, 16)
                sp.dma_start(bo[:, :], p["bo"].partition_broadcast(128)).then_inc(w_loaded, 16)
                for t, part in sorted(enumerate(PARTS_Q), key=lambda x: x[1]):
                    sp.wait_ge(q_split, part + 1)
                    for a in range(2):
                        sp.dma_start(QR[F * t:F * t + F, 4 * a:4 * a + 4, :], Qparts[64 * a:64 * a + 64, part, :]).then_inc(q_stacked, 16)
                sp.wait_ge(w_loaded, 80)
                sp.wait_ge(q_stacked, 192)

            @block.gpsimd
            def _(pool):
                nc.gpsimd.memset(blk2[:, :], 0.0)
                nc.gpsimd.memset(eye2[:, :], 0.0).then_inc(const, 1)
                n = 1
                fills = [(blk2, 2, 8, r + F * h) for h in range(NP) for r in range(DH)]
                fills += [(eye2, S, 1, 64 * h) for h in range(2)]
                for dst, k, step, base in fills:
                    pool.wait_ge(const, n)
                    nc.gpsimd.affine_select(out=dst[:, :], in_=dst[:, :], compare_op=ALU.not_equal, fill=1.0, base=-base,
                                            pattern=[[-step, k]], channel_multiplier=1).then_inc(const, 1)
                    n += 1
                pool.wait_ge(const, n)
                nc.gpsimd.tensor_copy(eyes[:, :, :], eye2[0:S, :].unsqueeze(1).to_broadcast([S, 8, S])).then_inc(const, 1)
                nc.gpsimd.tensor_copy(identb[:, :], c.ident[:, :]).then_inc(const, 1)

            @block.tensor
            def _(pe):
                pe.wait_ge(w_loaded, 80)
                for q in range(4):
                    nc.tensor.matmul((S1 + S2)[q][:, :], wq[:, :], c.XNT[:, 512 * q:512 * q + 512], start=True, stop=True).then_inc(q_mm, 1)

            @block.scalar
            def _(act):
                for q in range(4):
                    act.wait_ge(q_mm, q + 1)
                    nc.scalar.activation(QT[:, 512 * q:512 * q + 512], (S1 + S2)[q][:, :], ACT.Copy, scale=float(DH) ** -0.5).then_inc(q_out, 1)
                act.wait_ge(q_out, 4)
                nc.scalar.activation(Qparts[:, 0, :], QT[:, :], ACT.Copy).then_inc(q_split, 1)

            @block.vector
            def _(dve):
                nc.vector.memset(OB[:, :], 0.0).then_inc(bank_zero, 1)
                for k in range(2):
                    nc.vector.memset(V[k][:, :, :, F:F + 1], 1.0)
                nc.vector.memset(KS[0][ROWS:ROWS + 3, :, :], 1.0)
                dve.wait_ge(q_split, 1)
                nc.vector.tensor_tensor(QT[:, :], QT[:, :], Qparts[:, 0, :], ALU.subtract).then_inc(q_rest, 1)
                dve.wait_ge(q_rest, 1)
                nc.vector.tensor_copy(Qparts[:, 1, :], QT[:, :]).then_inc(q_split, 1)
                dve.wait_ge(q_split, 2)
                nc.vector.tensor_tensor(Qparts[:, 2, :], QT[:, :], Qparts[:, 1, :], ALU.subtract).then_inc(q_split, 1)
                dve.wait_ge(q_stacked, 192)
                nc.vector.memset(KS[1][ROWS:ROWS + 3, :, :], 1.0)

        with nc.Block() as block:
            @block.sync
            def _(sp):
                def load_ctx(b, k):
                    sp.dma_start(cT[k][:, :], p["ctxT"][bass.ds(b, 1), :, :].rearrange("a d m -> (a d) m")).then_inc(ctx_loaded[k], 16)

                def load_mask(b):
                    rows = p["mask"][bass.ds(b, 1), :, :].rearrange("a s m -> (a s) m")
                    for h in range(2):
                        sp.dma_start(mraw[64 * h:64 * h + 64, :], rows).then_inc(mask_loaded, 16)

                def stack(b, k, a):
                    if a == 0:
                        sp.wait_ge(split, b + 1)
                    if not (isinstance(b, int) and b < 2):
                        sp.wait_ge(scored2, NC_ * (2 * b - 3 + a))
                    for t, part in enumerate(PARTS_K):
                        sp.dma_start(KS[k][F * t:F * t + F, 4 * a:4 * a + 4, :],
                                     KP[64 * a:64 * a + 64, part, :]).then_inc(stacked[a], 16)

                def batch(b, k, ahead=2):
                    if ahead == 2:
                        sp.wait_ge(projected, 8 * b + 8)
                        load_ctx(b + 2, k)
                    stack(b + 1, 1 - k, 0)
                    stack(b + 1, 1 - k, 1)
                    if ahead == 2:
                        sp.wait_ge(mask_ready, b + 2)
                        load_mask(b + 2)

                load_ctx(0, 0)
                load_mask(0)
                load_ctx(1, 1)
                stack(0, 0, 0)
                stack(0, 0, 1)
                sp.wait_ge(mask_ready, 1)
                load_mask(1)
                batch(0, 0)
                batch(1, 1)
                with sp.Fori(1, PAIRS - 1) as i:
                    batch(2 * i, 0)
                    batch(2 * i + 1, 1)
                batch(B - 2, 0, 1)

            @block.gpsimd
            def _(pool):
                def parts(b):
                    pool.wait_ge(k_out, 4 * b + 4)
                    pool.sem_inc(pool_passed, 1)
                    nc.gpsimd.tensor_copy(KP[:, 1, :], KR[:, :]).then_inc(pool_own, 1)
                    pool.wait_ge(pool_own, b + 1)
                    nc.gpsimd.tensor_tensor(KP[:, 2, :], KR[:, :], KP[:, 1, :], ALU.subtract).then_inc(split, 1)

                def prepare(b, k):
                    if not (isinstance(b, int) and b < 2):
                        pool.wait_ge(scored2, 2 * NC_ * (b - 1))
                    pool.wait_ge(mask_loaded, 32 * b + 32)
                    pool.sem_inc(pool_passed, 1)
                    nc.gpsimd.tensor_scalar(mb[k][:, :], mraw[:, :], 0, MASKED, ALU.is_equal, ALU.mult).then_inc(mask_ready, 1)
                    q = QR[:, :, bass.ds(64 * b, S)].unsqueeze(2).to_broadcast([ROWS, NP, 2, S])
                    blocks = blk2[0:ROWS, :].unsqueeze(1).unsqueeze(3).to_broadcast([ROWS, NP, 2, S])
                    nc.gpsimd.tensor_tensor(Q[k][0:ROWS, :, :].rearrange("p n (h q) -> p n h q", h=2), q, blocks, ALU.mult).then_inc(q_ready, 1)

                prepare(0, 0)
                parts(0)
                for b in range(2):
                    parts(b + 1)
                    prepare(b + 1, 1 - b)
                with pool.Fori(1, PAIRS - 1) as i:
                    for k in range(2):
                        parts(2 * i + k + 1)
                        prepare(2 * i + k + 1, 1 - k)
                parts(B - 1)
                prepare(B - 1, 1)

            @block.tensor
            def _(pe):
                def project(b, k, i, n):
                    if n == 0:
                        pe.wait_ge(ctx_loaded[k], 16 * i + 16)
                    if n in (0, 5, 6, 7) and not (isinstance(b, int) and b == 0 and n == 0):
                        pe.wait_ge(v_out, 4 * b + max(n - 4, 0))
                    if n in (1, 2, 3, 4):
                        pe.wait_ge(k_out, 4 * b + n)
                    if n < 4:
                        o, w = PIECES[n]
                        nc.tensor.matmul(PB[:, 0:w], wk[:, :], cT[k][:, o:o + w], start=True, stop=True).then_inc(projected, 1)
                        return
                    for ch in range(4 * (n - 4), min(4 * (n - 4) + 4, NC_)):
                        h = 128 if ch < FULL else TAIL
                        last = nc.tensor.matmul(PB[0:h, 128 * (ch % 4):128 * (ch % 4) + 128], cT[k][:, 128 * ch:128 * ch + h], wv[:, :], start=True, stop=True)
                    last.then_inc(projected, 1)

                def score(b, k, a, r):
                    j, (o, w) = r // 4, PIECES[r % 4]
                    n = 16 * (2 * b + a) + r
                    if r == 0:
                        if a == 0:
                            pe.wait_ge(q_ready, b + 1)
                        pe.wait_ge(stacked[a], STACKED * (b + 1))
                    if not (isinstance(n, int) and n < 2):
                        pe.wait_ge(maxed, n - 1)
                    nc.tensor.matmul(S1[r % 2][:, 0:w], Q[k][0:ROWS, 4 * a + j, :], KS[k][0:ROWS, 4 * a + j, o:o + w], start=True, stop=True).then_inc(scored, 1)

                def max_rows(u):
                    pe.wait_ge(max_ready, u)
                    for j in range(4):
                        last = nc.tensor.matmul(MB[ROWS:ROWS + 3, 128 * j:128 * j + 128], mp[:, j, :], identb[:, :], start=True, stop=True)
                    last.then_inc(rows_mm, 1)

                def score_turned(v, s, kb, av, ch):
                    h = 128 if ch < FULL else TAIL
                    g, (bank, lag) = NC_ * v + ch, bank_of(s, ch)
                    if ch == 0:
                        pe.wait_ge(rows_ready, v + 1)
                    if not (isinstance(g, int) and g < lag):
                        pe.wait_ge(exped, g - lag + 1)
                    out = S2[bank]
                    nc.tensor.matmul(out[0:h, :], mb[kb][0:S, 128 * ch:128 * ch + h], eyes[:, :, :].rearrange("p n q -> p (n q)"), start=True, stop=False)
                    for j in range(4):
                        last = nc.tensor.matmul(out[0:h, 128 * j:128 * j + 128], KS[kb][0:ROWS + 3, 4 * av + j, 128 * ch:128 * ch + h],
                                                Q[kb][0:ROWS + 3, 4 * av + j, :], start=False, stop=(j == 3))
                    last.then_inc(scored2, 1)

                def weigh(v, s, kb, av, ch):
                    h = 128 if ch < FULL else TAIL
                    if ch == 0:
                        if not (isinstance(v, int) and v == 0):
                            pe.wait_ge(o_read, v)
                    pe.wait_ge(exped, NC_ * v + ch + 1)
                    for j in range(4):
                        last = nc.tensor.matmul(OB[32 * j:32 * j + F + 1, 128 * av:128 * av + 128], V[kb][0:h, ch, 4 * av + j, :],
                                                ET[(NC_ * s + ch) % 4][0:h, 128 * j:128 * j + 128], start=(ch == 0), stop=(ch == NC_ - 1))
                    last.then_inc(weighed, 1)

                def slot(i, s, scores=True, before=True, ahead=True, finished=True):
                    k, a = s // 2, s % 2
                    b = 2 * i + k
                    u = 2 * b + a
                    kb, av = ((s - 1) // 2) % 2, (s - 1) % 2
                    for r in range(16):
                        if scores:
                            score(b, k, a, r)
                        if ahead and r in AHEAD:
                            project(b + 1, 1 - k, i + k, 4 * a + AHEAD.index(r))
                        if before and r == TURN_ROWS:
                            if a == 0 and not (isinstance(b, int) and b < 2):
                                pe.wait_ge(o_done, b - 1)
                            max_rows(u)
                        if before and FIRST <= r < FIRST + NC_:
                            score_turned(u - 1, s, kb, av, r - FIRST)
                            if r - FIRST >= LAG:
                                weigh(u - 1, s, kb, av, r - FIRST - LAG)
                        if finished and a == 1 and r == OUT1:
                            pe.wait_ge(o_read, 2 * b)
                            for x in range(2):
                                last = nc.tensor.transpose(MB[:, 128 * x:128 * x + 128], Osb[:, 128 * x:128 * x + 128], c.ident[:, :])
                            last.then_inc(o_turned, 1)
                        if finished and a == 1 and r == OUT2:
                            pe.wait_ge(o_normed, b)
                            nc.tensor.transpose(MB[:, 256:384], On[:, :], c.ident[:, :]).then_inc(o_back, 1)
                    if before:
                        for ch in range(NC_ - LAG, NC_):
                            weigh(u - 1, s, kb, av, ch)

                for n in range(8):
                    project(0, 0, 0, n)
                for s in range(4):
                    slot(0, s, before=s > 0, finished=s > 1)
                with pe.Fori(1, PAIRS - 1) as i:
                    for s in range(4):
                        slot(i, s)
                for s in range(4):
                    slot(PAIRS - 1, s, ahead=s < 2)
                slot(PAIRS, 0, scores=False, ahead=False)
                slot(PAIRS, 1, scores=False, before=False, ahead=False)

            @block.vector
            def _(dve):
                def rest(b, n):
                    o, w = PIECES[n]
                    dve.wait_ge(kh_out, 4 * b + n + 1)
                    nc.vector.tensor_tensor(KR[:, o:o + w], PB[:, 0:w], KP[:, 0, o:o + w], ALU.subtract).then_inc(k_out, 1)

                def values(b, k, n):
                    if n == 0 and not (isinstance(b, int) and b < 2):
                        dve.wait_ge(weighed, 2 * NC_ * (b - 1))
                    dve.wait_ge(projected, 8 * b + 5 + n)
                    w, h = (4, 128) if n < 3 else (1, TAIL)
                    nc.vector.tensor_copy(V[k][0:h, 4 * n:4 * n + w, :, 0:F],
                                          PB[0:h, 0:128 * w].rearrange("p (c n f) -> p c n f", c=w, f=F)).then_inc(v_out, 1)

                def slot(i, s, link, scores=True, ahead=True, finished=True):
                    k, a = s // 2, s % 2
                    b = 2 * i + k
                    u = 2 * b + a
                    if scores and a == 0:
                        dve.wait_ge(mask_ready, b + 1)
                    for r in range(16):
                        if scores:
                            o, w = PIECES[r % 4]
                            dve.wait_ge(scored, 16 * u + r + 1)
                            dve.sem_inc(dve_passed, 1)
                            nc.vector.tensor_tensor_reduce(out=masked[r % 2][:, 0:w], in0=S1[r % 2][:, 0:w], in1=mb[k][:, o:o + w],
                                                           scale=1.0, scalar=-3e38, op0=ALU.add, op1=ALU.max,
                                                           accum_out=mx[:, r // 4, r % 4:r % 4 + 1]).then_inc(maxed, 1)
                        if ahead and r in AHEAD:
                            if a == 0:
                                rest(b + 1, AHEAD.index(r))
                            else:
                                values(b + 1, 1 - k, AHEAD.index(r))
                        if finished and a == 1 and r == OUT1:
                            dve.wait_ge(o_turned, b)
                            turned = MB[:, 0:256].rearrange("p (n f) -> p n f", f=32)
                            link(nc.vector.reciprocal(rden[:, :], turned[:, :, F]))
                            nc.vector.tensor_tensor(On[:, :].rearrange("p (n f) -> p n f", f=F), turned[:, :, 0:F], bc(rden[:, :], F), ALU.mult).then_inc(o_normed, 1)
                        if finished and a == 1 and r == OUT2:
                            dve.wait_ge(o_back, b)
                            link(nc.vector.tensor_scalar(acc[:, :], MB[:, 256:256 + S], blk2[:, 0:1], None, ALU.mult))
                            nc.vector.scalar_tensor_tensor(out=OT[:, bass.ds(S * (b - 1), S)], in0=MB[:, 256 + S:256 + 2 * S], scalar=blk2[:, 1:2], in1=acc[:, :],
                                                           op0=ALU.mult, op1=ALU.add).then_inc(o_done, 1)
                    if scores:
                        dve.wait_ge(maxed, 16 * u + 16)
                        link(nc.vector.tensor_reduce(out=nmx[:, :], in_=mx[:, :, :], op=ALU.max, axis=AX.X, negate=True))
                        link(nc.vector.tensor_copy(mp[:, :, 0], nmx[:, :]))
                        link(nc.vector.tensor_tensor(nmx[:, :], nmx[:, :], mp[:, :, 0], ALU.subtract))
                        link(nc.vector.tensor_copy(mp[:, :, 1], nmx[:, :]))
                        nc.vector.tensor_tensor(mp[:, :, 2], nmx[:, :], mp[:, :, 1], ALU.subtract).then_inc(max_ready, 1)

                OWN = 4 * 4 + 2 * 2

                for n in range(4):
                    rest(0, n)
                for n in range(4):
                    values(0, 0, n)
                link = Chain(dve, own_first)
                for s in range(4):
                    slot(0, s, link, finished=s > 1)
                with dve.Fori(1, PAIRS - 1) as i:
                    link = Chain(dve, own, OWN, i - 1)
                    for s in range(4):
                        slot(i, s, link)
                    link.close()
                link = Chain(dve, own_last)
                for s in range(4):
                    slot(PAIRS - 1, s, link, ahead=s < 2)
                slot(PAIRS, 1, link, scores=False, ahead=False)

            @block.scalar
            def _(act):
                def high(b, n):
                    if n == 0 and not (isinstance(b, int) and b == 0):
                        for a in range(2):
                            act.wait_ge(stacked[a], STACKED * b)
                    act.wait_ge(projected, 8 * b + n + 1)
                    o, w = PIECES[n]
                    nc.scalar.activation(KP[:, 0, o:o + w], PB[:, 0:w], ACT.Copy).then_inc(kh_out, 1)

                def slot(i, s, before=True, ahead=True, sums=True):
                    k, a = s // 2, s % 2
                    b = 2 * i + k
                    u = 2 * b + a
                    if sums:
                        act.wait_ge(weighed, NC_ * (u - 1))
                        x = 128 * (s % 2)
                        nc.scalar.activation(Osb[:, x:x + 128], OB[:, x:x + 128], ACT.Copy).then_inc(o_read, 1)
                    for r in range(16):
                        if ahead and a == 0 and r in AHEAD:
                            high(b + 1, AHEAD.index(r))
                        if before and r == TURN_ROWS:
                            act.wait_ge(rows_mm, u)
                            kb, av = ((s - 1) // 2) % 2, (s - 1) % 2
                            nc.scalar.activation(Q[kb][ROWS:ROWS + 3, 4 * av:4 * av + 4, :], MB[ROWS:ROWS + 3, :].rearrange("p (n q) -> p n q", n=4), ACT.Copy).then_inc(rows_ready, 1)
                        if before and FIRST <= r < FIRST + NC_:
                            ch = r - FIRST
                            h, g = 128 if ch < FULL else TAIL, NC_ * (u - 1) + ch
                            if not (isinstance(g, int) and g < 4):
                                act.wait_ge(weighed, g - 3)
                            act.wait_ge(scored2, g + 1)
                            nc.scalar.activation(ET[(NC_ * s + ch) % 4][0:h, :], S2[bank_of(s, ch)[0]][0:h, :], ACT.Exp).then_inc(exped, 1)

                for n in range(4):
                    high(0, n)
                for s in range(4):
                    slot(0, s, before=s > 0, sums=s > 1)
                with act.Fori(1, PAIRS - 1) as i:
                    for s in range(4):
                        slot(i, s)
                for s in range(4):
                    slot(PAIRS - 1, s, ahead=s < 2)
                slot(PAIRS, 0, ahead=False)
                slot(PAIRS, 1, before=False, ahead=False)

        with nc.Block() as block:
            @block.tensor
            def _(pe):
                for t in range(T):
                    last = nc.tensor.matmul((S1 + S2)[t // 4][:, 128 * (t % 4):128 * (t % 4) + 128], OT[:, 128 * t:128 * t + 128], wo[:, :], start=True, stop=True)
                    if t % 4 == 3:
                        last.then_inc(out_mm, 1)

            @block.vector
            def _(dve):
                nc.vector.tensor_tensor(c.X[:, :, :], c.X[:, :, :], bo[:, :].unsqueeze(1).to_broadcast([128, T, D]), ALU.add).then_inc(added, 1)
                dve.wait_ge(added, 1)
                for q in range(4):
                    dve.wait_ge(out_mm, q + 1)
                    nc.vector.tensor_tensor(c.X[:, 4 * q:4 * q + 4, :], (S1 + S2)[q][:, :].rearrange("p (t d) -> p t d", d=D), c.X[:, 4 * q:4 * q + 4, :], ALU.add).then_inc(added, 1)


def retention_stage(nc, c, p):
    NH, DQ, DV = 8, 16, 32
    HH, NG = 2, 4
    with ExitStack() as ctx:
        m = Memory(nc, ctx, "re")
        w = {n: m.sb(n, [128, 128]) for n in ("rWq", "rWqs", "rWk", "rWks")}
        wv, wg, wo, woraw = m.sb("wv", [128, 256]), m.sb("wg", [128, 256]), m.sb("wo", [128, 2, 128]), m.sb("wo_raw", [128, 2, 128])
        cosT, sinT, gcol, head = m.sb("cos", [128, S]), m.sb("sin", [128, S]), m.sb("gcol", [128, 1]), m.sb("head", [128, HH])
        decay = m.sb("decay", [128, 512])
        tmp = [m.sb(f"tmp{k}", [128, 512]) for k in range(2)]
        qr, kr, QB = c.XN[:, :, :].rearrange("p t d -> p (t d)"), m.sb("k_rot", [128, T * 128]), m.sb("q_blocks", [128, HH, T * 128])
        V, G, P = m.sb("v", [128, T, 256]), m.sb("gate", [128, T, 256]), m.sb("weights", [128, T, 512])
        O, ms = V, m.sb("ms", [128, 3, T * NH])
        big_half = m.sb("big_half", [128, T * NH])
        OT = P[:, :, :].rearrange("p t n -> p (t n)")[:, 0:2 * T * 128].rearrange("p (j n) -> p j n", j=2)
        bank = [m.ps(f"bank{q}") for q in range(8)]
        (loaded, qk_mm, roped, blocked, vg_mm, v_out, g_act, g_out, s_mm, p_out, o_mm, o_sq, o_ms, o_rs, o_done, t_mm, t_act, y_mm, added, own, half_set) = (
            m.sem(n) for n in ("loaded", "qk_projected", "roped", "q_blocked", "vg_projected", "v_out", "gate_tanh", "gate_out", "scored", "decayed",
                               "o_summed", "o_squared", "o_meansq", "o_rstd", "o_done", "turned", "turned_out", "y_projected", "added", "dve_own", "half_set"))
        loads = [(w[n], p[n]) for n in w] + [(wv, p["rWv"]), (wg, p["rWg"]), (cosT, p["cosT"]), (sinT, p["sinT"]), (gcol, p["gcol"]),
                                             (head, p["head"]), (decay, p["decay"])]

        with nc.Block() as block:
            @block.sync
            def _(sp):
                for dst, src in loads:
                    sp.dma_start(dst[:, :], src).then_inc(loaded, 16)
                sp.dma_start(woraw[:, :, :], p["rWo"].rearrange("(j i) d -> i j d", i=128)).then_inc(loaded, 16)
                sp.wait_ge(loaded, 16 * (len(loads) + 1))

            @block.tensor
            def _(pe):
                pe.wait_ge(loaded, 16 * (len(loads) + 1))
                for q in range(4):
                    if q >= 2:
                        pe.wait_ge(roped, 2 * (q - 1))
                    for k, n in enumerate(w):
                        nc.tensor.matmul(bank[4 * (q % 2) + k][:, :], w[n][:, :], c.XNT[:, 512 * q:512 * q + 512], start=True, stop=True).then_inc(qk_mm, 1)

            @block.vector
            def _(dve):
                link = Chain(dve, own)
                cs, sn = (v[:, :].unsqueeze(1).to_broadcast([128, 8, S]) for v in (cosT, sinT))
                for q in range(4):
                    for k, dst in enumerate((qr, kr)):
                        straight, swapped = (bank[4 * (q % 2) + 2 * k + x][:, :].rearrange("p (b s) -> p b s", s=S) for x in range(2))
                        dve.wait_ge(qk_mm, 4 * q + 2 * k + 2)
                        nc.vector.tensor_tensor(tmp[0][:, :].rearrange("p (b s) -> p b s", s=S), straight, cs, ALU.mult)
                        link(nc.vector.tensor_tensor(tmp[1][:, :].rearrange("p (b s) -> p b s", s=S), swapped, sn, ALU.mult))
                        nc.vector.tensor_tensor(dst[:, 512 * q:512 * q + 512], tmp[0][:, :], tmp[1][:, :], ALU.add).then_inc(roped, 1)
                        dve.wait_ge(roped, 2 * q + k + 1)
                for j in range(2):
                    nc.vector.tensor_scalar(wo[:, j, :], woraw[:, j, :], gcol[:, 0:1], 0.5, ALU.mult, ALU.mult)
                nc.vector.memset(big_half[:, :], -0.5).then_inc(half_set, 1)

            @block.scalar
            def _(act):
                for q in range(4):
                    act.wait_ge(roped, 2 * q + 1)
                    for hh in range(HH):
                        nc.scalar.activation(QB[:, hh, 512 * q:512 * q + 512], qr[:, 512 * q:512 * q + 512], ACT.Copy, scale=head[:, hh:hh + 1]).then_inc(blocked, 1)

        with nc.Block() as block:
            @block.tensor
            def _(pe):
                for n in range(T // 2):
                    for k, wt in enumerate((wv, wg)):
                        if n >= 4:
                            pe.wait_ge((v_out, g_out)[k], n - 3)
                        for t in (2 * n, 2 * n + 1):
                            last = nc.tensor.matmul(bank[4 * k + n % 4][:, 256 * (t % 2):256 * (t % 2) + 256], c.XNT[:, 128 * t:128 * t + 128], wt[:, :], start=True, stop=True)
                        last.then_inc(vg_mm, 1)

            @block.scalar
            def _(act):
                for n in range(T // 2):
                    act.wait_ge(vg_mm, 2 * n + 1)
                    nc.scalar.activation(V[:, 2 * n:2 * n + 2, :], bank[n % 4][:, :].rearrange("p (t d) -> p t d", t=2), ACT.Copy).then_inc(v_out, 1)
                    act.wait_ge(vg_mm, 2 * n + 2)
                    nc.scalar.activation(G[:, 2 * n:2 * n + 2, :], bank[4 + n % 4][:, :].rearrange("p (t d) -> p t d", t=2), ACT.Tanh, scale=0.5).then_inc(g_act, 1)

            @block.vector
            def _(dve):
                for n in range(T // 2):
                    dve.wait_ge(g_act, n + 1)
                    g2 = G[:, 2 * n:2 * n + 2, :].rearrange("p t d -> p (t d)")
                    nc.vector.scalar_tensor_tensor(out=g2, in0=g2, scalar=1.0, in1=bank[4 + n % 4][:, :], op0=ALU.add, op1=ALU.mult).then_inc(g_out, 1)

        with nc.Block() as block:
            @block.tensor
            def _(pe):
                for r in range(4):
                    for g in range(NG):
                        if r >= 2:
                            pe.wait_ge(p_out, NG * (r - 2) + g + 1)
                        for t in range(4 * r, 4 * r + 4):
                            for b in (2 * t, 2 * t + 1):
                                h = 64 * (b % 2)
                                last = nc.tensor.matmul(bank[4 * (r % 2) + g][h:h + 64, 128 * (t % 4):128 * (t % 4) + 128],
                                                        kr[32 * g:32 * g + 32, 64 * b:64 * b + 64],
                                                        QB[32 * g:32 * g + 32, :, 64 * b:64 * b + 64], start=True, stop=True)
                        last.then_inc(s_mm, 1)

            @block.vector
            def _(dve):
                for r in range(4):
                    for g in range(NG):
                        dve.wait_ge(s_mm, NG * r + g + 1)
                        dec = decay[:, 128 * g:128 * g + 128].unsqueeze(1).to_broadcast([128, 4, 128])
                        nc.vector.tensor_tensor(P[:, 4 * r:4 * r + 4, 128 * g:128 * g + 128], bank[4 * (r % 2) + g][:, :].rearrange("p (t n) -> p t n", t=4),
                                                dec, ALU.mult).then_inc(p_out, 1)

        with nc.Block() as block:
            @block.tensor
            def _(pe):
                for n in range(T // 2):
                    for t in (2 * n, 2 * n + 1):
                        for hd in range(NH):
                            for b in (2 * t, 2 * t + 1):
                                h = 64 * (b % 2)
                                o = 256 * (t % 2) + DV * hd
                                last = nc.tensor.matmul(bank[n][h:h + 64, o:o + DV], P[h:h + 64, t, 64 * hd:64 * hd + 64], V[h:h + 64, t, DV * hd:DV * hd + DV],
                                                        start=True, stop=True)
                    last.then_inc(o_mm, 1)

            @block.scalar
            def _(act):
                sq = QB[:, :, :].rearrange("p h n -> p (h n)")
                for n in range(T // 2):
                    act.wait_ge(o_mm, n + 1)
                    nc.scalar.activation(sq[:, 512 * n:512 * n + 512], bank[n][:, :], ACT.Square).then_inc(o_sq, 1)

            @block.gpsimd
            def _(pool):
                for n in range(4):
                    pool.wait_ge(o_ms, n + 1)
                    part = slice(4 * NH * n, 4 * NH * n + 4 * NH)
                    nc.gpsimd.tensor_tensor(ms[:, 2, part], ms[:, 1, part], big_half[:, part], ALU.pow).then_inc(o_rs, 1)

            @block.vector
            def _(dve):
                link = Chain(dve, own)
                link.n = 8
                sq = QB[:, :, :].rearrange("p h n -> p (h n)")
                for n in range(4):
                    part = slice(4 * NH * n, 4 * NH * n + 4 * NH)
                    dve.wait_ge(o_sq, 2 * n + 2)
                    link(nc.vector.tensor_reduce(out=ms[:, 0, part], in_=sq[:, 1024 * n:1024 * n + 1024].rearrange("p (h d) -> p h d", d=DV), op=ALU.add, axis=AX.X))
                    nc.vector.tensor_scalar(ms[:, 1, part], ms[:, 0, part], 1.0 / DV, 1e-5, ALU.mult, ALU.add).then_inc(o_ms, 1)
                dve.wait_ge(o_mm, T // 2)
                for n in range(T // 2):
                    dve.wait_ge(o_rs, n // 2 + 1)
                    o2 = O[:, 2 * n:2 * n + 2, :].rearrange("p t d -> p (t d)")
                    rs = ms[:, 2, 2 * NH * n:2 * NH * n + 2 * NH]
                    link(nc.vector.tensor_tensor(o2.rearrange("p (h d) -> p h d", d=DV), bank[n][:, :].rearrange("p (h d) -> p h d", d=DV), bc(rs, DV), ALU.mult))
                    nc.vector.tensor_tensor(o2, o2, G[:, 2 * n:2 * n + 2, :].rearrange("p t d -> p (t d)"), ALU.mult).then_inc(o_done, 1)

        with nc.Block() as block:
            @block.tensor
            def _(pe):
                for n in range(T // 2):
                    j, q = n % 2, n // 2
                    if n >= 4:
                        pe.wait_ge(t_act, n - 3)
                    for t in range(4 * q, 4 * q + 4):
                        last = nc.tensor.transpose(bank[n % 4][:, 128 * (t % 4):128 * (t % 4) + 128], O[:, t, 128 * j:128 * j + 128], c.ident[:, :])
                    last.then_inc(t_mm, 1)
                for q in range(4):
                    pe.wait_ge(t_act, 2 * q + 2)
                    for t in range(4 * q, 4 * q + 4):
                        for j in range(2):
                            last = nc.tensor.matmul(bank[4 + q][:, 128 * (t % 4):128 * (t % 4) + 128], OT[:, j, 128 * t:128 * t + 128], wo[:, j, :], start=(j == 0), stop=(j == 1))
                    last.then_inc(y_mm, 1)

            @block.scalar
            def _(act):
                for n in range(T // 2):
                    j, q = n % 2, n // 2
                    act.wait_ge(t_mm, n + 1)
                    nc.scalar.activation(OT[:, j, 512 * q:512 * q + 512], bank[n % 4][:, :], ACT.Copy).then_inc(t_act, 1)

            @block.vector
            def _(dve):
                for q in range(4):
                    dve.wait_ge(y_mm, q + 1)
                    xs = c.X[:, 4 * q:4 * q + 4, :]
                    nc.vector.tensor_tensor(xs, bank[4 + q][:, :].rearrange("p (t d) -> p t d", d=D), xs, ALU.add).then_inc(added, 1)


def top2_moe_stage(nc, c, p):
    X8, H = 8, 256
    J, Q = H // 128, 4
    N = X8 + 1
    with ExitStack() as ctx:
        m = Memory(nc, ctx, "tm")
        w1, w2, w3 = m.sb("w1", [128, N, H]), m.sb("w2", [128, N, H]), m.sb("w3", [128, N, J, D])
        gw = m.sb("gate", [128, X8])
        lg, a1, a2, o1, o2 = (m.sb(n, [128, T, X8]) for n in ("logits", "work1", "work2", "first", "second"))
        col, wt = m.sb("col", [128, 8, T]), m.sb("weights", [128, T, N])
        rev = m.sb("rev", [128, X8])
        SIL = [m.sb(f"silu{k}", [128, 512]) for k in range(3)]
        G = [m.sb(f"hidden{k}", [128, J, 512]) for k in range(3)]
        bank = [m.ps(f"bank{q}") for q in range(8)]
        g_loaded, w_loaded, rev_set, logit, expd, shifted, weighed, up, silu, gated, down, added, own = (m.sem(n) for n in (
            "g_loaded", "w_loaded", "rev_set", "logits", "exp", "shifted", "weighed", "up", "silu", "gated", "down", "added", "dve_own"))
        with nc.Block() as block:
            @block.sync
            def _(sp):
                sp.dma_start(gw[:, :], p["gate1"]).then_inc(g_loaded, 16)
                for e in range(N):
                    src = [p[n][e] for n in ("ew1", "ew2", "ew3")] if e < X8 else [p[n] for n in ("sw1", "sw2", "sw3")]
                    sp.dma_start(w1[:, e, :], src[0]).then_inc(w_loaded, 16)
                    sp.dma_start(w2[:, e, :], src[1]).then_inc(w_loaded, 16)
                    sp.dma_start(w3[:, e, :, :], src[2].rearrange("(j i) d -> i j d", i=128)).then_inc(w_loaded, 16)
                sp.wait_ge(w_loaded, 48 * N)

            @block.gpsimd
            def _(pool):
                nc.gpsimd.iota(rev[:, :], pattern=[[-1, X8]], base=X8, channel_multiplier=0, allow_small_or_imprecise_dtypes=True).then_inc(rev_set, 1)

            @block.tensor
            def _(pe):
                pe.wait_ge(g_loaded, 16)
                for t in range(T):
                    last = nc.tensor.matmul(bank[6][:, X8 * t:X8 * t + X8], c.XNT[:, 128 * t:128 * t + 128], gw[:, :], start=True, stop=True)
                last.then_inc(logit, 1)

                def rise(e, q):
                    for j in range(J):
                        n = (e * Q + q) * J + j
                        if n >= 3:
                            pe.wait_ge(gated, n - 2)
                        for k, w in enumerate((w1, w2)):
                            last = nc.tensor.matmul(bank[2 * (n % 3) + k][:, :], w[:, e, 128 * j:128 * j + 128], c.XNT[:, 512 * q:512 * q + 512], start=True, stop=True)
                        last.then_inc(up, 1)

                def fall(e, q):
                    n = e * Q + q
                    pe.wait_ge(gated, J * n + J)
                    if n >= 2:
                        pe.wait_ge(added, n - 1)
                    if n == 0:
                        pe.wait_ge(weighed, 1)
                    for t in range(4):
                        for j in range(J):
                            last = nc.tensor.matmul(bank[6 + n % 2][:, 128 * t:128 * t + 128], G[n % 3][:, j, 128 * t:128 * t + 128], w3[:, e, j, :],
                                                    start=(j == 0), stop=(j == J - 1))
                    last.then_inc(down, 1)

                pe.wait_ge(w_loaded, 48 * N)
                before = None
                for e in range(N):
                    for q in range(Q):
                        rise(e, q)
                        if before:
                            fall(*before)
                        before = (e, q)
                fall(*before)

            @block.scalar
            def _(act):
                act.wait_ge(shifted, 1)
                nc.scalar.activation(col[:, 3, :], col[:, 2, :], ACT.Exp).then_inc(expd, 1)
                for n in range(N * Q * J):
                    act.wait_ge(up, n + 1)
                    if n >= 3:
                        act.wait_ge(gated, n - 2)
                    nc.scalar.activation(SIL[n % 3][:, :], bank[2 * (n % 3)][:, :], ACT.Silu).then_inc(silu, 1)

            @block.vector
            def _(dve):
                link = Chain(dve, own)
                rev_all = rev[:, :].unsqueeze(1).to_broadcast([128, T, X8])
                dve.wait_ge(logit, 1)
                link(nc.vector.tensor_copy(lg[:, :, :], bank[6][:, 0:T * X8].rearrange("p (t e) -> p t e", e=X8)))
                dve.wait_ge(rev_set, 1)

                def best(src, top, onehot):
                    link(nc.vector.tensor_reduce(out=col[:, top, :], in_=src, op=ALU.max, axis=AX.X))
                    link(nc.vector.tensor_tensor(a1[:, :, :], src, bc(col[:, top, :], X8), ALU.is_equal))
                    link(nc.vector.tensor_tensor(a1[:, :, :], a1[:, :, :], rev_all, ALU.mult))
                    link(nc.vector.tensor_reduce(out=col[:, 7, :], in_=a1[:, :, :], op=ALU.max, axis=AX.X))
                    link(nc.vector.tensor_tensor(onehot, a1[:, :, :], bc(col[:, 7, :], X8), ALU.is_equal))

                best(lg[:, :, :], 0, o1[:, :, :])
                link(nc.vector.tensor_scalar(a2[:, :, :], o1[:, :, :], -1e38, None, ALU.mult))
                link(nc.vector.tensor_tensor(a2[:, :, :], a2[:, :, :], lg[:, :, :], ALU.add))
                best(a2[:, :, :], 1, o2[:, :, :])
                nc.vector.tensor_tensor(col[:, 2, :], col[:, 1, :], col[:, 0, :], ALU.subtract).then_inc(shifted, 1)
                dve.wait_ge(expd, 1)
                link(nc.vector.tensor_scalar(col[:, 4, :], col[:, 3, :], 1.0, None, ALU.add))
                link(nc.vector.reciprocal(col[:, 5, :], col[:, 4, :]))
                link(nc.vector.tensor_tensor(col[:, 6, :], col[:, 5, :], col[:, 3, :], ALU.mult))
                nc.vector.tensor_tensor(o1[:, :, :], o1[:, :, :], bc(col[:, 5, :], X8), ALU.mult)
                link(nc.vector.tensor_tensor(o2[:, :, :], o2[:, :, :], bc(col[:, 6, :], X8), ALU.mult))
                nc.vector.tensor_tensor(wt[:, :, 0:X8], o1[:, :, :], o2[:, :, :], ALU.add)
                nc.vector.memset(wt[:, :, X8:N], 1.0).then_inc(weighed, 1)
                dve.wait_ge(weighed, 1)

                def gate(e, q):
                    for j in range(J):
                        n = (e * Q + q) * J + j
                        dve.wait_ge(silu, n + 1)
                        nc.vector.tensor_tensor(G[(n // J) % 3][:, j, :], bank[2 * (n % 3) + 1][:, :], SIL[n % 3][:, :], ALU.mult).then_inc(gated, 1)

                def collect(e, q):
                    n = e * Q + q
                    dve.wait_ge(down, n + 1)
                    for t in range(4):
                        last = nc.vector.scalar_tensor_tensor(out=c.X[:, 4 * q + t, :], in0=bank[6 + n % 2][:, 128 * t:128 * t + 128],
                                                              scalar=wt[:, 4 * q + t, e:e + 1], in1=c.X[:, 4 * q + t, :], op0=ALU.mult, op1=ALU.add)
                    last.then_inc(added, 1)
                    if n >= 1:
                        dve.wait_ge(added, n)

                before = []
                for e in range(N):
                    for q in range(Q):
                        gate(e, q)
                        before.append((e, q))
                        if len(before) > 2:
                            collect(*before.pop(0))
                for b in before:
                    collect(*b)


def store_stage(nc, c, out):
    with ExitStack() as ctx:
        m = Memory(nc, ctx, "st")
        stored = m.sem("stored")
        with nc.Block() as block:
            @block.sync
            def _(sp):
                sp.dma_start(out.rearrange("b s d -> (b s) d").rearrange("(t p) d -> p t d", p=128), c.X[:, :, :]).then_inc(stored, 16)
                sp.wait_ge(stored, 16)


def perceiver(nc, p, out):
    with ExitStack() as ctx:
        m = Memory(nc, ctx, "c")
        c = Common()
        c.X, c.XN, c.XNT = m.sb("X", [128, T, D]), m.sb("XN", [128, T, D]), m.sb("XNT", [128, T * 128])
        c.ident, c.ones, c.half = m.sb("ident", [128, 128]), m.sb("ones", [128, 128]), m.sb("minus_half", [128, 16])
        c.mq, c.wcT, c.whhT, c.bias = m.sb("mq", [128, 128]), m.sb("wcT", [128, 384]), m.sb("whhT", [128, 384]), m.sb("bias", [128, 5])
        setup_stage(nc, c, p)
        norm_block(nc, c, "n0")
        slot_attention_stage(nc, c, p["ctx"])
        norm_block(nc, c, "n1")
        linear_attention_stage(nc, c, p)
        norm_block(nc, c, "n2")
        capacity_moe_stage(nc, c, p)
        norm_block(nc, c, "n3")
        masked_attention_stage(nc, c, p)
        norm_block(nc, c, "n4")
        retention_stage(nc, c, p)
        norm_block(nc, c, "n5")
        top2_moe_stage(nc, c, p)
        store_stage(nc, c, out)


def rotary_tables(np):
    NH, DQ = 8, 16
    inv = 1.0 / 10000.0 ** (np.arange(0, DQ, 2, dtype=np.float32) / DQ)
    ang = (np.arange(S, dtype=np.float32)[None, :] * inv.astype(np.float32)[:, None]).astype(np.float32)
    row = np.arange(128)
    sign = np.where(row % 2 == 0, -1.0, 1.0)[:, None]
    pair = row % DQ // 2
    s = np.log2(1.0 - np.exp2(-5.0 - np.arange(NH)))
    diff = np.arange(S)[None, :] - np.arange(S)[:, None]
    dec = np.where(diff[:, None, :] >= 0, np.exp2(diff[:, None, :] * s[None, :, None]), 0.0).reshape(S, NH * S)
    head = (row[:, None] // DQ % 2 == np.arange(2)[None, :]) * float(DQ) ** -0.5
    f = np.float32
    return {"cosT": np.cos(ang)[pair].astype(f), "sinT": (np.sin(ang)[pair] * sign).astype(f),
            "decay": np.concatenate([dec, dec]).astype(f), "head": head.astype(f)}


def by_feature(w):
    return w.T.reshape(D, 2, 4, D // 8).transpose(0, 1, 3, 2).reshape(D, D)


def kernel(**inputs):
    import numpy as np
    import concourse.bacc as bacc
    from concourse.bass_utils import run_bass_kernel_spmd

    a = {k: np.asarray(v) for k, v in inputs.items()}
    swap = np.arange(128) ^ 1
    laid = {
        "x": a["x"], "ctx": a["ctx_1024"],
        "L0_xattn_Wq": a["L0_xattn_Wq"], "L0_xattn_Wk": a["L0_xattn_Wk"], "L0_xattn_Wv": a["L0_xattn_Wv"],
        "wihT": a["L0_xattn_gru_wih"].T, "whhT": a["L0_xattn_gru_whh"].T,
        "bih3": a["L0_xattn_gru_bih"].reshape(3, 128).T, "bhh3": a["L0_xattn_gru_bhh"].reshape(3, 128).T,
        "ws_col": a["L0_xattn_slot_norm_w"].reshape(128, 1), "wp_col": a["L0_xattn_input_norm_w"].reshape(128, 1),
        "wp_row": a["L0_xattn_input_norm_w"],
        "L0_attn_q_proj": a["L0_attn_q_proj"], "L0_attn_k_proj": a["L0_attn_k_proj"],
        "gateT0": a["L0_ffn_gate_weight"].T, "ln_cols": np.stack([a["L0_ffn_ln_gamma"], a["L0_ffn_ln_beta"]], 1),
        "wi": a["L0_ffn_wi"], "wo": a["L0_ffn_wo"],
        "ctxT": a["ctx_1024"].transpose(0, 2, 1), "mask": a["mask_Bx1xSxS2_if1"].reshape(B, S, M),
        "WqT1": by_feature(a["L1_xattn_Wq"]), "WkT1": by_feature(a["L1_xattn_Wk"]), "WvT1": a["L1_xattn_Wv"].T, "WoT1": a["L1_xattn_Wo"].T,
        "bo": a["L1_xattn_bo"],
        "rWq": a["L1_attn_Wq"], "rWqs": a["L1_attn_Wq"][:, swap], "rWk": a["L1_attn_Wk"], "rWks": a["L1_attn_Wk"][:, swap],
        "rWv": a["L1_attn_Wv"], "rWg": a["L1_attn_Wg"], "rWo": a["L1_attn_Wo"],
        "gcol": np.tile(a["L1_attn_g_norm_w"], 4).reshape(128, 1), **rotary_tables(np),
        "gate1": a["L1_ffn_gate_w"], "ew1": a["L1_ffn_ew1"], "ew2": a["L1_ffn_ew2"], "ew3": a["L1_ffn_ew3"],
        "sw1": a["L1_ffn_sw1"], "sw2": a["L1_ffn_sw2"], "sw3": a["L1_ffn_sw3"],

    }
    nc = bacc.Bacc("TRN2", target_bir_lowering=False, num_devices=1)
    arrays, p = {}, {}
    for name, v in laid.items():
        v = np.ascontiguousarray(v)
        arrays["in_" + name] = v
        p[name] = nc.dram_tensor("in_" + name, v.shape, mybir.dt.from_np(v.dtype), kind="ExternalInput").ap()
    out = nc.dram_tensor("out", (B, S, D), fp32, kind="ExternalOutput").ap()
    perceiver(nc, p, out)
    r = run_bass_kernel_spmd(nc, [arrays], core_ids=[0])
    return r.results[0]["out"]
```

```python
import concourse.bass as bass
from concourse import mybir
from contextlib import ExitStack

fp32 = mybir.dt.float32
bf16 = mybir.dt.bfloat16
i32 = mybir.dt.int32
ALU = mybir.AluOpType
ACT = mybir.ActivationFunctionType
AX = mybir.AxisListType

B, S, D, M = 32, 64, 128, 1601
T = B * S // 128
NC_ = -(-M // 128)
FULL = M // 128
TAIL = M - 128 * FULL
GROUPS = [(c, min(4, FULL - c)) for c in range(0, FULL, 4)]


class Chain:

    def __init__(self, eng, sem, per_turn=0, turn=None):
        self.eng, self.sem, self.n, self.per_turn, self.turn = eng, sem, 0, per_turn, turn

    def __call__(self, instruction):
        self.n += 1
        instruction.then_inc(self.sem, 1)
        at = self.n if self.turn is None else self.turn * self.per_turn + self.n
        self.eng.wait_ge(self.sem, at)

    def close(self):
        assert self.turn is None or self.n == self.per_turn, (self.n, self.per_turn)


def bc(ap, n):
    return ap.unsqueeze(2).to_broadcast([ap.shape[0], ap.shape[1], n])


class Memory:

    def __init__(self, nc, ctx, tag):
        self.nc, self.ctx, self.tag, self.sems = nc, ctx, tag, []
        ctx.callback(self.clear)

    def sb(self, name, shape, dt=fp32):
        return self.ctx.enter_context(self.nc.sbuf_tensor(f"{self.tag}_{name}", shape, dt))

    def ps(self, name, shape=(128, 512), dt=fp32):
        return self.ctx.enter_context(self.nc.psum_tensor(f"{self.tag}_{name}", list(shape), dt))

    def sem(self, name):
        self.sems.append(self.nc.alloc_semaphore(f"{self.tag}_{name}"))
        return self.sems[-1]

    def clear(self):
        self.nc.clear_and_free_semaphores(self.sems)
        self.nc.all_engine_barrier()


class NormSems:
    def __init__(self, m):
        self.centred, self.squared, self.variance = m.sem("ln_centred"), m.sem("ln_squared"), m.sem("ln_variance")
        self.rstd, self.normed, self.transposed = m.sem("ln_rstd"), m.sem("ln_normed"), m.sem("ln_transposed")
        self.xnt_dve, self.xnt_act = m.sem("ln_xnt_dve"), m.sem("ln_xnt_act")


HALVES = [slice(0, T // 2), slice(T // 2, T)]


def norm_dve(nc, dve, link, X, XN, work, st, s, eps):
    for h in HALVES:
        link(nc.vector.tensor_reduce(out=st[:, 0, h], in_=X[:, h, :], op=ALU.add, axis=AX.X))
        link(nc.vector.tensor_scalar(st[:, 1, h], st[:, 0, h], -1.0 / D, None, ALU.mult))
        nc.vector.tensor_tensor(XN[:, h, :], X[:, h, :], bc(st[:, 1, h], D), ALU.add).then_inc(s.centred, 1)
    for n, h in enumerate(HALVES):
        dve.wait_ge(s.squared, n + 1)
        link(nc.vector.tensor_reduce(out=st[:, 2, h], in_=work[:, h, :], op=ALU.add, axis=AX.X))
        nc.vector.tensor_scalar(st[:, 3, h], st[:, 2, h], 1.0 / D, eps, ALU.mult, ALU.add).then_inc(s.variance, 1)
    for n, h in enumerate(HALVES):
        dve.wait_ge(s.rstd, n + 1)
        nc.vector.tensor_tensor(XN[:, h, :], XN[:, h, :], bc(st[:, 4, h], D), ALU.mult).then_inc(s.normed, 1)


def norm_act(nc, act, XN, work, s):
    for n, h in enumerate(HALVES):
        act.wait_ge(s.centred, n + 1)
        nc.scalar.activation(work[:, h, :], XN[:, h, :], ACT.Square).then_inc(s.squared, 1)


def norm_pool(nc, pool, st, half, s):
    for n, h in enumerate(HALVES):
        pool.wait_ge(s.variance, n + 1)
        nc.gpsimd.tensor_tensor(st[:, 4, h], st[:, 3, h], half[:, h], ALU.pow).then_inc(s.rstd, 1)


def transpose_pe(nc, pe, XN, banks, ident, s):
    for q in range(T // 4):
        pe.wait_ge(s.normed, q // 2 + 1)
        for j in range(4):
            last = nc.tensor.transpose(banks[q][:, 128 * j:128 * j + 128], XN[:, 4 * q + j, :], ident[:, :])
        last.then_inc(s.transposed, 1)


def transpose_out_dve(nc, dve, XNT, banks, s):
    for q in range(0, T // 4, 2):
        dve.wait_ge(s.transposed, q + 1)
        nc.vector.tensor_copy(XNT[:, 512 * q:512 * q + 512], banks[q][:, :]).then_inc(s.xnt_dve, 1)


def transpose_out_act(nc, act, XNT, banks, s):
    for q in range(1, T // 4, 2):
        act.wait_ge(s.transposed, q + 1)
        nc.scalar.activation(XNT[:, 512 * q:512 * q + 512], banks[q][:, :], ACT.Copy).then_inc(s.xnt_act, 1)


def norm_block(nc, c, tag, eps=1e-5, x_out=False):
    with ExitStack() as ctx:
        m = Memory(nc, ctx, tag)
        work, st = m.sb("work", [128, T, D]), m.sb("stats", [128, 5, T])
        banks = [m.ps(f"bank{q}") for q in range(T // 4)]
        s, own = NormSems(m), m.sem("dve_own")
        with nc.Block() as block:
            @block.vector
            def _(dve):
                norm_dve(nc, dve, Chain(dve, own), c.X, c.XN, work, st, s, eps)
                transpose_out_dve(nc, dve, c.XNT, banks, s)

            @block.scalar
            def _(act):
                norm_act(nc, act, c.XN, work, s)
                transpose_out_act(nc, act, c.XNT, banks, s)

            @block.gpsimd
            def _(pool):
                norm_pool(nc, pool, st, c.half, s)

            @block.tensor
            def _(pe):
                transpose_pe(nc, pe, c.XN, banks, c.ident, s)


class Common:
    pass


def setup_stage(nc, c, p):
    with ExitStack() as ctx:
        m = Memory(nc, ctx, "su")
        wq, wk, wv = m.sb("wq", [128, 128]), m.sb("wk", [128, 128]), m.sb("wv", [128, 128])
        wpb, wkw = m.sb("wp_bc", [128, 128]), m.sb("wk_scaled", [128, 128])
        wih = m.sb("wihT", [128, 384])
        bih, bhh, ws, wp = m.sb("bih", [128, 3]), m.sb("bhh", [128, 3]), m.sb("ws", [128, 1]), m.sb("wp", [128, 1])
        mq_ps, wc_ps = m.ps("mq"), m.ps("wc")
        loaded, x_loaded, zeroed, wk_scaled, folded = (m.sem(n) for n in ("loaded", "x_loaded", "zeroed", "wk_scaled", "folded"))
        own = m.sem("dve_own")
        loads = [(wq, p["L0_xattn_Wq"]), (wk, p["L0_xattn_Wk"]), (wv, p["L0_xattn_Wv"]), (wih, p["wihT"]),
                 (c.whhT, p["whhT"]), (bih, p["bih3"]), (bhh, p["bhh3"]), (ws, p["ws_col"]), (wp, p["wp_col"])]
        with nc.Block() as block:
            @block.sync
            def _(sp):
                sp.dma_start(c.X[:, :, :], p["x"].rearrange("b s d -> (b s) d").rearrange("(t p) d -> p t d", p=128)).then_inc(x_loaded, 16)
                for dst, src in loads:
                    sp.dma_start(dst[:, :], src).then_inc(loaded, 16)
                sp.dma_start(wpb[:, :], p["wp_row"].partition_broadcast(128)).then_inc(loaded, 16)
                sp.wait_ge(x_loaded, 16)
                sp.wait_ge(loaded, 16 * (len(loads) + 1))

            @block.gpsimd
            def _(pool):
                nc.gpsimd.memset(c.ones[:, :], 1.0)
                nc.gpsimd.memset(c.half[:, :], -0.5)
                nc.gpsimd.memset(c.ident[:, :], 0.0).then_inc(zeroed, 1)
                pool.wait_ge(zeroed, 1)
                nc.gpsimd.affine_select(out=c.ident[:, :], in_=c.ident[:, :], compare_op=ALU.not_equal, fill=1.0,
                                        base=0, pattern=[[-1, 128]], channel_multiplier=1).then_inc(zeroed, 1)
                pool.wait_ge(zeroed, 2)

            @block.vector
            def _(dve):
                link = Chain(dve, own)
                dve.wait_ge(loaded, 16 * (len(loads) + 1))
                nc.vector.tensor_tensor(wkw[:, :], wk[:, :], wpb[:, :], ALU.mult).then_inc(wk_scaled, 1)
                link(nc.vector.tensor_tensor(c.bias[:, 0:3], bih[:, :], bhh[:, :], ALU.add))
                link(nc.vector.tensor_scalar(c.bias[:, 0:2], c.bias[:, 0:2], 0.5, None, ALU.mult))
                nc.vector.tensor_copy(c.bias[:, 3:4], bih[:, 2:3])
                nc.vector.tensor_copy(c.bias[:, 4:5], bhh[:, 2:3])
                dve.wait_ge(folded, 2)
                nc.vector.tensor_scalar(c.mq[:, :], mq_ps[:, 0:128], ws[:, 0:1], float(D) ** -0.5, ALU.mult, ALU.mult)
                link(nc.vector.tensor_scalar(c.wcT[:, :], wc_ps[:, 0:384], wp[:, 0:1], None, ALU.mult))

            @block.tensor
            def _(pe):
                pe.wait_ge(wk_scaled, 1)
                nc.tensor.matmul(mq_ps[:, 0:128], wq[:, :], wkw[:, :], start=True, stop=True).then_inc(folded, 1)
                nc.tensor.matmul(wc_ps[:, 0:384], wv[:, :], wih[:, :], start=True, stop=True).then_inc(folded, 1)


def slot_attention_stage(nc, c, ctx_dram):
    R, L, NB = 3, 4, 2
    STEPS = R * L
    TURNS = B // (L * NB)
    EPS = 1e-6
    SUM, GRU = 1, 2
    with ExitStack() as ctx:
        m = Memory(nc, ctx, "sa")
        pn = [[m.sb(f"pn{l}{b}", [128, NC_, D + 1]) for b in range(NB)] for l in range(L)]
        pnT = [[m.sb(f"pnT{l}{b}", [128, NC_ * 128]) for b in range(NB)] for l in range(L)]
        e = [[m.sb(f"e{l}{b}", [128, NC_, S]) for b in range(NB)] for l in range(L)]
        ms = [[m.sb(f"ms{l}{b}", [128, 3, NC_]) for b in range(NB)] for l in range(L)]
        col = [[m.sb(f"col{l}{b}", [128, 3, NC_]) for b in range(NB)] for l in range(L)]
        slT, slsq = ([m.sb(f"{n}{l}", [128, 128]) for l in range(L)] for n in ("slotsT", "slots_sq"))
        sc = [m.sb(f"sc{l}", [128, 4]) for l in range(L)]
        qn, un, uT, nn = (m.sb(n, [128, 128]) for n in ("qn", "un", "uT", "nn"))
        qT = [m.sb(f"qT{k}", [128, 128]) for k in range(2)]
        tr, hn = m.sb("tr", [128, 2, 128]), m.sb("hn", [128, 2, 128])
        Sb = [m.ps(f"scores{b}", [128, 1024]) for b in range(NB)]
        QB, G = m.ps("query"), m.ps("gates")
        U = [m.ps(f"u{k}") for k in range(2)]

        squared, meansq, rstd, normed, turned, turned_act, turned_dve, slots_in, out_turned, added = (m.sem(n) for n in (
            "ctx_squared", "ctx_meansq", "ctx_rstd", "ctx_normed", "ctxT_psum", "ctxT_act", "ctxT_dve",
            "slots_in", "out_turned", "x_added"))
        (sl_sq, q_nat, sl_meansq, sl_rstd, q_scaled, q_turned, q_ready, scored, centred, exped, slot_sum, attn,
         summed, u_inv, u_scaled, u_turned, u_ready, gates, rz, n_in, n_out, slots) = (m.sem(n) for n in (
            "slots_squared", "q_natural", "slots_meansq", "slots_rstd", "q_scaled", "q_turned", "q_ready", "scored", "centred",
            "exped", "slot_sum_inv", "attn_ready", "u_summed", "u_inv", "u_scaled", "u_turned", "u_ready", "gates", "rz",
            "n_in", "n_out", "slots_new"))
        lane_loaded = [m.sem(f"ctx_loaded{l}") for l in range(L)]
        zeroed, own_first, own, own_last = m.sem("zeroed"), m.sem("dve_own_first"), m.sem("dve_own"), m.sem("dve_own_last")

        def none(x):
            return isinstance(x, int) and x <= 0

        with nc.Block() as block:
            @block.sync
            def _(sp):
                def load(i, l):
                    for b in range(NB):
                        rows = ctx_dram[bass.ds(NB * L * i + NB * l + b, 1), :, :].rearrange("a m d -> (a m) d")
                        sp.dma_start(pn[l][b][:, 0:FULL, 0:D], rows[0:128 * FULL, :].rearrange("(p c) d -> p c d", p=128)).then_inc(lane_loaded[l], 16)
                        sp.dma_start(pn[l][b][0:TAIL, FULL, 0:D], rows[128 * FULL:M, :]).then_inc(lane_loaded[l], 16)

                sp.wait_ge(zeroed, 1)
                for l in range(L):
                    load(0, l)
                with sp.Fori(0, TURNS - 1) as i:
                    for l in range(L):
                        sp.wait_ge(summed, STEPS * i + STEPS - L + l + 1)
                        load(i + 1, l)

            @block.gpsimd
            def _(pool):
                def prepare(p, l):
                    for b in range(NB):
                        pool.wait_ge(meansq, NB * p + b + 1)
                        nc.gpsimd.tensor_tensor(ms[l][b][:, 2, :], ms[l][b][:, 1, :], c.half[:, 0:NC_], ALU.pow).then_inc(rstd, 1)
                        pool.wait_ge(rstd, NB * p + b + 1)
                        nc.gpsimd.tensor_tensor(pn[l][b][:, :, 0:D], pn[l][b][:, :, 0:D], bc(ms[l][b][:, 2, :], D), ALU.mult).then_inc(normed, 1)

                def query(s, l):
                    pool.wait_ge(sl_meansq, s + 1)
                    nc.gpsimd.tensor_tensor(sc[l][:, 1:2], sc[l][:, 0:1], c.half[:, 0:1], ALU.pow).then_inc(sl_rstd, 1)

                def step(i, n, last):
                    s, l = STEPS * i + n, n % L
                    if not (last and n == STEPS - 1):
                        query(s + 1, (n + 1) % L)
                    for b in range(NB):
                        pool.wait_ge(slot_sum, NB * s + b + 1)
                        nc.gpsimd.tensor_tensor(e[l][b][:, :, :], e[l][b][:, :, :], bc(col[l][b][:, 2, :], S), ALU.mult).then_inc(attn, 1)
                    if n < 2:
                        prepare(L * i + n + 2, n + 2)
                    elif n >= STEPS - 2 and not last:
                        prepare(L * (i + 1) + n - (STEPS - 2), n - (STEPS - 2))

                query(0, 0)
                prepare(0, 0)
                prepare(1, 1)
                for n in range(STEPS):
                    step(0, n, False)
                with pool.Fori(1, TURNS - 1) as i:
                    for n in range(STEPS):
                        step(i, n, False)
                for n in range(STEPS):
                    step(TURNS - 1, n, True)

            @block.scalar
            def _(act):
                def prepare(p, i, l):
                    act.wait_ge(lane_loaded[l], 32 * NB * (i + 1))
                    for b in range(NB):
                        nc.scalar.activation(pnT[l][b][:, :].rearrange("p (c d) -> p c d", d=D), pn[l][b][:, :, 0:D], ACT.Square).then_inc(squared, 1)

                def turn_rows(p, l):
                    for b in range(NB):
                        for q in (0, 2):
                            act.wait_ge(turned, 4 * (NB * p + b) + q + 1)
                            nc.scalar.activation(pnT[l][b][:, 512 * q:512 * q + 512], Sb[q // 2][:, 0:512], ACT.Copy).then_inc(turned_act, 1)

                def square(l):
                    nc.scalar.activation(slsq[l][:, :], slT[l][:, :], ACT.Square).then_inc(sl_sq, 1)

                def scale_q(s, l):
                    act.wait_ge(sl_rstd, s + 1)
                    nc.scalar.activation(qn[:, :], QB[:, 0:128], ACT.Copy, scale=sc[l][:, 1:2]).then_inc(q_scaled, 1)

                def copy_q(s, n):
                    act.wait_ge(q_turned, s + 1)
                    nc.scalar.activation(qT[n % 2][:, :], QB[:, 0:128], ACT.Copy).then_inc(q_ready, 1)

                def exp(s, l, b):
                    act.wait_ge(centred, NB * s + b + 1)
                    nc.scalar.activation(e[l][b][:, :, :], e[l][b][:, :, :], ACT.Exp).then_inc(exped, 1)

                def step(i, n, last, scores=True):
                    s, l, g = STEPS * i + n, n % L, (n - GRU) % L
                    k = s - GRU + 1
                    gru = not none(k)
                    ahead = scores and not (last and n == STEPS - 1)
                    if n < L and scores:
                        turn_rows(L * i + l, l)
                    if ahead and (n + 1) % STEPS < L:
                        act.wait_ge(slots_in, L * i + (n + 2 if n < L else L + 1))
                        square((n + 1) % L)
                    if gru:
                        act.wait_ge(u_inv, k)
                        nc.scalar.activation(un[:, :], U[g % 2][:, 0:D], ACT.Copy, scale=sc[g][:, 3:4]).then_inc(u_scaled, 1)
                        act.wait_ge(u_turned, k)
                        nc.scalar.activation(uT[:, :], U[g % 2][:, 0:128], ACT.Copy).then_inc(u_ready, 1)
                    if scores:
                        exp(s, l, 0)
                    if ahead:
                        scale_q(s + 1, (n + 1) % L)
                    if gru:
                        act.wait_ge(gates, k)
                        if not none(k - 1):
                            act.wait_ge(slots, k - 1)
                        nc.scalar.activation(tr[:, 0, :], G[:, 0:128], ACT.Tanh, bias=c.bias[:, 0:1], scale=0.5)
                        nc.scalar.activation(tr[:, 1, :], G[:, 128:256], ACT.Tanh, bias=c.bias[:, 1:2], scale=0.5).then_inc(rz, 1)
                    if scores:
                        exp(s, l, 1)
                    if ahead:
                        copy_q(s + 1, n + 1)
                    if gru:
                        act.wait_ge(n_in, k)
                        nc.scalar.activation(nn[:, :], hn[:, 1, :], ACT.Tanh, bias=c.bias[:, 3:4]).then_inc(n_out, 1)
                    if gru and (n - GRU) % STEPS < STEPS - L:
                        act.wait_ge(slots, k)
                        square(g)
                    if scores and n < 2:
                        prepare(L * i + n + 2, i, n + 2)
                    elif scores and n >= STEPS - 2 and not last:
                        prepare(L * (i + 1) + n - (STEPS - 2), i + 1, n - (STEPS - 2))

                prepare(0, 0, 0)
                act.wait_ge(slots_in, 1)
                square(0)
                scale_q(0, 0)
                copy_q(0, 0)
                prepare(1, 0, 1)
                for n in range(STEPS):
                    step(0, n, False)
                with act.Fori(1, TURNS - 1) as i:
                    for n in range(STEPS):
                        step(i, n, False)
                for n in range(STEPS):
                    step(TURNS - 1, n, True)
                for n in range(GRU):
                    step(TURNS, n, True, scores=False)

            @block.vector
            def _(dve):
                def prepare(p, l, link):
                    for b in range(NB):
                        dve.wait_ge(squared, NB * p + b + 1)
                        link(nc.vector.tensor_reduce(out=ms[l][b][:, 0, :], in_=pnT[l][b][:, :].rearrange("p (c d) -> p c d", d=D), op=ALU.add, axis=AX.X))
                        nc.vector.tensor_scalar(ms[l][b][:, 1, :], ms[l][b][:, 0, :], 1.0 / D, EPS, ALU.mult, ALU.add).then_inc(meansq, 1)

                def turn_rows(p, l):
                    for b in range(NB):
                        for q in (1, 3):
                            w = min(512, NC_ * 128 - 512 * q)
                            dve.wait_ge(turned, 4 * (NB * p + b) + q + 1)
                            nc.vector.tensor_copy(pnT[l][b][:, 512 * q:512 * q + w], Sb[q // 2][:, 512:512 + w]).then_inc(turned_dve, 1)

                def start(i, l):
                    nc.vector.tensor_copy(slT[l][:, :], c.XNT[:, bass.ds(128 * (L * i + l), 128)]).then_inc(slots_in, 1)

                def centre(s, l, b, link):
                    view = Sb[b][:, 0:NC_ * S].rearrange("p (c s) -> p c s", s=S)
                    dve.wait_ge(scored, NB * s + b + 1)
                    link(nc.vector.tensor_reduce(out=col[l][b][:, 0, :], in_=view, op=ALU.max, axis=AX.X))
                    nc.vector.tensor_tensor(e[l][b][:, :, :], view, bc(col[l][b][:, 0, :], S), ALU.subtract).then_inc(centred, 1)

                def total(s, l, b, link):
                    dve.wait_ge(exped, NB * s + b + 1)
                    link(nc.vector.tensor_reduce(out=col[l][b][:, 1, :], in_=e[l][b][:, :, :], op=ALU.add, axis=AX.X))
                    nc.vector.reciprocal(col[l][b][:, 2, :], col[l][b][:, 1, :]).then_inc(slot_sum, 1)

                def finish(i, n):
                    tile = L * i + (n - 1 - GRU) % L - (0 if n == STEPS - 1 else L)
                    dve.wait_ge(out_turned, tile + 1)
                    xs = c.X[:, bass.ds(tile, 1), :]
                    nc.vector.tensor_tensor(xs, QB[:, 256:384].unsqueeze(1), xs, ALU.add).then_inc(added, 1)

                def query(s, l):
                    dve.wait_ge(q_nat, s + 1)
                    nc.vector.tensor_scalar(sc[l][:, 0:1], QB[:, 128:129], 1.0 / D, EPS, ALU.mult, ALU.add).then_inc(sl_meansq, 1)

                def step(i, n, last, link, scores=True):
                    s, l, g = STEPS * i + n, n % L, (n - GRU) % L
                    k = s - GRU + 1
                    gru = not none(k)
                    ahead = scores and not (last and n == STEPS - 1)
                    if n < L and scores:
                        turn_rows(L * i + l, l)
                    if (n - 1 - GRU) % STEPS >= STEPS - L and (n == STEPS - 1 or not none(s - STEPS + 1)):
                        finish(i, n)
                    if ahead and (n + 1) % STEPS < L:
                        start(i if n < L else i + 1, (n + 1) % L)
                    if gru:
                        dve.wait_ge(summed, k)
                        link(nc.vector.tensor_scalar(sc[g][:, 2:3], U[g % 2][:, D:D + 1], EPS, None, ALU.add))
                        nc.vector.reciprocal(sc[g][:, 3:4], sc[g][:, 2:3]).then_inc(u_inv, 1)
                    if scores:
                        centre(s, l, 0, link)
                    if ahead:
                        query(s + 1, (n + 1) % L)
                    if scores:
                        centre(s, l, 1, link)
                    if gru:
                        dve.wait_ge(rz, k)
                        link(nc.vector.tensor_scalar(hn[:, 0, :], G[:, 384:512], c.bias[:, 4:5], 0.5, ALU.add, ALU.mult))
                        link(nc.vector.scalar_tensor_tensor(out=hn[:, 0, :], in0=tr[:, 0, :], scalar=1.0, in1=hn[:, 0, :], op0=ALU.add, op1=ALU.mult))
                        nc.vector.tensor_tensor(hn[:, 1, :], G[:, 256:384], hn[:, 0, :], ALU.add).then_inc(n_in, 1)
                    if scores:
                        total(s, l, 0, link)
                    if gru:
                        dve.wait_ge(n_out, k)
                        link(nc.vector.tensor_tensor(slT[g][:, :], slT[g][:, :], nn[:, :], ALU.subtract))
                        link(nc.vector.scalar_tensor_tensor(out=hn[:, 0, :], in0=tr[:, 1, :], scalar=1.0, in1=slT[g][:, :], op0=ALU.add, op1=ALU.mult))
                        nc.vector.scalar_tensor_tensor(out=slT[g][:, :], in0=hn[:, 0, :], scalar=0.5, in1=nn[:, :],
                                                       op0=ALU.mult, op1=ALU.add).then_inc(slots, 1)
                    if scores:
                        total(s, l, 1, link)
                    if scores and n < 2:
                        prepare(L * i + n + 2, n + 2, link)
                    elif scores and n >= STEPS - 2 and not last:
                        prepare(L * (i + 1) + n - (STEPS - 2), n - (STEPS - 2), link)

                for l in range(L):
                    for b in range(NB):
                        nc.vector.memset(pn[l][b][:, FULL, 0:D], 0.0)
                        last = nc.vector.memset(pn[l][b][:, :, D:D + 1], 1.0)
                last.then_inc(zeroed, 1)
                link = Chain(dve, own_first)
                start(0, 0)
                query(0, 0)
                prepare(0, 0, link)
                prepare(1, 1, link)
                for n in range(STEPS):
                    step(0, n, False, link)
                OWN = L * NB + STEPS * (1 + 2 * NB + 2 + 2)
                with dve.Fori(1, TURNS - 1) as i:
                    link = Chain(dve, own, OWN, i - 1)
                    for n in range(STEPS):
                        step(i, n, False, link)
                    link.close()
                link = Chain(dve, own_last)
                for n in range(STEPS):
                    step(TURNS - 1, n, True, link)
                for n in range(GRU):
                    step(TURNS, n, True, link, scores=False)
                finish(TURNS, GRU)

            @block.tensor
            def _(pe):
                def turn_rows(p, l, s):
                    if not none(s):
                        pe.wait_ge(centred, NB * s)
                    for b in range(NB):
                        if b and not none(s):
                            sums(s, (l - SUM) % L)
                        pe.wait_ge(normed, NB * p + b + 1)
                        for q in range(4):
                            if b:
                                pe.wait_ge((turned_act, turned_dve)[q % 2], 2 * (NB * p + b - 1) + q // 2 + 1)
                            for ch in range(4 * q, min(4 * q + 4, NC_)):
                                o = 128 * (ch % 8)
                                last = nc.tensor.transpose(Sb[q // 2][:, o:o + 128], pn[l][b][:, ch, 0:D], c.ident[:, :])
                            last.then_inc(turned, 1)

                def score(s, l, b, n):
                    if not none(NB * s + b - 1):
                        pe.wait_ge(centred, NB * s + b - 1)
                    for ch in range(NC_):
                        last = nc.tensor.matmul(Sb[b][:, S * ch:S * ch + S], pnT[l][b][:, 128 * ch:128 * ch + 128],
                                                qT[n % 2][:, S * b:S * b + S], start=True, stop=True)
                    last.then_inc(scored, 1)

                def sums(s, p):
                    pe.wait_ge(attn, NB * s)
                    for ch in range(NC_):
                        h = 128 if ch < FULL else TAIL
                        for b in range(NB):
                            last = nc.tensor.matmul(U[p % 2][S * b:S * b + S, 0:D + 1], e[p][b][0:h, ch, :],
                                                    pn[p][b][0:h, ch, :], start=(ch == 0), stop=(ch == NC_ - 1))
                    last.then_inc(summed, 1)

                def gate(k, g):
                    pe.wait_ge(u_ready, k)
                    if not none(k - 1):
                        pe.wait_ge(n_in, k - 1)
                    for out, f, parts in ((0, 0, "xh"), (1, 1, "xh"), (2, 2, "x"), (3, 2, "h")):
                        for part in parts:
                            w, v = (c.wcT, uT) if part == "x" else (c.whhT, slT[g])
                            last = nc.tensor.matmul(G[:, 128 * out:128 * out + 128], w[:, 128 * f:128 * f + 128], v[:, :], start=(part == parts[0]), stop=(part == parts[-1]))
                    last.then_inc(gates, 1)

                def query(i, n):
                    s, l = STEPS * i + n, n % L
                    pe.wait_ge(sl_sq, s + 1)
                    nc.tensor.matmul(QB[:, 128:129], slsq[l][:, :], c.ones[:, 0:1], start=True, stop=True)
                    nc.tensor.matmul(QB[:, 0:128], slT[l][:, :], c.mq[:, :], start=True, stop=True).then_inc(q_nat, 1)

                def flip_q(s):
                    pe.wait_ge(q_scaled, s + 1)
                    nc.tensor.transpose(QB[:, 0:128], qn[:, :], c.ident[:, :]).then_inc(q_turned, 1)

                def step(i, n, scores=True, sum_before=True, ahead=True):
                    s, l, g = STEPS * i + n, n % L, (n - GRU) % L
                    k = s - GRU + 1
                    gru = not none(k)
                    if n < L and scores:
                        turn_rows(L * i + l, l, s)
                    if scores:
                        pe.wait_ge(q_ready, s + 1)
                        if n < L:
                            pe.wait_ge(turned_act, 2 * NB * (L * i + l + 1))
                            pe.wait_ge(turned_dve, 2 * NB * (L * i + l + 1))
                        score(s, l, 0, n)
                    if gru:
                        pe.wait_ge(u_scaled, k)
                        nc.tensor.transpose(U[g % 2][:, 0:128], un[:, :], c.ident[:, :]).then_inc(u_turned, 1)
                    if (n - 1 - GRU) % STEPS >= STEPS - L and (n == STEPS - 1 or not none(s - STEPS + 1)):
                        pe.wait_ge(added, L * i + (n - 1 - GRU) % L + (1 if n == STEPS - 1 else 1 - L))
                    if ahead:
                        query(i, n + 1)
                    if scores:
                        score(s, l, 1, n)
                    if gru:
                        gate(k, g)
                    if ahead:
                        flip_q(s + 1)
                    if sum_before and (n >= L or not scores):
                        sums(s, (n - SUM) % L)
                    if gru and (n - GRU) % STEPS >= STEPS - L:
                        pe.wait_ge(slots, k)
                        if ahead:
                            pe.wait_ge(q_ready, s + 2)
                        nc.tensor.transpose(QB[:, 256:384], slT[g][:, :], c.ident[:, :]).then_inc(out_turned, 1)

                query(0, 0)
                flip_q(0)
                for n in range(STEPS):
                    step(0, n)
                with pe.Fori(1, TURNS - 1) as i:
                    for n in range(STEPS):
                        step(i, n)
                for n in range(STEPS):
                    step(TURNS - 1, n, ahead=n < STEPS - 1)
                step(TURNS, 0, scores=False, ahead=False)
                step(TURNS, 1, scores=False, sum_before=False, ahead=False)


def linear_attention_stage(nc, c, p):
    E = 32
    with ExitStack() as ctx:
        m = Memory(nc, ctx, "la")
        wq, wk = m.sb("wq", [128, E]), m.sb("wk", [128, E])
        qe, ke, kv = m.sb("q_expT", [E, T * 128]), m.sb("k_exp", [128, T, E]), m.sb("kv", [E, B, D + 1])
        z = m.sb("z", [128, 2, T])
        bank = [m.ps(f"bank{q}") for q in range(8)]
        loaded, q_mm, q_exp, k_mm, k_exp, kv_mm, kv_out, num_mm, ones_set, done = (m.sem(n) for n in (
            "loaded", "q_projected", "q_exp", "k_projected", "k_exp", "kv_summed", "kv_copied", "numerators", "ones_set", "added"))
        own = m.sem("dve_own")
        PER = 3
        SETS = [(t, min(PER, T - t)) for t in range(0, T, PER)]
        with nc.Block() as block:
            @block.sync
            def _(sp):
                sp.dma_start(wq[:, :], p["L0_attn_q_proj"]).then_inc(loaded, 16)
                sp.dma_start(wk[:, :], p["L0_attn_k_proj"]).then_inc(loaded, 16)

            @block.tensor
            def _(pe):
                pe.wait_ge(loaded, 32)
                for t in range(T):
                    last = nc.tensor.matmul(bank[4][:, E * t:E * t + E], c.XNT[:, 128 * t:128 * t + 128], wk[:, :], start=True, stop=True)
                last.then_inc(k_mm, 1)
                for q in range(4):
                    nc.tensor.matmul(bank[q][0:E, :], wq[:, :], c.XNT[:, 512 * q:512 * q + 512], start=True, stop=True).then_inc(q_mm, 1)
                pe.wait_ge(k_exp, 1)
                for b in range(B):
                    q, h, o = 2 * (b // 8) + b % 2, 64 * (b % 2), 128 * (b // 2 % 4)
                    if q < 4 and b % 8 < 2:
                        pe.wait_ge(q_exp, q + 1)
                    last = nc.tensor.matmul(bank[q][0:E, o:o + 128], ke[h:h + 64, b // 2, :],
                                            c.XN[h:h + 64, b // 2, :], start=True, stop=True)
                    if b % 8 >= 6:
                        last.then_inc(kv_mm, 1)
                for n, (t0, k) in enumerate(SETS):
                    pe.wait_ge(kv_out, 9)
                    for t in range(t0, t0 + k):
                        for b in (2 * t, 2 * t + 1):
                            h, o = 64 * (b % 2), (D + 1) * (t - t0)
                            last = nc.tensor.matmul(bank[n][h:h + 64, o:o + D + 1], qe[:, 64 * b:64 * b + 64], kv[:, b, :], start=True, stop=True)
                    last.then_inc(num_mm, 1)

            @block.scalar
            def _(act):
                act.wait_ge(k_mm, 1)
                nc.scalar.activation(ke[:, :, :], bank[4][:, 0:T * E].rearrange("p (t e) -> p t e", e=E), ACT.Exp).then_inc(k_exp, 1)
                for q in range(4):
                    act.wait_ge(q_mm, q + 1)
                    nc.scalar.activation(qe[:, 512 * q:512 * q + 512], bank[q][0:E, :], ACT.Exp).then_inc(q_exp, 1)

            @block.vector
            def _(dve):
                link = Chain(dve, own)
                nc.vector.memset(kv[:, :, D:D + 1], 1.0).then_inc(kv_out, 1)
                for q in range(8):
                    dve.wait_ge(kv_mm, q + 1)
                    b0 = 8 * (q // 2) + q % 2
                    nc.vector.tensor_copy(kv[:, b0:b0 + 7:2, 0:D], bank[q][0:E, :].rearrange("p (b d) -> p b d", d=D)).then_inc(kv_out, 1)
                for n, (t0, k) in enumerate(SETS):
                    dve.wait_ge(num_mm, n + 1)
                    sums = bank[n][:, 0:k * (D + 1)].rearrange("p (t d) -> p t d", d=D + 1)[:, :, D]
                    link(nc.vector.tensor_scalar(z[:, 0, t0:t0 + k], sums, 1e-8, None, ALU.add))
                    link(nc.vector.reciprocal(z[:, 1, t0:t0 + k], z[:, 0, t0:t0 + k]))
                    for t in range(t0, t0 + k):
                        o = (D + 1) * (t - t0)
                        last = nc.vector.scalar_tensor_tensor(out=c.X[:, t, :], in0=bank[n][:, o:o + D], scalar=z[:, 1, t:t + 1],
                                                              in1=c.X[:, t, :], op0=ALU.mult, op1=ALU.add)
                last.then_inc(done, 1)


def capacity_moe_stage(nc, c, p):
    X8, I, CAP = 8, 512, 256
    J, SL = I // 128, CAP // 128
    TRASH = X8 * CAP
    with ExitStack() as ctx:
        m = Memory(nc, ctx, "cm")
        TK, DS, DT = m.sb("tokens", [128, T, D]), m.sb("dispatched", [128, T, D]), m.sb("dispatchedT", [128, T * 128])
        wi, wo = m.sb("wi", [128, X8, I]), m.sb("wo", [128, X8, J, D])
        H = [m.sb(f"hidden{k}", [128, J, CAP]) for k in range(2)]
        gw, ln = m.sb("gateT", [128, X8]), m.sb("ln", [128, 2])
        tokT = m.sb("tokT", [128, T * 128])
        before, rev, offs = m.sb("before", [128, 128]), m.sb("rev", [128, X8]), m.sb("offs", [128, X8])
        lg, w1, w2, oh = (m.sb(n, [128, T, X8]) for n in ("logits", "work1", "work2", "onehot"))
        col = m.sb("col", [128, 8, T])
        idx, gidx = m.sb("idx", [128, T], i32), m.sb("gather_idx", [128, T], i32)
        zrow, trash = m.sb("zrow", [128, D]), m.sb("trash_row", [128, T])
        st, work = m.sb("stats", [128, 5, T]), DS
        bank = [m.ps(f"bank{q}") for q in range(8)]
        slots_dram = nc.dram_tensor("slots_in", (TRASH + 128 * T, D), fp32, kind="Internal").ap()
        eout_dram = nc.dram_tensor("slots_out", (TRASH + 128, D), fp32, kind="Internal").ap()
        s, own = NormSems(m), m.sem("dve_own")
        loaded, w_loaded, const, zero, zeroed, logit, expd, chose, ranked, routed = (m.sem(n) for n in (
            "loaded", "w_loaded", "const", "zero", "zeroed", "logits", "exp", "chosen", "ranks", "routed"))
        sent, back, turned, dt_out, up, act_out, down, eo, eo_out, got, added, trashed, dve_up = (m.sem(n) for n in (
            "sent", "back", "turned", "dispT", "up", "hidden", "down", "expert_rows", "stored", "gathered", "added", "trashed", "dve_up"))
        with nc.Block() as block:
            @block.sync
            def _(sp):
                sp.dma_start(gw[:, :], p["gateT0"]).then_inc(loaded, 16)
                sp.dma_start(ln[:, :], p["ln_cols"]).then_inc(loaded, 16)
                sp.dma_start(wi[:, :, :], p["wi"].rearrange("e h i -> h e i")).then_inc(w_loaded, 16)
                sp.dma_start(wo[:, :, :, :], p["wo"].rearrange("e (j i) h -> i e j h", i=128)).then_inc(w_loaded, 16)
                sp.wait_ge(zero, 1)
                sp.dma_start(slots_dram[0:TRASH, :].rearrange("(t p) d -> p t d", p=128), TK[:, :, :]).then_inc(zeroed, 16)
                sp.dma_start(eout_dram[TRASH:TRASH + 128, :], zrow[:, :]).then_inc(zeroed, 16)
                sp.wait_ge(sent, 16 * T)
                sp.dma_start(DS[:, :, :], slots_dram[0:TRASH, :].rearrange("(t p) d -> p t d", p=128)).then_inc(back, 16)
                for e in range(X8):
                    sp.wait_ge(eo, e + 1)
                    rows = eout_dram[CAP * e:CAP * e + CAP, :].rearrange("(t p) d -> p t d", p=128)
                    sp.dma_start(rows, DS[:, SL * e:SL * e + SL, :]).then_inc(eo_out, 16)
                sp.wait_ge(eo_out, 16 * X8)
                sp.wait_ge(zeroed, 32)

            @block.gpsimd
            def _(pool):
                nc.gpsimd.memset(TK[:, :, :], 0.0)
                nc.gpsimd.memset(zrow[:, :], 0.0).then_inc(zero, 1)
                nc.gpsimd.iota(trash[:, :], pattern=[[128, T]], base=TRASH, channel_multiplier=1, allow_small_or_imprecise_dtypes=True)
                nc.gpsimd.iota(rev[:, :], pattern=[[-1, X8]], base=X8, channel_multiplier=0, allow_small_or_imprecise_dtypes=True)
                nc.gpsimd.iota(offs[:, :], pattern=[[CAP, X8]], base=0, channel_multiplier=0, allow_small_or_imprecise_dtypes=True).then_inc(const, 1)
                nc.gpsimd.affine_select(out=before[:, :], in_=c.ones[:, :], compare_op=ALU.is_gt, fill=0.0,
                                        base=0, pattern=[[1, 128]], channel_multiplier=-1).then_inc(const, 1)
                norm_pool(nc, pool, st, c.half, s)
                pool.wait_ge(routed, 1)
                pool.wait_ge(zeroed, 32)
                pool.wait_ge(s.normed, 1)
                for t in range(T):
                    nc.gpsimd.indirect_dma_start(out=slots_dram, out_offset=bass.IndirectOffsetOnAxis(ap=idx[:, t:t + 1], axis=0),
                                                 in_=TK[:, t, :], in_offset=None).then_inc(sent, 16)
                pool.wait_ge(eo_out, 16 * X8)
                pool.wait_ge(sent, 16 * T)
                for t in range(T):
                    nc.gpsimd.indirect_dma_start(out=TK[:, t, :], out_offset=None, in_=eout_dram,
                                                 in_offset=bass.IndirectOffsetOnAxis(ap=gidx[:, t:t + 1], axis=0)).then_inc(got, 16)
                pool.wait_ge(got, 16 * T)

            @block.vector
            def _(dve):
                link = Chain(dve, own)
                dve.wait_ge(zeroed, 32)
                norm_dve(nc, dve, link, c.XN, TK, work, st, s, 1e-5)
                dve.wait_ge(loaded, 32)
                for q in range(4):
                    dve.wait_ge(s.transposed, q + 1)
                    nc.vector.tensor_scalar(tokT[:, 512 * q:512 * q + 512], bank[q][:, :], ln[:, 0:1], ln[:, 1:2], ALU.mult, ALU.add).then_inc(s.xnt_dve, 1)
                dve.wait_ge(logit, 1)
                dve.wait_ge(const, 2)
                link(nc.vector.tensor_copy(lg[:, :, :], bank[4][:, 0:T * X8].rearrange("p (t e) -> p t e", e=X8)))
                link(nc.vector.tensor_reduce(out=col[:, 0, :], in_=lg[:, :, :], op=ALU.max, axis=AX.X))
                link(nc.vector.tensor_tensor(w1[:, :, :], lg[:, :, :], bc(col[:, 0, :], X8), ALU.subtract))
                nc.vector.tensor_scalar(w2[:, :, :], w1[:, :, :], 0.0, None, ALU.is_equal).then_inc(chose, 1)
                dve.wait_ge(chose, 1)
                rev_all = rev[:, :].unsqueeze(1).to_broadcast([128, T, X8])
                link(nc.vector.tensor_tensor(w2[:, :, :], w2[:, :, :], rev_all, ALU.mult))
                link(nc.vector.tensor_reduce(out=col[:, 1, :], in_=w2[:, :, :], op=ALU.max, axis=AX.X))
                nc.vector.tensor_tensor(oh[:, :, :], w2[:, :, :], bc(col[:, 1, :], X8), ALU.is_equal).then_inc(chose, 1)
                dve.wait_ge(expd, 1)
                link(nc.vector.tensor_reduce(out=col[:, 2, :], in_=w1[:, :, :], op=ALU.add, axis=AX.X))
                link(nc.vector.reciprocal(col[:, 3, :], col[:, 2, :]))
                dve.wait_ge(ranked, 1)
                src, dst = w1, w2
                link(nc.vector.memset(src[:, 0:1, :], 0.0))
                link(nc.vector.tensor_copy(src[:, 1:T, :], bank[5][:, 128:128 + (T - 1) * X8].rearrange("p (t e) -> p t e", e=X8)))
                k = 1
                while k < T:
                    nc.vector.tensor_copy(dst[:, 0:k, :], src[:, 0:k, :])
                    link(nc.vector.tensor_tensor(dst[:, k:T, :], src[:, k:T, :], src[:, 0:T - k, :], ALU.add))
                    src, dst, k = dst, src, 2 * k
                link(nc.vector.tensor_tensor(dst[:, :, :], bank[5][:, 0:128].rearrange("p (t e) -> p t e", e=X8), src[:, :, :], ALU.add))
                link(nc.vector.tensor_tensor(dst[:, :, :], dst[:, :, :], oh[:, :, :], ALU.mult))
                link(nc.vector.tensor_reduce(out=col[:, 4, :], in_=dst[:, :, :], op=ALU.add, axis=AX.X))
                link(nc.vector.tensor_scalar(col[:, 5, :], col[:, 4, :], float(CAP), None, ALU.is_lt))
                link(nc.vector.tensor_tensor(col[:, 3, :], col[:, 3, :], col[:, 5, :], ALU.mult))
                link(nc.vector.tensor_tensor(src[:, :, :], oh[:, :, :], offs[:, :].unsqueeze(1).to_broadcast([128, T, X8]), ALU.mult))
                link(nc.vector.tensor_reduce(out=col[:, 6, :], in_=src[:, :, :], op=ALU.add, axis=AX.X))
                link(nc.vector.tensor_tensor(col[:, 6, :], col[:, 6, :], col[:, 4, :], ALU.add))
                link(nc.vector.tensor_tensor(col[:, 0, :], col[:, 6, :], trash[:, :], ALU.subtract))
                link(nc.vector.tensor_tensor(col[:, 0, :], col[:, 0, :], col[:, 5, :], ALU.mult))
                nc.vector.tensor_tensor(idx[:, :], col[:, 0, :], trash[:, :], ALU.add)
                link(nc.vector.tensor_scalar(col[:, 1, :], col[:, 6, :], -float(TRASH), None, ALU.add))
                link(nc.vector.tensor_tensor(col[:, 1, :], col[:, 1, :], col[:, 5, :], ALU.mult))
                nc.vector.tensor_scalar(gidx[:, :], col[:, 1, :], float(TRASH), None, ALU.add).then_inc(routed, 1)
                link(nc.vector.tensor_tensor(c.X[:, :, :], c.X[:, :, :], c.XN[:, :, :], ALU.add))
                for q in range(4):
                    dve.wait_ge(turned, q + 1)
                    nc.vector.tensor_scalar(DT[:, 512 * q:512 * q + 512], bank[q][:, :], ln[:, 0:1], ln[:, 1:2], ALU.mult, ALU.add).then_inc(dt_out, 1)
                for e in range(X8):
                    dve.wait_ge(down, e + 1)
                    nc.vector.tensor_copy(DS[:, SL * e:SL * e + SL, :], bank[6 + e % 2][:, 0:SL * D].rearrange("p (t d) -> p t d", d=D)).then_inc(eo, 1)
                dve.wait_ge(got, 16 * T)
                for t in range(T):
                    last = nc.vector.scalar_tensor_tensor(out=c.X[:, t, :], in0=TK[:, t, :], scalar=col[:, 3, t:t + 1], in1=c.X[:, t, :],
                                                          op0=ALU.mult, op1=ALU.add)
                last.then_inc(added, 1)

            @block.scalar
            def _(act):
                norm_act(nc, act, TK, work, s)
                act.wait_ge(chose, 1)
                nc.scalar.activation(w1[:, :, :], w1[:, :, :], ACT.Exp).then_inc(expd, 1)
                for e in range(X8):
                    for j in range(J):
                        n = J * e + j
                        act.wait_ge(up, n + 1)
                        if e >= 2 and j == 0:
                            act.wait_ge(down, e - 1)
                        nc.scalar.activation(H[e % 2][:, j, :], bank[n % 4][:, 0:CAP], ACT.Gelu).then_inc(act_out, 1)

            @block.tensor
            def _(pe):
                transpose_pe(nc, pe, TK, bank, c.ident, s)
                pe.wait_ge(s.xnt_dve, 4)
                for t in range(T):
                    last = nc.tensor.matmul(bank[4][:, X8 * t:X8 * t + X8], tokT[:, 128 * t:128 * t + 128], gw[:, :], start=True, stop=True)
                last.then_inc(logit, 1)
                pe.wait_ge(chose, 2)
                oh2 = oh[:, :, :].rearrange("p t e -> p (t e)")
                nc.tensor.matmul(bank[5][:, 0:128], before[:, :], oh2, start=True, stop=True)
                nc.tensor.matmul(bank[5][:, 128:256], c.ones[:, :], oh2, start=True, stop=True).then_inc(ranked, 1)
                pe.wait_ge(back, 16)
                for q in range(4):
                    for j in range(4):
                        last = nc.tensor.transpose(bank[q][:, 128 * j:128 * j + 128], DS[:, 4 * q + j, :], c.ident[:, :])
                    last.then_inc(turned, 1)
                pe.wait_ge(w_loaded, 32)
                pe.wait_ge(dt_out, 4)
                for e in range(X8):
                    for j in range(J):
                        n = J * e + j
                        if n >= 4:
                            pe.wait_ge(act_out, n - 3)
                        nc.tensor.matmul(bank[n % 4][:, 0:CAP], wi[:, e, 128 * j:128 * j + 128], DT[:, CAP * e:CAP * e + CAP],
                                         start=True, stop=True).then_inc(up, 1)
                    pe.wait_ge(act_out, J * e + J)
                    if e >= 2:
                        pe.wait_ge(eo, e - 1)
                    for k in range(SL):
                        for j in range(J):
                            last = nc.tensor.matmul(bank[6 + e % 2][:, D * k:D * k + D], H[e % 2][:, j, 128 * k:128 * k + 128], wo[:, e, j, :],
                                                    start=(j == 0), stop=(j == J - 1))
                    last.then_inc(down, 1)


def masked_attention_stage(nc, c, p):
    H, DH, MASKED = 16, 8, -1e30
    NP, F = H // 2, 2 * DH
    PARTS_Q, PARTS_K = (0, 0, 1, 1, 0, 2), (0, 1, 0, 1, 2, 0)
    ROWS = F * len(PARTS_Q)
    PIECES = [(512 * w, min(512, M - 512 * w)) for w in range(4)]
    AHEAD = (0, 2, 5, 8)
    TURN_ROWS = 1
    FIRST, LAG = 2, 3
    OUT1, OUT2 = 6, 10
    STACKED = 16 * len(PARTS_K)
    with ExitStack() as ctx:
        m = Memory(nc, ctx, "ma")
        wq, wk, wv, wo, bo = (m.sb(n, [128, 128]) for n in ("wq", "wk", "wv", "wo", "bo"))
        QT = OT = c.XN[:, :, :].rearrange("p t d -> p (t d)")
        cT = [m.sb(f"ctxT{k}", [128, M]) for k in range(2)]
        KP, KR = m.sb("k_parts", [128, 3, M], bf16), m.sb("k_rest", [128, M])
        KF = [m.sb(f"k_stack{k}", [128, NP * M], bf16) for k in range(2)]
        KS = [flat[:, :].rearrange("p (n m) -> p n m", n=NP) for flat in KF]
        QR = m.sb("q_stack", [ROWS, NP, B * S], bf16)
        Q = [m.sb(f"q_blocks{k}", [128, NP, 2 * S], bf16) for k in range(2)]
        V = [m.sb(f"v{k}", [128, NC_, NP, F + 1]) for k in range(2)]
        mraw = m.sb("mask_raw", [128, M], i32)
        mb = [m.sb(f"mask_bias{k}", [128, M], bf16) for k in range(2)]
        masked = [m.sb(f"masked_scores{k}", [128, 512], bf16) for k in range(2)]
        ET = [m.sb(f"eT{k}", [128, 512]) for k in range(4)]
        mx, nmx = m.sb("mx", [128, 4, 4]), m.sb("nmx", [128, 4])
        mp = m.sb("max_parts", [128, 4, 3], bf16)
        Osb, On, rden, acc = m.sb("sums_sb", [128, 256]), m.sb("out_norm", [128, 128]), m.sb("rden", [128, NP]), m.sb("acc", [128, S])
        blk2, eye2 = m.sb("blk2", [128, 2]), m.sb("eye2", [128, S])
        identb, eyes = m.sb("identb", [128, 128], bf16), m.sb("eyes", [S, 8, S], bf16)
        S1 = [m.ps(f"scores{w}") for w in range(2)]
        S2 = [m.ps(f"scoresT{w}") for w in range(3)]
        OB, PB, MB = m.ps("sums"), m.ps("proj"), m.ps("misc")
        Qparts = KF[1][:, 0:3 * B * S].rearrange("p (t q) -> p t q", t=3)

        (w_loaded, const, q_mm, q_out, q_rest, q_split, q_stacked, mask_ready, q_ready, scored, maxed, max_ready, rows_mm, rows_ready,
         scored2, exped, weighed, o_read, o_turned, o_normed, o_back, o_done, projected, kh_out, k_out, split, v_out,
         out_mm, added, mask_loaded, bank_zero) = (m.sem(n) for n in (
            "w_loaded", "const", "q_projected", "q_scaled", "q_rest", "q_split", "q_stacked", "mask_ready", "q_ready", "scored", "maxed",
            "max_ready", "max_rows_mm", "max_rows", "scoredT", "exped", "weighed", "o_read", "o_turned", "o_normed",
            "o_back", "o_done", "projected", "kh_out", "k_out", "k_split", "v_out", "out_projected", "added", "mask_loaded", "bank_zero"))
        pool_own, ones_set = m.sem("pool_own"), m.sem("ones_set")
        ctx_loaded = [m.sem(f"ctx_loaded{k}") for k in range(2)]
        stacked = [m.sem(f"k_stacked{a}") for a in range(2)]
        own, own_first, own_last = m.sem("dve_own"), m.sem("dve_own_first"), m.sem("dve_own_last")
        dve_passed, pool_passed = m.sem("dve_passed"), m.sem("pool_passed")
        PAIRS = B // 2

        def bank_of(s, ch):
            x = NC_ * s + ch
            return x % 3, 3 if x > 2 else (1, 4, 4)[x]

        ONES = 1.0 + 0x3F80 / 2 ** 23

        def ones_rows(flat):
            return flat[ROWS:ROWS + 3, :].bitcast(fp32)

        def load_ctx(sp, b, k):
            sp.dma_start(cT[k][:, :], p["ctxT"][bass.ds(b, 1), :, :].rearrange("a d m -> (a d) m")).then_inc(ctx_loaded[k], 16)

        def load_mask(sp, b):
            rows = p["mask"][bass.ds(b, 1), :, :].rearrange("a s m -> (a s) m")
            for h in range(2):
                sp.dma_start(mraw[64 * h:64 * h + 64, :], rows).then_inc(mask_loaded, 16)

        with nc.Block() as block:
            @block.sync
            def _(sp):
                for dst, name in ((wq, "WqT1"), (wk, "WkT1"), (wv, "WvT1"), (wo, "WoT1")):
                    sp.dma_start(dst[:, :], p[name]).then_inc(w_loaded, 16)
                sp.dma_start(bo[:, :], p["bo"].partition_broadcast(128)).then_inc(w_loaded, 16)
                load_ctx(sp, 0, 0)
                load_mask(sp, 0)
                load_ctx(sp, 1, 1)
                for t, part in sorted(enumerate(PARTS_Q), key=lambda x: x[1]):
                    sp.wait_ge(q_split, part + 1)
                    for a in range(2):
                        sp.dma_start(QR[F * t:F * t + F, 4 * a:4 * a + 4, :], Qparts[64 * a:64 * a + 64, part, :]).then_inc(q_stacked, 16)
                sp.wait_ge(w_loaded, 80)
                sp.wait_ge(q_stacked, 192)

            @block.gpsimd
            def _(pool):
                nc.gpsimd.memset(blk2[:, :], 0.0)
                nc.gpsimd.memset(eye2[:, :], 0.0).then_inc(const, 1)
                n = 1
                fills = [(blk2, 2, 8, r + F * h) for h in range(NP) for r in range(DH)]
                fills += [(eye2, S, 1, 64 * h) for h in range(2)]
                for dst, k, step, base in fills:
                    pool.wait_ge(const, n)
                    nc.gpsimd.affine_select(out=dst[:, :], in_=dst[:, :], compare_op=ALU.not_equal, fill=1.0, base=-base,
                                            pattern=[[-step, k]], channel_multiplier=1).then_inc(const, 1)
                    n += 1
                pool.wait_ge(const, n)
                nc.gpsimd.tensor_copy(eyes[:, :, :], eye2[0:S, :].unsqueeze(1).to_broadcast([S, 8, S])).then_inc(const, 1)
                nc.gpsimd.tensor_copy(identb[:, :], c.ident[:, :]).then_inc(const, 1)

            @block.tensor
            def _(pe):
                pe.wait_ge(w_loaded, 80)
                for q in range(4):
                    nc.tensor.matmul((S1 + S2)[q][:, :], wq[:, :], c.XNT[:, 512 * q:512 * q + 512], start=True, stop=True).then_inc(q_mm, 1)

            @block.scalar
            def _(act):
                for q in range(4):
                    act.wait_ge(q_mm, q + 1)
                    nc.scalar.activation(QT[:, 512 * q:512 * q + 512], (S1 + S2)[q][:, :], ACT.Copy, scale=float(DH) ** -0.5).then_inc(q_out, 1)
                act.wait_ge(q_out, 4)
                nc.scalar.activation(Qparts[:, 0, :], QT[:, :], ACT.Copy).then_inc(q_split, 1)

            @block.vector
            def _(dve):
                nc.vector.memset(OB[:, :], 0.0).then_inc(bank_zero, 1)
                for k in range(2):
                    nc.vector.memset(V[k][:, :, :, F:F + 1], 1.0)
                dve.wait_ge(q_split, 1)
                nc.vector.tensor_tensor(QT[:, :], QT[:, :], Qparts[:, 0, :], ALU.subtract).then_inc(q_rest, 1)
                dve.wait_ge(q_rest, 1)
                nc.vector.tensor_copy(Qparts[:, 1, :], QT[:, :]).then_inc(q_split, 1)
                dve.wait_ge(q_split, 2)
                nc.vector.tensor_tensor(Qparts[:, 2, :], QT[:, :], Qparts[:, 1, :], ALU.subtract).then_inc(q_split, 1)
                nc.vector.memset(ones_rows(KF[0]), ONES)

        with nc.Block() as block:
            @block.sync
            def _(sp):
                def stack(b, k, a):
                    if a == 0:
                        sp.wait_ge(split, b + 1)
                    if not (isinstance(b, int) and b < 2):
                        sp.wait_ge(scored2, NC_ * (2 * b - 3 + a))
                    for t, part in enumerate(PARTS_K):
                        sp.dma_start(KS[k][F * t:F * t + F, 4 * a:4 * a + 4, :],
                                     KP[64 * a:64 * a + 64, part, :]).then_inc(stacked[a], 16)

                def batch(b, k, ahead=2):
                    if ahead == 2:
                        sp.wait_ge(projected, 8 * b + 8)
                        load_ctx(sp, b + 2, k)
                    stack(b + 1, 1 - k, 0)
                    stack(b + 1, 1 - k, 1)
                    if ahead == 2:
                        sp.wait_ge(mask_ready, b + 2)
                        load_mask(sp, b + 2)

                stack(0, 0, 0)
                stack(0, 0, 1)
                sp.wait_ge(mask_ready, 1)
                load_mask(sp, 1)
                batch(0, 0)
                batch(1, 1)
                with sp.Fori(1, PAIRS - 1) as i:
                    batch(2 * i, 0)
                    batch(2 * i + 1, 1)
                batch(B - 2, 0, 1)

            @block.gpsimd
            def _(pool):
                def parts(b):
                    pool.wait_ge(k_out, 4 * b + 4)
                    pool.sem_inc(pool_passed, 1)
                    nc.gpsimd.tensor_copy(KP[:, 1, :], KR[:, :]).then_inc(pool_own, 1)
                    pool.wait_ge(pool_own, b + 1)
                    nc.gpsimd.tensor_tensor(KP[:, 2, :], KR[:, :], KP[:, 1, :], ALU.subtract).then_inc(split, 1)

                def prepare(b, k):
                    if not (isinstance(b, int) and b < 2):
                        pool.wait_ge(scored2, 2 * NC_ * (b - 1))
                    pool.wait_ge(mask_loaded, 32 * b + 32)
                    pool.sem_inc(pool_passed, 1)
                    nc.gpsimd.tensor_scalar(mb[k][:, :], mraw[:, :], 0, MASKED, ALU.is_equal, ALU.mult).then_inc(mask_ready, 1)
                    q = QR[:, :, bass.ds(64 * b, S)].unsqueeze(2).to_broadcast([ROWS, NP, 2, S])
                    blocks = blk2[0:ROWS, :].unsqueeze(1).unsqueeze(3).to_broadcast([ROWS, NP, 2, S])
                    nc.gpsimd.tensor_tensor(Q[k][0:ROWS, :, :].rearrange("p n (h q) -> p n h q", h=2), q, blocks, ALU.mult).then_inc(q_ready, 1)

                prepare(0, 0)
                parts(0)
                pool.wait_ge(split, 1)
                nc.gpsimd.memset(ones_rows(KF[1]), ONES).then_inc(ones_set, 1)
                pool.wait_ge(ones_set, 1)
                for b in range(2):
                    parts(b + 1)
                    prepare(b + 1, 1 - b)
                with pool.Fori(1, PAIRS - 1) as i:
                    for k in range(2):
                        parts(2 * i + k + 1)
                        prepare(2 * i + k + 1, 1 - k)
                parts(B - 1)
                prepare(B - 1, 1)

            @block.tensor
            def _(pe):
                def project(b, k, i, n):
                    if n == 0:
                        pe.wait_ge(ctx_loaded[k], 16 * i + 16)
                    if n in (0, 5, 6, 7) and not (isinstance(b, int) and b == 0 and n == 0):
                        pe.wait_ge(v_out, 4 * b + max(n - 4, 0))
                    if n in (1, 2, 3, 4):
                        pe.wait_ge(k_out, 4 * b + n)
                    if n < 4:
                        o, w = PIECES[n]
                        nc.tensor.matmul(PB[:, 0:w], wk[:, :], cT[k][:, o:o + w], start=True, stop=True).then_inc(projected, 1)
                        return
                    for ch in range(4 * (n - 4), min(4 * (n - 4) + 4, NC_)):
                        h = 128 if ch < FULL else TAIL
                        last = nc.tensor.matmul(PB[0:h, 128 * (ch % 4):128 * (ch % 4) + 128], cT[k][:, 128 * ch:128 * ch + h], wv[:, :], start=True, stop=True)
                    last.then_inc(projected, 1)

                def score(b, k, a, r):
                    j, (o, w) = r // 4, PIECES[r % 4]
                    n = 16 * (2 * b + a) + r
                    if r == 0:
                        if a == 0:
                            pe.wait_ge(q_ready, b + 1)
                        pe.wait_ge(stacked[a], STACKED * (b + 1))
                    if not (isinstance(n, int) and n < 2):
                        pe.wait_ge(maxed, n - 1)
                    nc.tensor.matmul(S1[r % 2][:, 0:w], Q[k][0:ROWS, 4 * a + j, :], KS[k][0:ROWS, 4 * a + j, o:o + w], start=True, stop=True).then_inc(scored, 1)

                def max_rows(u):
                    pe.wait_ge(max_ready, u)
                    for j in range(4):
                        last = nc.tensor.matmul(MB[ROWS:ROWS + 3, 128 * j:128 * j + 128], mp[:, j, :], identb[:, :], start=True, stop=True)
                    last.then_inc(rows_mm, 1)

                def score_turned(v, s, kb, av, ch):
                    h = 128 if ch < FULL else TAIL
                    g, (bank, lag) = NC_ * v + ch, bank_of(s, ch)
                    if ch == 0:
                        pe.wait_ge(rows_ready, v + 1)
                    if not (isinstance(g, int) and g < lag):
                        pe.wait_ge(exped, g - lag + 1)
                    out = S2[bank]
                    nc.tensor.matmul(out[0:h, :], mb[kb][0:S, 128 * ch:128 * ch + h], eyes[:, :, :].rearrange("p n q -> p (n q)"), start=True, stop=False)
                    for j in range(4):
                        last = nc.tensor.matmul(out[0:h, 128 * j:128 * j + 128], KS[kb][0:ROWS + 3, 4 * av + j, 128 * ch:128 * ch + h],
                                                Q[kb][0:ROWS + 3, 4 * av + j, :], start=False, stop=(j == 3))
                    last.then_inc(scored2, 1)

                def weigh(v, s, kb, av, ch):
                    h = 128 if ch < FULL else TAIL
                    if ch == 0:
                        if not (isinstance(v, int) and v == 0):
                            pe.wait_ge(o_read, v)
                    pe.wait_ge(exped, NC_ * v + ch + 1)
                    for j in range(4):
                        last = nc.tensor.matmul(OB[32 * j:32 * j + F + 1, 128 * av:128 * av + 128], V[kb][0:h, ch, 4 * av + j, :],
                                                ET[(NC_ * s + ch) % 4][0:h, 128 * j:128 * j + 128], start=(ch == 0), stop=(ch == NC_ - 1))
                    last.then_inc(weighed, 1)

                def slot(i, s, scores=True, before=True, ahead=True, finished=True):
                    k, a = s // 2, s % 2
                    b = 2 * i + k
                    u = 2 * b + a
                    kb, av = ((s - 1) // 2) % 2, (s - 1) % 2
                    for r in range(16):
                        if scores:
                            score(b, k, a, r)
                        if ahead and r in AHEAD:
                            project(b + 1, 1 - k, i + k, 4 * a + AHEAD.index(r))
                        if before and r == TURN_ROWS:
                            if a == 0 and not (isinstance(b, int) and b < 2):
                                pe.wait_ge(o_done, b - 1)
                            max_rows(u)
                        if before and FIRST <= r < FIRST + NC_:
                            score_turned(u - 1, s, kb, av, r - FIRST)
                            if r - FIRST >= LAG:
                                weigh(u - 1, s, kb, av, r - FIRST - LAG)
                        if finished and a == 1 and r == OUT1:
                            pe.wait_ge(o_read, 2 * b)
                            for x in range(2):
                                last = nc.tensor.transpose(MB[:, 128 * x:128 * x + 128], Osb[:, 128 * x:128 * x + 128], c.ident[:, :])
                            last.then_inc(o_turned, 1)
                        if finished and a == 1 and r == OUT2:
                            pe.wait_ge(o_normed, b)
                            nc.tensor.transpose(MB[:, 256:384], On[:, :], c.ident[:, :]).then_inc(o_back, 1)
                    if before:
                        for ch in range(NC_ - LAG, NC_):
                            weigh(u - 1, s, kb, av, ch)

                for n in range(8):
                    project(0, 0, 0, n)
                for s in range(4):
                    slot(0, s, before=s > 0, finished=s > 1)
                with pe.Fori(1, PAIRS - 1) as i:
                    for s in range(4):
                        slot(i, s)
                for s in range(4):
                    slot(PAIRS - 1, s, ahead=s < 2)
                slot(PAIRS, 0, scores=False, ahead=False)
                slot(PAIRS, 1, scores=False, before=False, ahead=False)

            @block.vector
            def _(dve):
                def rest(b, n):
                    o, w = PIECES[n]
                    dve.wait_ge(kh_out, 4 * b + n + 1)
                    nc.vector.tensor_tensor(KR[:, o:o + w], PB[:, 0:w], KP[:, 0, o:o + w], ALU.subtract).then_inc(k_out, 1)

                def values(b, k, n):
                    if n == 0 and not (isinstance(b, int) and b < 2):
                        dve.wait_ge(weighed, 2 * NC_ * (b - 1))
                    dve.wait_ge(projected, 8 * b + 5 + n)
                    w, h = (4, 128) if n < 3 else (1, TAIL)
                    nc.vector.tensor_copy(V[k][0:h, 4 * n:4 * n + w, :, 0:F],
                                          PB[0:h, 0:128 * w].rearrange("p (c n f) -> p c n f", c=w, f=F)).then_inc(v_out, 1)

                def slot(i, s, link, scores=True, ahead=True, finished=True):
                    k, a = s // 2, s % 2
                    b = 2 * i + k
                    u = 2 * b + a
                    if scores and a == 0:
                        dve.wait_ge(mask_ready, b + 1)
                    for r in range(16):
                        if scores:
                            o, w = PIECES[r % 4]
                            dve.wait_ge(scored, 16 * u + r + 1)
                            dve.sem_inc(dve_passed, 1)
                            nc.vector.tensor_tensor_reduce(out=masked[r % 2][:, 0:w], in0=S1[r % 2][:, 0:w], in1=mb[k][:, o:o + w],
                                                           scale=1.0, scalar=-3e38, op0=ALU.add, op1=ALU.max,
                                                           accum_out=mx[:, r // 4, r % 4:r % 4 + 1]).then_inc(maxed, 1)
                        if ahead and r in AHEAD:
                            if a == 0:
                                rest(b + 1, AHEAD.index(r))
                            else:
                                values(b + 1, 1 - k, AHEAD.index(r))
                        if finished and a == 1 and r == OUT1:
                            dve.wait_ge(o_turned, b)
                            turned = MB[:, 0:256].rearrange("p (n f) -> p n f", f=32)
                            link(nc.vector.reciprocal(rden[:, :], turned[:, :, F]))
                            nc.vector.tensor_tensor(On[:, :].rearrange("p (n f) -> p n f", f=F), turned[:, :, 0:F], bc(rden[:, :], F), ALU.mult).then_inc(o_normed, 1)
                        if finished and a == 1 and r == OUT2:
                            dve.wait_ge(o_back, b)
                            link(nc.vector.tensor_scalar(acc[:, :], MB[:, 256:256 + S], blk2[:, 0:1], None, ALU.mult))
                            nc.vector.scalar_tensor_tensor(out=OT[:, bass.ds(S * (b - 1), S)], in0=MB[:, 256 + S:256 + 2 * S], scalar=blk2[:, 1:2], in1=acc[:, :],
                                                           op0=ALU.mult, op1=ALU.add).then_inc(o_done, 1)
                    if scores:
                        dve.wait_ge(maxed, 16 * u + 16)
                        link(nc.vector.tensor_reduce(out=nmx[:, :], in_=mx[:, :, :], op=ALU.max, axis=AX.X, negate=True))
                        link(nc.vector.tensor_copy(mp[:, :, 0], nmx[:, :]))
                        link(nc.vector.tensor_tensor(nmx[:, :], nmx[:, :], mp[:, :, 0], ALU.subtract))
                        link(nc.vector.tensor_copy(mp[:, :, 1], nmx[:, :]))
                        nc.vector.tensor_tensor(mp[:, :, 2], nmx[:, :], mp[:, :, 1], ALU.subtract).then_inc(max_ready, 1)

                OWN = 4 * 4 + 2 * 2

                for n in range(4):
                    rest(0, n)
                for n in range(4):
                    values(0, 0, n)
                link = Chain(dve, own_first)
                for s in range(4):
                    slot(0, s, link, finished=s > 1)
                with dve.Fori(1, PAIRS - 1) as i:
                    link = Chain(dve, own, OWN, i - 1)
                    for s in range(4):
                        slot(i, s, link)
                    link.close()
                link = Chain(dve, own_last)
                for s in range(4):
                    slot(PAIRS - 1, s, link, ahead=s < 2)
                slot(PAIRS, 1, link, scores=False, ahead=False)

            @block.scalar
            def _(act):
                def high(b, n):
                    if n == 0 and not (isinstance(b, int) and b == 0):
                        for a in range(2):
                            act.wait_ge(stacked[a], STACKED * b)
                    act.wait_ge(projected, 8 * b + n + 1)
                    o, w = PIECES[n]
                    nc.scalar.activation(KP[:, 0, o:o + w], PB[:, 0:w], ACT.Copy).then_inc(kh_out, 1)

                def slot(i, s, before=True, ahead=True, sums=True):
                    k, a = s // 2, s % 2
                    b = 2 * i + k
                    u = 2 * b + a
                    if sums:
                        act.wait_ge(weighed, NC_ * (u - 1))
                        x = 128 * (s % 2)
                        nc.scalar.activation(Osb[:, x:x + 128], OB[:, x:x + 128], ACT.Copy).then_inc(o_read, 1)
                    for r in range(16):
                        if ahead and a == 0 and r in AHEAD:
                            high(b + 1, AHEAD.index(r))
                        if before and r == TURN_ROWS:
                            act.wait_ge(rows_mm, u)
                            kb, av = ((s - 1) // 2) % 2, (s - 1) % 2
                            nc.scalar.activation(Q[kb][ROWS:ROWS + 3, 4 * av:4 * av + 4, :], MB[ROWS:ROWS + 3, :].rearrange("p (n q) -> p n q", n=4), ACT.Copy).then_inc(rows_ready, 1)
                        if before and FIRST <= r < FIRST + NC_:
                            ch = r - FIRST
                            h, g = 128 if ch < FULL else TAIL, NC_ * (u - 1) + ch
                            if not (isinstance(g, int) and g < 4):
                                act.wait_ge(weighed, g - 3)
                            act.wait_ge(scored2, g + 1)
                            nc.scalar.activation(ET[(NC_ * s + ch) % 4][0:h, :], S2[bank_of(s, ch)[0]][0:h, :], ACT.Exp).then_inc(exped, 1)

                for n in range(4):
                    high(0, n)
                for s in range(4):
                    slot(0, s, before=s > 0, sums=s > 1)
                with act.Fori(1, PAIRS - 1) as i:
                    for s in range(4):
                        slot(i, s)
                for s in range(4):
                    slot(PAIRS - 1, s, ahead=s < 2)
                slot(PAIRS, 0, ahead=False)
                slot(PAIRS, 1, before=False, ahead=False)

        with nc.Block() as block:
            @block.tensor
            def _(pe):
                for t in range(T):
                    last = nc.tensor.matmul((S1 + S2)[t // 4][:, 128 * (t % 4):128 * (t % 4) + 128], OT[:, 128 * t:128 * t + 128], wo[:, :], start=True, stop=True)
                    if t % 4 == 3:
                        last.then_inc(out_mm, 1)

            @block.vector
            def _(dve):
                nc.vector.tensor_tensor(c.X[:, :, :], c.X[:, :, :], bo[:, :].unsqueeze(1).to_broadcast([128, T, D]), ALU.add).then_inc(added, 1)
                dve.wait_ge(added, 1)
                for q in range(4):
                    dve.wait_ge(out_mm, q + 1)
                    nc.vector.tensor_tensor(c.X[:, 4 * q:4 * q + 4, :], (S1 + S2)[q][:, :].rearrange("p (t d) -> p t d", d=D), c.X[:, 4 * q:4 * q + 4, :], ALU.add).then_inc(added, 1)


def retention_stage(nc, c, p):
    NH, DQ, DV = 8, 16, 32
    HH, NG = 2, 4
    with ExitStack() as ctx:
        m = Memory(nc, ctx, "re")
        w = {n: m.sb(n, [128, 128]) for n in ("rWq", "rWqs", "rWk", "rWks")}
        wv, wg, wo, woraw = m.sb("wv", [128, 256]), m.sb("wg", [128, 256]), m.sb("wo", [128, 2, 128]), m.sb("wo_raw", [128, 2, 128])
        cosT, sinT, gcol, head = m.sb("cos", [128, S]), m.sb("sin", [128, S]), m.sb("gcol", [128, 1]), m.sb("head", [128, HH])
        decay = m.sb("decay", [128, 512])
        tmp = [m.sb(f"tmp{k}", [128, 512]) for k in range(2)]
        qr, kr, QB = c.XN[:, :, :].rearrange("p t d -> p (t d)"), m.sb("k_rot", [128, T * 128]), m.sb("q_blocks", [128, HH, T * 128])
        V, G, P = m.sb("v", [128, T, 256]), m.sb("gate", [128, T, 256]), m.sb("weights", [128, T, 512])
        O, ms = V, m.sb("ms", [128, 3, T * NH])
        big_half = m.sb("big_half", [128, T * NH])
        OT = P[:, :, :].rearrange("p t n -> p (t n)")[:, 0:2 * T * 128].rearrange("p (j n) -> p j n", j=2)
        bank = [m.ps(f"bank{q}") for q in range(8)]
        (loaded, qk_mm, roped, blocked, vg_mm, v_out, g_act, g_out, s_mm, p_out, o_mm, o_sq, o_ms, o_rs, o_done, t_mm, t_act, y_mm, added, own, half_set) = (
            m.sem(n) for n in ("loaded", "qk_projected", "roped", "q_blocked", "vg_projected", "v_out", "gate_tanh", "gate_out", "scored", "decayed",
                               "o_summed", "o_squared", "o_meansq", "o_rstd", "o_done", "turned", "turned_out", "y_projected", "added", "dve_own", "half_set"))
        loads = [(w[n], p[n]) for n in w] + [(wv, p["rWv"]), (wg, p["rWg"]), (cosT, p["cosT"]), (sinT, p["sinT"]), (gcol, p["gcol"]),
                                             (head, p["head"]), (decay, p["decay"])]

        with nc.Block() as block:
            @block.sync
            def _(sp):
                for dst, src in loads:
                    sp.dma_start(dst[:, :], src).then_inc(loaded, 16)
                sp.dma_start(woraw[:, :, :], p["rWo"].rearrange("(j i) d -> i j d", i=128)).then_inc(loaded, 16)
                sp.wait_ge(loaded, 16 * (len(loads) + 1))

            @block.tensor
            def _(pe):
                pe.wait_ge(loaded, 16 * (len(loads) + 1))
                for q in range(4):
                    if q >= 2:
                        pe.wait_ge(roped, 2 * (q - 1))
                    for k, n in enumerate(w):
                        nc.tensor.matmul(bank[4 * (q % 2) + k][:, :], w[n][:, :], c.XNT[:, 512 * q:512 * q + 512], start=True, stop=True).then_inc(qk_mm, 1)

            @block.vector
            def _(dve):
                link = Chain(dve, own)
                cs, sn = (v[:, :].unsqueeze(1).to_broadcast([128, 8, S]) for v in (cosT, sinT))
                for q in range(4):
                    for k, dst in enumerate((qr, kr)):
                        straight, swapped = (bank[4 * (q % 2) + 2 * k + x][:, :].rearrange("p (b s) -> p b s", s=S) for x in range(2))
                        dve.wait_ge(qk_mm, 4 * q + 2 * k + 2)
                        nc.vector.tensor_tensor(tmp[0][:, :].rearrange("p (b s) -> p b s", s=S), straight, cs, ALU.mult)
                        link(nc.vector.tensor_tensor(tmp[1][:, :].rearrange("p (b s) -> p b s", s=S), swapped, sn, ALU.mult))
                        nc.vector.tensor_tensor(dst[:, 512 * q:512 * q + 512], tmp[0][:, :], tmp[1][:, :], ALU.add).then_inc(roped, 1)
                        dve.wait_ge(roped, 2 * q + k + 1)
                for j in range(2):
                    nc.vector.tensor_scalar(wo[:, j, :], woraw[:, j, :], gcol[:, 0:1], 0.5, ALU.mult, ALU.mult)
                nc.vector.memset(big_half[:, :], -0.5).then_inc(half_set, 1)

            @block.scalar
            def _(act):
                for q in range(4):
                    act.wait_ge(roped, 2 * q + 1)
                    for hh in range(HH):
                        nc.scalar.activation(QB[:, hh, 512 * q:512 * q + 512], qr[:, 512 * q:512 * q + 512], ACT.Copy, scale=head[:, hh:hh + 1]).then_inc(blocked, 1)

        with nc.Block() as block:
            @block.tensor
            def _(pe):
                for n in range(T // 2):
                    for k, wt in enumerate((wv, wg)):
                        if n >= 4:
                            pe.wait_ge((v_out, g_out)[k], n - 3)
                        for t in (2 * n, 2 * n + 1):
                            last = nc.tensor.matmul(bank[4 * k + n % 4][:, 256 * (t % 2):256 * (t % 2) + 256], c.XNT[:, 128 * t:128 * t + 128], wt[:, :], start=True, stop=True)
                        last.then_inc(vg_mm, 1)

            @block.scalar
            def _(act):
                for n in range(T // 2):
                    act.wait_ge(vg_mm, 2 * n + 1)
                    nc.scalar.activation(V[:, 2 * n:2 * n + 2, :], bank[n % 4][:, :].rearrange("p (t d) -> p t d", t=2), ACT.Copy).then_inc(v_out, 1)
                    act.wait_ge(vg_mm, 2 * n + 2)
                    nc.scalar.activation(G[:, 2 * n:2 * n + 2, :], bank[4 + n % 4][:, :].rearrange("p (t d) -> p t d", t=2), ACT.Tanh, scale=0.5).then_inc(g_act, 1)

            @block.vector
            def _(dve):
                for n in range(T // 2):
                    dve.wait_ge(g_act, n + 1)
                    g2 = G[:, 2 * n:2 * n + 2, :].rearrange("p t d -> p (t d)")
                    nc.vector.scalar_tensor_tensor(out=g2, in0=g2, scalar=1.0, in1=bank[4 + n % 4][:, :], op0=ALU.add, op1=ALU.mult).then_inc(g_out, 1)

        with nc.Block() as block:
            @block.tensor
            def _(pe):
                for r in range(4):
                    for g in range(NG):
                        if r >= 2:
                            pe.wait_ge(p_out, NG * (r - 2) + g + 1)
                        for t in range(4 * r, 4 * r + 4):
                            for b in (2 * t, 2 * t + 1):
                                h = 64 * (b % 2)
                                last = nc.tensor.matmul(bank[4 * (r % 2) + g][h:h + 64, 128 * (t % 4):128 * (t % 4) + 128],
                                                        kr[32 * g:32 * g + 32, 64 * b:64 * b + 64],
                                                        QB[32 * g:32 * g + 32, :, 64 * b:64 * b + 64], start=True, stop=True)
                        last.then_inc(s_mm, 1)

            @block.vector
            def _(dve):
                for r in range(4):
                    for g in range(NG):
                        dve.wait_ge(s_mm, NG * r + g + 1)
                        dec = decay[:, 128 * g:128 * g + 128].unsqueeze(1).to_broadcast([128, 4, 128])
                        nc.vector.tensor_tensor(P[:, 4 * r:4 * r + 4, 128 * g:128 * g + 128], bank[4 * (r % 2) + g][:, :].rearrange("p (t n) -> p t n", t=4),
                                                dec, ALU.mult).then_inc(p_out, 1)

        with nc.Block() as block:
            @block.tensor
            def _(pe):
                for n in range(T // 2):
                    for t in (2 * n, 2 * n + 1):
                        for hd in range(NH):
                            for b in (2 * t, 2 * t + 1):
                                h = 64 * (b % 2)
                                o = 256 * (t % 2) + DV * hd
                                last = nc.tensor.matmul(bank[n][h:h + 64, o:o + DV], P[h:h + 64, t, 64 * hd:64 * hd + 64], V[h:h + 64, t, DV * hd:DV * hd + DV],
                                                        start=True, stop=True)
                    last.then_inc(o_mm, 1)

            @block.scalar
            def _(act):
                sq = QB[:, :, :].rearrange("p h n -> p (h n)")
                for n in range(T // 2):
                    act.wait_ge(o_mm, n + 1)
                    nc.scalar.activation(sq[:, 512 * n:512 * n + 512], bank[n][:, :], ACT.Square).then_inc(o_sq, 1)

            @block.gpsimd
            def _(pool):
                for n in range(4):
                    pool.wait_ge(o_ms, n + 1)
                    part = slice(4 * NH * n, 4 * NH * n + 4 * NH)
                    nc.gpsimd.tensor_tensor(ms[:, 2, part], ms[:, 1, part], big_half[:, part], ALU.pow).then_inc(o_rs, 1)

            @block.vector
            def _(dve):
                link = Chain(dve, own)
                link.n = 8
                sq = QB[:, :, :].rearrange("p h n -> p (h n)")
                for n in range(4):
                    part = slice(4 * NH * n, 4 * NH * n + 4 * NH)
                    dve.wait_ge(o_sq, 2 * n + 2)
                    link(nc.vector.tensor_reduce(out=ms[:, 0, part], in_=sq[:, 1024 * n:1024 * n + 1024].rearrange("p (h d) -> p h d", d=DV), op=ALU.add, axis=AX.X))
                    nc.vector.tensor_scalar(ms[:, 1, part], ms[:, 0, part], 1.0 / DV, 1e-5, ALU.mult, ALU.add).then_inc(o_ms, 1)
                dve.wait_ge(o_mm, T // 2)
                for n in range(T // 2):
                    dve.wait_ge(o_rs, n // 2 + 1)
                    o2 = O[:, 2 * n:2 * n + 2, :].rearrange("p t d -> p (t d)")
                    rs = ms[:, 2, 2 * NH * n:2 * NH * n + 2 * NH]
                    link(nc.vector.tensor_tensor(o2.rearrange("p (h d) -> p h d", d=DV), bank[n][:, :].rearrange("p (h d) -> p h d", d=DV), bc(rs, DV), ALU.mult))
                    nc.vector.tensor_tensor(o2, o2, G[:, 2 * n:2 * n + 2, :].rearrange("p t d -> p (t d)"), ALU.mult).then_inc(o_done, 1)

        with nc.Block() as block:
            @block.tensor
            def _(pe):
                for n in range(T // 2):
                    j, q = n % 2, n // 2
                    if n >= 4:
                        pe.wait_ge(t_act, n - 3)
                    for t in range(4 * q, 4 * q + 4):
                        last = nc.tensor.transpose(bank[n % 4][:, 128 * (t % 4):128 * (t % 4) + 128], O[:, t, 128 * j:128 * j + 128], c.ident[:, :])
                    last.then_inc(t_mm, 1)
                for q in range(4):
                    pe.wait_ge(t_act, 2 * q + 2)
                    for t in range(4 * q, 4 * q + 4):
                        for j in range(2):
                            last = nc.tensor.matmul(bank[4 + q][:, 128 * (t % 4):128 * (t % 4) + 128], OT[:, j, 128 * t:128 * t + 128], wo[:, j, :], start=(j == 0), stop=(j == 1))
                    last.then_inc(y_mm, 1)

            @block.scalar
            def _(act):
                for n in range(T // 2):
                    j, q = n % 2, n // 2
                    act.wait_ge(t_mm, n + 1)
                    nc.scalar.activation(OT[:, j, 512 * q:512 * q + 512], bank[n % 4][:, :], ACT.Copy).then_inc(t_act, 1)

            @block.vector
            def _(dve):
                for q in range(4):
                    dve.wait_ge(y_mm, q + 1)
                    xs = c.X[:, 4 * q:4 * q + 4, :]
                    nc.vector.tensor_tensor(xs, bank[4 + q][:, :].rearrange("p (t d) -> p t d", d=D), xs, ALU.add).then_inc(added, 1)


def top2_moe_stage(nc, c, p):
    X8, H = 8, 256
    J, Q = H // 128, 4
    N = X8 + 1
    with ExitStack() as ctx:
        m = Memory(nc, ctx, "tm")
        w1, w2, w3 = m.sb("w1", [128, N, H]), m.sb("w2", [128, N, H]), m.sb("w3", [128, N, J, D])
        gw = m.sb("gate", [128, X8])
        lg, a1, a2, o1, o2 = (m.sb(n, [128, T, X8]) for n in ("logits", "work1", "work2", "first", "second"))
        col, wt = m.sb("col", [128, 8, T]), m.sb("weights", [128, T, N])
        rev = m.sb("rev", [128, X8])
        SIL = [m.sb(f"silu{k}", [128, 512]) for k in range(3)]
        G = [m.sb(f"hidden{k}", [128, J, 512]) for k in range(3)]
        bank = [m.ps(f"bank{q}") for q in range(8)]
        g_loaded, w_loaded, rev_set, logit, expd, shifted, weighed, up, silu, gated, down, added, own = (m.sem(n) for n in (
            "g_loaded", "w_loaded", "rev_set", "logits", "exp", "shifted", "weighed", "up", "silu", "gated", "down", "added", "dve_own"))
        with nc.Block() as block:
            @block.sync
            def _(sp):
                sp.dma_start(gw[:, :], p["gate1"]).then_inc(g_loaded, 16)
                for e in range(N):
                    src = [p[n][e] for n in ("ew1", "ew2", "ew3")] if e < X8 else [p[n] for n in ("sw1", "sw2", "sw3")]
                    sp.dma_start(w1[:, e, :], src[0]).then_inc(w_loaded, 16)
                    sp.dma_start(w2[:, e, :], src[1]).then_inc(w_loaded, 16)
                    sp.dma_start(w3[:, e, :, :], src[2].rearrange("(j i) d -> i j d", i=128)).then_inc(w_loaded, 16)
                sp.wait_ge(w_loaded, 48 * N)

            @block.gpsimd
            def _(pool):
                nc.gpsimd.iota(rev[:, :], pattern=[[-1, X8]], base=X8, channel_multiplier=0, allow_small_or_imprecise_dtypes=True).then_inc(rev_set, 1)

            @block.tensor
            def _(pe):
                pe.wait_ge(g_loaded, 16)
                for t in range(T):
                    last = nc.tensor.matmul(bank[6][:, X8 * t:X8 * t + X8], c.XNT[:, 128 * t:128 * t + 128], gw[:, :], start=True, stop=True)
                last.then_inc(logit, 1)

                def rise(e, q):
                    for j in range(J):
                        n = (e * Q + q) * J + j
                        if n >= 3:
                            pe.wait_ge(gated, n - 2)
                        for k, w in enumerate((w1, w2)):
                            last = nc.tensor.matmul(bank[2 * (n % 3) + k][:, :], w[:, e, 128 * j:128 * j + 128], c.XNT[:, 512 * q:512 * q + 512], start=True, stop=True)
                        last.then_inc(up, 1)

                def fall(e, q):
                    n = e * Q + q
                    pe.wait_ge(gated, J * n + J)
                    if n >= 2:
                        pe.wait_ge(added, n - 1)
                    if n == 0:
                        pe.wait_ge(weighed, 1)
                    for t in range(4):
                        for j in range(J):
                            last = nc.tensor.matmul(bank[6 + n % 2][:, 128 * t:128 * t + 128], G[n % 3][:, j, 128 * t:128 * t + 128], w3[:, e, j, :],
                                                    start=(j == 0), stop=(j == J - 1))
                    last.then_inc(down, 1)

                pe.wait_ge(w_loaded, 48 * N)
                before = None
                for e in range(N):
                    for q in range(Q):
                        rise(e, q)
                        if before:
                            fall(*before)
                        before = (e, q)
                fall(*before)

            @block.scalar
            def _(act):
                act.wait_ge(shifted, 1)
                nc.scalar.activation(col[:, 3, :], col[:, 2, :], ACT.Exp).then_inc(expd, 1)
                for n in range(N * Q * J):
                    act.wait_ge(up, n + 1)
                    if n >= 3:
                        act.wait_ge(gated, n - 2)
                    nc.scalar.activation(SIL[n % 3][:, :], bank[2 * (n % 3)][:, :], ACT.Silu).then_inc(silu, 1)

            @block.vector
            def _(dve):
                link = Chain(dve, own)
                rev_all = rev[:, :].unsqueeze(1).to_broadcast([128, T, X8])
                dve.wait_ge(logit, 1)
                link(nc.vector.tensor_copy(lg[:, :, :], bank[6][:, 0:T * X8].rearrange("p (t e) -> p t e", e=X8)))
                dve.wait_ge(rev_set, 1)

                def best(src, top, onehot):
                    link(nc.vector.tensor_reduce(out=col[:, top, :], in_=src, op=ALU.max, axis=AX.X))
                    link(nc.vector.tensor_tensor(a1[:, :, :], src, bc(col[:, top, :], X8), ALU.is_equal))
                    link(nc.vector.tensor_tensor(a1[:, :, :], a1[:, :, :], rev_all, ALU.mult))
                    link(nc.vector.tensor_reduce(out=col[:, 7, :], in_=a1[:, :, :], op=ALU.max, axis=AX.X))
                    link(nc.vector.tensor_tensor(onehot, a1[:, :, :], bc(col[:, 7, :], X8), ALU.is_equal))

                best(lg[:, :, :], 0, o1[:, :, :])
                link(nc.vector.tensor_scalar(a2[:, :, :], o1[:, :, :], -1e38, None, ALU.mult))
                link(nc.vector.tensor_tensor(a2[:, :, :], a2[:, :, :], lg[:, :, :], ALU.add))
                best(a2[:, :, :], 1, o2[:, :, :])
                nc.vector.tensor_tensor(col[:, 2, :], col[:, 1, :], col[:, 0, :], ALU.subtract).then_inc(shifted, 1)
                dve.wait_ge(expd, 1)
                link(nc.vector.tensor_scalar(col[:, 4, :], col[:, 3, :], 1.0, None, ALU.add))
                link(nc.vector.reciprocal(col[:, 5, :], col[:, 4, :]))
                link(nc.vector.tensor_tensor(col[:, 6, :], col[:, 5, :], col[:, 3, :], ALU.mult))
                nc.vector.tensor_tensor(o1[:, :, :], o1[:, :, :], bc(col[:, 5, :], X8), ALU.mult)
                link(nc.vector.tensor_tensor(o2[:, :, :], o2[:, :, :], bc(col[:, 6, :], X8), ALU.mult))
                nc.vector.tensor_tensor(wt[:, :, 0:X8], o1[:, :, :], o2[:, :, :], ALU.add)
                nc.vector.memset(wt[:, :, X8:N], 1.0).then_inc(weighed, 1)
                dve.wait_ge(weighed, 1)

                def gate(e, q):
                    for j in range(J):
                        n = (e * Q + q) * J + j
                        dve.wait_ge(silu, n + 1)
                        nc.vector.tensor_tensor(G[(n // J) % 3][:, j, :], bank[2 * (n % 3) + 1][:, :], SIL[n % 3][:, :], ALU.mult).then_inc(gated, 1)

                def collect(e, q):
                    n = e * Q + q
                    dve.wait_ge(down, n + 1)
                    for t in range(4):
                        last = nc.vector.scalar_tensor_tensor(out=c.X[:, 4 * q + t, :], in0=bank[6 + n % 2][:, 128 * t:128 * t + 128],
                                                              scalar=wt[:, 4 * q + t, e:e + 1], in1=c.X[:, 4 * q + t, :], op0=ALU.mult, op1=ALU.add)
                    last.then_inc(added, 1)
                    if n >= 1:
                        dve.wait_ge(added, n)

                before = []
                for e in range(N):
                    for q in range(Q):
                        gate(e, q)
                        before.append((e, q))
                        if len(before) > 2:
                            collect(*before.pop(0))
                for b in before:
                    collect(*b)


def store_stage(nc, c, out):
    with ExitStack() as ctx:
        m = Memory(nc, ctx, "st")
        stored = m.sem("stored")
        with nc.Block() as block:
            @block.sync
            def _(sp):
                sp.dma_start(out.rearrange("b s d -> (b s) d").rearrange("(t p) d -> p t d", p=128), c.X[:, :, :]).then_inc(stored, 16)
                sp.wait_ge(stored, 16)


def perceiver(nc, p, out):
    with ExitStack() as ctx:
        m = Memory(nc, ctx, "c")
        c = Common()
        c.X, c.XN, c.XNT = m.sb("X", [128, T, D]), m.sb("XN", [128, T, D]), m.sb("XNT", [128, T * 128])
        c.ident, c.ones, c.half = m.sb("ident", [128, 128]), m.sb("ones", [128, 128]), m.sb("minus_half", [128, 16])
        c.mq, c.wcT, c.whhT, c.bias = m.sb("mq", [128, 128]), m.sb("wcT", [128, 384]), m.sb("whhT", [128, 384]), m.sb("bias", [128, 5])
        setup_stage(nc, c, p)
        norm_block(nc, c, "n0")
        slot_attention_stage(nc, c, p["ctx"])
        norm_block(nc, c, "n1")
        linear_attention_stage(nc, c, p)
        norm_block(nc, c, "n2")
        capacity_moe_stage(nc, c, p)
        norm_block(nc, c, "n3")
        masked_attention_stage(nc, c, p)
        norm_block(nc, c, "n4")
        retention_stage(nc, c, p)
        norm_block(nc, c, "n5")
        top2_moe_stage(nc, c, p)
        store_stage(nc, c, out)


def rotary_tables(np):
    NH, DQ = 8, 16
    inv = 1.0 / 10000.0 ** (np.arange(0, DQ, 2, dtype=np.float32) / DQ)
    ang = (np.arange(S, dtype=np.float32)[None, :] * inv.astype(np.float32)[:, None]).astype(np.float32)
    row = np.arange(128)
    sign = np.where(row % 2 == 0, -1.0, 1.0)[:, None]
    pair = row % DQ // 2
    s = np.log2(1.0 - np.exp2(-5.0 - np.arange(NH)))
    diff = np.arange(S)[None, :] - np.arange(S)[:, None]
    dec = np.where(diff[:, None, :] >= 0, np.exp2(diff[:, None, :] * s[None, :, None]), 0.0).reshape(S, NH * S)
    head = (row[:, None] // DQ % 2 == np.arange(2)[None, :]) * float(DQ) ** -0.5
    f = np.float32
    return {"cosT": np.cos(ang)[pair].astype(f), "sinT": (np.sin(ang)[pair] * sign).astype(f),
            "decay": np.concatenate([dec, dec]).astype(f), "head": head.astype(f)}


def by_feature(w):
    return w.T.reshape(D, 2, 4, D // 8).transpose(0, 1, 3, 2).reshape(D, D)


def kernel(**inputs):
    import numpy as np
    import concourse.bacc as bacc
    from concourse.bass_utils import run_bass_kernel_spmd

    a = {k: np.asarray(v) for k, v in inputs.items()}
    swap = np.arange(128) ^ 1
    laid = {
        "x": a["x"], "ctx": a["ctx_1024"],
        "L0_xattn_Wq": a["L0_xattn_Wq"], "L0_xattn_Wk": a["L0_xattn_Wk"], "L0_xattn_Wv": a["L0_xattn_Wv"],
        "wihT": a["L0_xattn_gru_wih"].T, "whhT": a["L0_xattn_gru_whh"].T,
        "bih3": a["L0_xattn_gru_bih"].reshape(3, 128).T, "bhh3": a["L0_xattn_gru_bhh"].reshape(3, 128).T,
        "ws_col": a["L0_xattn_slot_norm_w"].reshape(128, 1), "wp_col": a["L0_xattn_input_norm_w"].reshape(128, 1),
        "wp_row": a["L0_xattn_input_norm_w"],
        "L0_attn_q_proj": a["L0_attn_q_proj"], "L0_attn_k_proj": a["L0_attn_k_proj"],
        "gateT0": a["L0_ffn_gate_weight"].T, "ln_cols": np.stack([a["L0_ffn_ln_gamma"], a["L0_ffn_ln_beta"]], 1),
        "wi": a["L0_ffn_wi"], "wo": a["L0_ffn_wo"],
        "ctxT": a["ctx_1024"].transpose(0, 2, 1), "mask": a["mask_Bx1xSxS2_if1"].reshape(B, S, M),
        "WqT1": by_feature(a["L1_xattn_Wq"]), "WkT1": by_feature(a["L1_xattn_Wk"]), "WvT1": a["L1_xattn_Wv"].T, "WoT1": a["L1_xattn_Wo"].T,
        "bo": a["L1_xattn_bo"],
        "rWq": a["L1_attn_Wq"], "rWqs": a["L1_attn_Wq"][:, swap], "rWk": a["L1_attn_Wk"], "rWks": a["L1_attn_Wk"][:, swap],
        "rWv": a["L1_attn_Wv"], "rWg": a["L1_attn_Wg"], "rWo": a["L1_attn_Wo"],
        "gcol": np.tile(a["L1_attn_g_norm_w"], 4).reshape(128, 1), **rotary_tables(np),
        "gate1": a["L1_ffn_gate_w"], "ew1": a["L1_ffn_ew1"], "ew2": a["L1_ffn_ew2"], "ew3": a["L1_ffn_ew3"],
        "sw1": a["L1_ffn_sw1"], "sw2": a["L1_ffn_sw2"], "sw3": a["L1_ffn_sw3"],

    }
    nc = bacc.Bacc("TRN2", target_bir_lowering=False, num_devices=1)
    arrays, p = {}, {}
    for name, v in laid.items():
        v = np.ascontiguousarray(v)
        arrays["in_" + name] = v
        p[name] = nc.dram_tensor("in_" + name, v.shape, mybir.dt.from_np(v.dtype), kind="ExternalInput").ap()
    out = nc.dram_tensor("out", (B, S, D), fp32, kind="ExternalOutput").ap()
    perceiver(nc, p, out)
    r = run_bass_kernel_spmd(nc, [arrays], core_ids=[0])
    return r.results[0]["out"]
```
